# Optimizing a Trainium2 kernel written in Bass

```python
import numpy as np
import jax
import jax.numpy as jnp

def _softmax(x, axis=-1):
    return jax.nn.softmax(x, axis=axis)

def _gelu(x):
    return jax.nn.gelu(x, approximate=True)

def _silu(x):
    return jax.nn.silu(x)

def _sigmoid(x):
    return jax.nn.sigmoid(x)

def _layernorm(x, axis=-1, eps=1e-05):
    m = jnp.mean(x, axis=axis, keepdims=True)
    v = jnp.var(x, axis=axis, keepdims=True)
    return (x - m) / jnp.sqrt(v + eps)

def _scatter_add(tgt, idx, src, axis=0):
    return tgt.at[idx].add(src)

def _segment_sum(src, seg, n):
    return jax.ops.segment_sum(src, seg, n)
kernel_name = 'mk_gnn_resnorm_d2_gnn_r16_a52e92'

def setup_inputs(seed: int=0):
    np.random.seed(seed)
    _w = jnp.asarray

    def _rec_inputs():
        import jax
        import jax.numpy as jnp
        _gk = jax.random.key(seed)
        x = -0.0003713 + 1 * jax.random.normal(jax.random.fold_in(_gk, 1), (3125, 256), jnp.float32)
        _s = jax.random.randint(jax.random.fold_in(_gk, 2), (50000,), 0, 3125, jnp.int32)
        _d = jax.random.randint(jax.random.fold_in(_gk, 3), (50000,), 0, 3125, jnp.int32)
        _loop = jnp.arange(3125, dtype=jnp.int32)
        src = jnp.concatenate([_s, _d, _loop])
        dst = jnp.concatenate([_d, _s, _loop])
        _o = jnp.argsort(dst, stable=True)
        src = src[_o]
        dst = dst[_o]
        edge_weight = jax.random.uniform(jax.random.fold_in(_gk, 12), (103125,), jnp.float32, 0.0, 0.999998)
        return (x, src, dst, edge_weight)
    x, src, dst, edge_weight = _rec_inputs()

    def _L0_gnn_setup():
        import jax, jax.numpy as jnp
        import numpy as np
        N_NODES = 3125
        NEG_SLOPE = 0.01

        def gcn_conv(x, src, dst, ew, W, b):
            n = x.shape[0]
            h = x @ W
            loop = jnp.arange(n, dtype=src.dtype)
            src_f = jnp.concatenate([src, loop])
            dst_f = jnp.concatenate([dst, loop])
            ew_f = jnp.concatenate([ew, jnp.ones((n,), dtype=ew.dtype)])
            deg = jax.ops.segment_sum(ew_f, dst_f, num_segments=n)
            dis = jnp.where(deg > 0, jax.lax.rsqrt(jnp.where(deg > 0, deg, 1.0)), 0.0)
            norm = dis[src_f] * ew_f * dis[dst_f]
            msg = h[src_f] * norm[:, None]
            out = jax.ops.segment_sum(msg, dst_f, num_segments=n)
            return out + b
        key = jax.random.key(seed)
        k = jax.random.split(key, 6)
        nfeat, nhid, E = (256, 256, 31250)
        x = jax.random.normal(k[0], (N_NODES, nfeat), dtype=jnp.float32)
        edge_index = jax.random.randint(k[1], (2, E), 0, N_NODES, dtype=jnp.int64)
        edge_weight = jax.random.uniform(k[2], (E,), dtype=jnp.float32)
        s1 = 1.0 / np.sqrt(nfeat)
        s2 = 1.0 / np.sqrt(nhid)
        W1 = jax.random.normal(k[3], (nfeat, nhid), dtype=jnp.float32) * s1
        b1 = jnp.zeros((nhid,), dtype=jnp.float32)
        W2 = jax.random.normal(k[4], (nhid, nhid), dtype=jnp.float32) * s2
        b2 = jnp.zeros((nhid,), dtype=jnp.float32)
        return {'x': x, 'edge_index': edge_index, 'edge_weight': edge_weight, 'W1': W1, 'b1': b1, 'W2': W2, 'b2': b2}
    _L0_gnn_all = _L0_gnn_setup()
    _L0_gnn_in = {k: v for k, v in _L0_gnn_all.items() if k in ('W1', 'b1', 'W2', 'b2')}
    del _L0_gnn_all

    def _L1_gnn_setup():
        import jax, jax.numpy as jnp
        import numpy as np
        NEG_SLOPE = 0.2

        def gatv2_layer(x, Wl, Wr, att, bias, src, dst, n_nodes, heads, ch, concat):
            xl = (x @ Wl).reshape(n_nodes, heads, ch)
            xr = (x @ Wr).reshape(n_nodes, heads, ch)
            m = xl[src] + xr[dst]
            e = jax.nn.leaky_relu(m, NEG_SLOPE)
            logits = jnp.einsum('ehc,hc->eh', e, att)
            mx = jax.ops.segment_max(logits, dst, num_segments=n_nodes)
            ex = jnp.exp(logits - mx[dst])
            denom = jax.ops.segment_sum(ex, dst, num_segments=n_nodes)
            alpha = ex / denom[dst]
            out = jax.ops.segment_sum(alpha[:, :, None] * xl[src], dst, num_segments=n_nodes)
            if concat:
                out = out.reshape(n_nodes, heads * ch)
            else:
                out = out.mean(axis=1)
            return out + bias
        N, E = (3125, 50000)
        IN, HID, OUT, H = (256, 64, 256, 4)
        key = jax.random.key(seed)
        ks = jax.random.split(key, 12)
        s = lambda fan_in: 1.0 / np.sqrt(fan_in)
        return {'x': jax.random.normal(ks[0], (N, IN), dtype=jnp.float32), 'edge_index': jax.random.randint(ks[1], (2, E), 0, N, dtype=jnp.int64), 'Wl1': jax.random.normal(ks[2], (IN, H * HID), jnp.float32) * s(IN), 'Wr1': jax.random.normal(ks[3], (IN, H * HID), jnp.float32) * s(IN), 'att1': jax.random.normal(ks[4], (H, HID), jnp.float32) * s(HID), 'b1': jnp.zeros((H * HID,), jnp.float32), 'Wl2': jax.random.normal(ks[5], (H * HID, OUT), jnp.float32) * s(H * HID), 'Wr2': jax.random.normal(ks[6], (H * HID, OUT), jnp.float32) * s(H * HID), 'att2': jax.random.normal(ks[7], (1, OUT), jnp.float32) * s(OUT), 'b2': jnp.zeros((OUT,), jnp.float32)}
    _L1_gnn_all = _L1_gnn_setup()
    _L1_gnn_in = {k: v for k, v in _L1_gnn_all.items() if k in ('Wl1', 'Wr1', 'att1', 'b1', 'Wl2', 'Wr2', 'att2', 'b2')}
    del _L1_gnn_all
    return {'x': x, 'src': src, 'dst': dst, 'edge_weight': edge_weight, 'L0_gnn_W1': _L0_gnn_in['W1'], 'L0_gnn_b1': _L0_gnn_in['b1'], 'L0_gnn_W2': _L0_gnn_in['W2'], 'L0_gnn_b2': _L0_gnn_in['b2'], 'L1_gnn_Wl1': _L1_gnn_in['Wl1'], 'L1_gnn_Wr1': _L1_gnn_in['Wr1'], 'L1_gnn_att1': _L1_gnn_in['att1'], 'L1_gnn_b1': _L1_gnn_in['b1'], 'L1_gnn_Wl2': _L1_gnn_in['Wl2'], 'L1_gnn_Wr2': _L1_gnn_in['Wr2'], 'L1_gnn_att2': _L1_gnn_in['att2'], 'L1_gnn_b2': _L1_gnn_in['b2']}

def reference(x, src, dst, edge_weight, L0_gnn_W1, L0_gnn_b1, L0_gnn_W2, L0_gnn_b2, L1_gnn_Wl1, L1_gnn_Wr1, L1_gnn_att1, L1_gnn_b1, L1_gnn_Wl2, L1_gnn_Wr2, L1_gnn_att2, L1_gnn_b2):
    import jax
    import jax.numpy as jnp

    def _L0_gnn_ref(x, edge_index, edge_weight, W1, b1, W2, b2):
        import jax, jax.numpy as jnp
        import numpy as np
        N_NODES = 3125
        NEG_SLOPE = 0.01

        def gcn_conv(x, src, dst, ew, W, b):
            n = x.shape[0]
            h = x @ W
            loop = jnp.arange(n, dtype=src.dtype)
            src_f = jnp.concatenate([src, loop])
            dst_f = jnp.concatenate([dst, loop])
            ew_f = jnp.concatenate([ew, jnp.ones((n,), dtype=ew.dtype)])
            deg = jax.ops.segment_sum(ew_f, dst_f, num_segments=n)
            dis = jnp.where(deg > 0, jax.lax.rsqrt(jnp.where(deg > 0, deg, 1.0)), 0.0)
            norm = dis[src_f] * ew_f * dis[dst_f]
            msg = h[src_f] * norm[:, None]
            out = jax.ops.segment_sum(msg, dst_f, num_segments=n)
            return out + b
        src, dst = (edge_index[0], edge_index[1])
        h = gcn_conv(x, src, dst, edge_weight, W1, b1)
        h = jnp.where(h >= 0, h, NEG_SLOPE * h)
        out = gcn_conv(h, src, dst, edge_weight, W2, b2)
        return out

    def _L1_gnn_ref(x, edge_index, Wl1, Wr1, att1, b1, Wl2, Wr2, att2, b2):
        import jax, jax.numpy as jnp
        import numpy as np
        NEG_SLOPE = 0.2

        def gatv2_layer(x, Wl, Wr, att, bias, src, dst, n_nodes, heads, ch, concat):
            xl = (x @ Wl).reshape(n_nodes, heads, ch)
            xr = (x @ Wr).reshape(n_nodes, heads, ch)
            m = xl[src] + xr[dst]
            e = jax.nn.leaky_relu(m, NEG_SLOPE)
            logits = jnp.einsum('ehc,hc->eh', e, att)
            mx = jax.ops.segment_max(logits, dst, num_segments=n_nodes)
            ex = jnp.exp(logits - mx[dst])
            denom = jax.ops.segment_sum(ex, dst, num_segments=n_nodes)
            alpha = ex / denom[dst]
            out = jax.ops.segment_sum(alpha[:, :, None] * xl[src], dst, num_segments=n_nodes)
            if concat:
                out = out.reshape(n_nodes, heads * ch)
            else:
                out = out.mean(axis=1)
            return out + bias
        N = x.shape[0]
        loops = jnp.arange(N, dtype=edge_index.dtype)
        src = jnp.concatenate([edge_index[0], loops])
        dst = jnp.concatenate([edge_index[1], loops])
        h = gatv2_layer(x, Wl1, Wr1, att1, b1, src, dst, N, 4, 64, concat=True)
        h = jax.nn.elu(h)
        out = gatv2_layer(h, Wl2, Wr2, att2, b2, src, dst, N, 1, 256, concat=False)
        return out
    edge_index = jnp.stack([src, dst])
    x = _layernorm(x + _L0_gnn_ref(x, edge_index, edge_weight, L0_gnn_W1, L0_gnn_b1, L0_gnn_W2, L0_gnn_b2), axis=-1)
    x = _layernorm(x + _L1_gnn_ref(x, edge_index, L1_gnn_Wl1, L1_gnn_Wr1, L1_gnn_att1, L1_gnn_b1, L1_gnn_Wl2, L1_gnn_Wr2, L1_gnn_att2, L1_gnn_b2), axis=-1)
    return x

_drawn_inputs = setup_inputs


def setup_inputs(seed=0):
    import zlib

    import numpy as np

    out = dict(_drawn_inputs(seed))
    spreads = {'L0_gnn_b1': (0.0, 0.1),
     'L0_gnn_b2': (0.0, 0.1),
     'L1_gnn_b1': (0.0, 0.1),
     'L1_gnn_b2': (0.0, 0.1)}
    factors = {'edge_weight': 3.163, 'L1_gnn_Wr1': 5.399, 'L1_gnn_Wr2': 8.0, 'L1_gnn_att2': 8.0}
    for name, (base, spread) in spreads.items():
        noise = np.random.default_rng([zlib.crc32(name.encode()), seed]).standard_normal(out[name].shape)
        drawn = base * np.exp(spread * noise) if base else spread * noise
        out[name] = jnp.asarray(drawn.astype(out[name].dtype))
    for name, factor in factors.items():
        out[name] = (out[name] * factor).astype(out[name].dtype)
    return out
```

```python
from contextlib import ExitStack

import numpy as np

import concourse.bass as bass
from concourse import mybir
from concourse.alu_op_type import AluOpType as ALU

ACT = mybir.ActivationFunctionType
AX = mybir.AxisListType
F32 = mybir.dt.float32
F32R = mybir.dt.float32r
BF16 = mybir.dt.bfloat16
I32 = mybir.dt.int32

TN = 125
CH = 256
GR = 5
GPT = TN // GR
BLK = 32
ROW = 256
KP = 17
BIG = 2.0 ** 100
MAGIC = 12582912.0
EPS = 1.0e-5
LG = 2
NRING = 4
RP = 2 * KP
LAGC = 22


class Counter:

    def __init__(self, handle):
        self.handle, self.value = handle, 0

    def raised(self, by):
        self.value += by
        return (self, self.value)


class Queues:

    def __init__(self, sem):
        self.lists = {n: [] for n in ("sync", "tensor", "vector", "scalar", "gpsimd")}
        self.done = {n: Counter(sem(f"{n}_done")) for n in ("tensor", "vector", "scalar", "gpsimd")}

    def put(self, engine, fn, after=(), counter=None, by=1):
        token = counter.raised(by) if counter else None
        self.lists[engine].append((fn, [a for a in after if a], counter, by))
        return token

    def pe(self, fn, after=(), last=False):
        return self.put("tensor", fn, after, self.done["tensor"] if last else None)

    def dve(self, fn, after=()):
        return self.put("vector", fn, after, self.done["vector"])

    def act(self, fn, after=()):
        return self.put("scalar", fn, after, self.done["scalar"])

    def pool(self, fn, after=()):
        return self.put("gpsimd", fn, after, self.done["gpsimd"])

    def dma(self, counter, out, in_, after=(), engine="sync"):
        return self.put(engine, lambda e: e.dma_start(out, in_), after, counter, 16)

    def emit(self, engine, e):
        seen = {}
        for fn, after, counter, by in self.lists[engine]:
            for c, value in after:
                if seen.get(c, 0) < value:
                    e.wait_ge(c.handle, value)
                    seen[c] = value
            i = fn(e) if fn else None
            if counter:
                i.then_inc(counter.handle, by)


def shape_constants(NT):
    NJ = NT // 5
    p = np.arange(128, dtype=np.float32)[:, None]
    R = 5 * KP
    parts = {}
    parts["iota"] = np.broadcast_to(np.arange(128, dtype=np.float32), (128, 128))
    parts["ident"] = np.eye(128, dtype=np.float32)
    parts["pidx"] = p
    parts["v5"] = GR * (np.arange(NJ, dtype=np.float32)[None] * TN + p)
    parts["v125"] = TN * (np.arange(NJ, dtype=np.float32)[None] * 5 + np.floor(p / KP))
    parts["k8"] = (ROW // BLK) * (p % KP)
    sel = np.zeros((128, R), np.float32)
    for m in range(R):
        sel[GPT * (m // KP), m] = 1
    parts["sel85"] = sel
    sh = np.zeros((128, R), np.float32)
    for m in range(R - 1):
        if m % KP != KP - 1:
            sh[m + 1, m] = 1
    parts["sh85"] = sh
    parts["k16"] = -(p % KP == KP - 1).astype(np.float32)
    s2 = np.zeros((128, 2 * KP), np.float32)
    for h in range(4):
        for k in range(KP):
            s2[h * KP + k, k] = s2[h * KP + k, KP + k] = 1
    parts["sel2"] = s2
    hm = np.zeros((128, 4), np.float32)
    for h in range(4):
        hm[h * KP:(h + 1) * KP, h] = 1
    parts["hm"] = hm
    hmt = np.zeros((128, 4 * KP), np.float32)
    hmt[:4, :] = hm[:4 * KP].T
    parts["hmt"] = hmt
    mb = np.zeros((128, 2), np.float32)
    mb[:64, 0] = mb[64:, 1] = 1
    parts["mb"] = mb
    parts["ones"] = np.ones((128, 1), np.float32)
    at, where = 0, {}
    for k, v in parts.items():
        where[k] = (at, at + v.shape[1])
        at += v.shape[1]
    return np.ascontiguousarray(np.concatenate(list(parts.values()), axis=1).astype(np.float32)), where


def gnn_program(nc, A, NT, E, where):
    NJ = NT // 5
    N = NT * TN
    R = 5 * KP
    NROW = NT * KP
    NB = A["first"].shape[1]
    CW = A["dsort"].shape[1] - 1
    NP = NT * KP
    SC = NT * TN

    ctx = ExitStack()
    sb = lambda name, shape, dt=F32: ctx.enter_context(nc.sbuf_tensor(name, shape, dt))
    sem = lambda name: ctx.enter_context(nc.semaphore(name))
    dram = lambda name, shape, dt=F32: nc.dram_tensor(name, shape, dt, kind="Internal").ap()
    Q = Queues(sem)
    cnt = lambda name: Counter(sem(name))

    DEGD = dram("deg_d", (N,))
    AD = dram("a_d", (NT, TN, SC))
    X1D = dram("x1_d", (N, CH))
    TAB = [dram("tab1_d", (N, CH + 4)), dram("tab2_d", (N, CH + 1))]
    XRD = [dram(f"xr{l}_d", (NT, TN, 2 * CH)) for l in range(2)]
    CSD = dram("cs_d", (NJ, R, 2))
    M3D = dram("m3_d", (NROW, 772), BF16)
    DLBD = dram("dlb_d", (NROW, ROW), BF16)

    PS = [ctx.enter_context(nc.psum_tensor(f"bank{i}", [128, 512], F32)) for i in range(8)]

    CON = sb("con", [128, A["const"].shape[1]])
    K = lambda name, p=128: CON[0:p, where[name][0]:where[name][1]]
    IOTA = K("iota")[:, 0:TN + 1]
    IDN = K("ident")
    W2S = sb("w2s", [128, 2, CH])
    HS = [4, 1]
    WL = [sb(f"wl{l}", [128, 2, CH + HS[l]]) for l in range(2)]
    WR = [sb(f"wr{l}", [128, 2, CH + HS[l]]) for l in range(2)]
    BB = [sb(f"bb{i}", [TN, CH]) for i in range(4)]
    ATB = [sb(f"atb{l}", [128, CH]) for l in range(2)]
    ATC = [sb(f"atc{l}", [128, 2]) for l in range(2)]
    HPN = [4, 2]
    AB = [sb(f"ab{l}", [128, 2, 2]) for l in range(2)]
    ARX = [sb(f"arx{l}", [TN, NT, 2, HPN[l]], F32R) for l in range(2)]
    LSF = [sb(f"lsf{l}", [TN, NT, HS[l]]) for l in range(2)]
    SRCI = sb("srci", [128, NJ, 2, R], I32)
    DLS = sb("dls", [128, NJ, 2, R])
    LAST = sb("last", [128, NJ, 2, R])
    CRF = sb("crf", [4, 1 + NROW])
    AFW = sb("afw", [4, NROW])
    ARV = sb("arv", [4, NROW])
    DIS = sb("dis", [TN, NT])
    FLAG = sb("flag", [1, 4], I32)

    d_con = cnt("d_con")
    t_con = Q.dma(d_con, CON[:], A["const"])

    def loaded(counter, out, in_, after=(), engine="sync"):
        return Q.dma(counter, out, in_, after, engine)

    gcn = ExitStack()
    sg = lambda name, shape, dt=F32: gcn.enter_context(nc.sbuf_tensor(name, shape, dt))
    HP = [sg(f"hp{i}", [TN, NT, CH]) for i in range(2)]
    RING = sg("ring", [128, NRING, SC])
    FLD = sg("fld", [128, NJ, 2, 3, TN])
    early = HP[1][:].rearrange("p t c -> p (t c)")
    GSD = early[:, 0:2 * ROW * NJ].bitcast(I32).rearrange("p (j c) -> p j c", j=NJ)
    GEW = early[:, 2 * ROW * NJ:3 * ROW * NJ].rearrange("p (j c) -> p j c", j=NJ)
    TSD = early[0:R, 3 * ROW * NJ:5 * ROW * NJ].bitcast(I32).rearrange("p (j c) -> p j c", j=NJ)
    XST = [sg(f"xst{i}", [TN, CH]) for i in range(3)]
    OHW = 12
    OHS = sg("ohs", [128, OHW, 2, TN + 1])
    W1S = sg("w1s", [128, 2, CH])
    CNT = sg("cnt", [TN, NJ])
    CNB = sg("cnb", [TN, NJ])
    STF = sg("stf", [TN, NJ])
    STI = sg("sti", [TN, NJ], I32)
    IXF = sg("ixf", [R, NJ])
    IXI = sg("ixi", [R, NJ], I32)
    GF = [sg(f"gf{i}", [TN, ROW]) for i in range(6)]
    KS = [[sg(f"ks{i}_{j}", [TN, ROW]) for i in range(3)] for j in range(2)]
    DEG = sg("deg", [TN, NJ, GR])
    VAL = sg("val", [TN, NJ])
    DGR = sg("dgr", [NT, TN])
    DG = [sg(f"dg{i}", [TN, NT]) for i in range(3)]
    HT = [sg(f"ht{i}", [128, 2, TN]) for i in range(2)]
    ZB = [sg(f"zb{i}", [TN, CH]) for i in range(4)]
    XL = [sg(f"xl{i}", [TN, CH + 4]) for i in range(2)]
    SMALL = [sg(f"small{i}", [TN, 16]) for i in range(2)]
    XRS = [sg(f"xrs{i}", [TN, 2 * CH]) for i in range(2)]
    PF = [XRS[i // 2][0:R, (i % 2) * CH:(i % 2 + 1) * CH] for i in range(4)] + [sg(f"pf{i}", [R, ROW]) for i in range(4, 7)]
    PB = sg("pb", [R, ROW], BF16)
    PM = sg("pm", [R, 772], BF16)
    LF = sg("lf", [R, NJ, ROW])
    FL = [sg(f"fl{i}", [R, NJ]) for i in range(5)]
    CS = sg("cs", [R, NJ, 2])
    CSB = sg("csb", [4, NROW, 2])
    VALT = sg("valt", [R, NJ])
    STAT = sg("stat", [128, 4])
    SUMS = sg("sums", [1, 8])
    DSI = RING[:, 1, SC - CW - 1:SC].bitcast(I32)
    ATW = [sg("atw0", [128, 2, CH])]
    ATR = sg("atr", [128, 2, 4])

    ring_flat = RING[:].rearrange("p r c -> p (r c)")
    FIRST = HP[1][:].rearrange("p t c -> p (t c)")[:, 0:NB]
    FIRSTI = ring_flat[0:TN, 0:NB].bitcast(I32)
    d_sort = cnt("d_sort")
    d_first, d_w1, d_w2, d_b, d_wl, d_at = (cnt(n) for n in ("d_first", "d_w1", "d_w2", "d_b", "d_wl", "d_at"))
    t_first = loaded(d_first, FIRSTI, A["first"][0:1, :].broadcast_to([TN, NB]), engine="scalar")
    t_w1 = loaded(d_w1, W1S[:], A["W1"].rearrange("(k p) n -> p k n", p=128), engine="scalar")
    t_dsi = loaded(d_sort, DSI, A["dsort"], engine="scalar")
    d_x = [cnt(f"d_x{i}") for i in range(3)]
    xTv = ring_flat[:, (NRING - 2) * SC:(NRING - 2) * SC + 2 * N].rearrange("p (k n) -> p k n", k=2)

    t_cvt = Q.dve(lambda e: e.tensor_copy(FIRST, FIRSTI), [t_first])
    junk = OHS[:].rearrange("p a b c -> p (a b c)").bitcast(BF16)
    junk_act = FLD[:].rearrange("p j h f n -> p (j h f n)").bitcast(BF16)
    t_cnt, t_sti = None, []
    t_nv = Q.dve(lambda e: e.tensor_scalar(CNB[:], K("v5", TN), -1.0, 0.5, op0=ALU.mult, op1=ALU.add), [t_con])
    for j in range(NJ):
        if j % 2 == 0:
            t_cnt = Q.dve(lambda e, j=j: e.tensor_scalar(junk[0:TN, 0:NB], FIRST, K("v5", TN)[:, j:j + 1], None, op0=ALU.is_lt, op1=ALU.add, accum_out=CNT[:, j:j + 1]), [t_cvt, t_con, t_cnt])
            t_stf = Q.dve(lambda e, j=j: e.tensor_scalar(STF[:, j:j + 1], CNT[:, j:j + 1], -1.0, 0.0, op0=ALU.add, op1=ALU.max), [t_cnt])
            t_sti.append(Q.dve(lambda e, j=j: e.tensor_copy(STI[:, j:j + 1], STF[:, j:j + 1]), [t_stf]))
        else:
            t_cnta = Q.act(lambda e, j=j: e.activation(junk_act[0:TN, 0:NB], FIRST, ACT.Sign, bias=CNB[:, j:j + 1], accum_out=CNT[:, j:j + 1]), [t_cvt, t_nv] + ([t_cnta] if j > 1 else []))
            t_sti.append(None)
    for j in range(1, NJ, 2):
        t_1 = Q.dve(lambda e, j=j: e.tensor_scalar(STF[:, j:j + 1], CNT[:, j:j + 1], -0.5, NB / 2 - 1.0, op0=ALU.mult, op1=ALU.add), [t_cnta])
        t_stf = Q.dve(lambda e, j=j: e.tensor_scalar(STF[:, j:j + 1], STF[:, j:j + 1], 0.0, None, op0=ALU.max), [t_1])
        t_sti[j] = Q.dve(lambda e, j=j: e.tensor_copy(STI[:, j:j + 1], STF[:, j:j + 1]), [t_stf])
    if NJ == 1:
        t_cnta = t_cvt
    t_stat = Q.dve(lambda e: e.memset(STAT[:], 0.0))
    t_uns = Q.dve(lambda e: e.scalar_tensor_tensor(junk[:, 0:CW], DSI[:, 0:CW], 0.0, DSI[:, 1:CW + 1], op0=ALU.add, op1=ALU.is_gt, accum_out=STAT[:, 2:3]), [t_dsi, t_stat, t_cnt])

    off = lambda ap: bass.IndirectOffsetOnAxis(ap=ap, axis=0)
    d_gsd, d_gew, d_tsd = ([cnt(f"{n}{j}") for j in range(NJ)] for n in ("d_gsd", "d_gew", "d_tsd"))
    t_gsd = []
    for j in range(NJ):
        t_1 = Q.put("gpsimd", lambda e, j=j: e.indirect_dma_start(out=GSD[:, j, :], out_offset=None, in_=A["sd"], in_offset=off(STI[:, j:j + 1])), [t_sti[j], t_cvt, t_cnt, t_cnta], d_gsd[j], 16)
        t_2 = Q.put("gpsimd", lambda e, j=j: e.indirect_dma_start(out=GEW[:, j, :], out_offset=None, in_=A["ew"], in_offset=off(STI[:, j:j + 1])), [], d_gew[j], 16)
        t_gsd.append([t_1, t_2])
    t_xload, t_xt_read = [None] * 3, [None] * 3
    t_xw = []
    t_ptfree = [None, None]
    t_xtw = []
    for t in range(NT):
        b = t % 3
        tl = loaded(d_x[b], XST[b][:], A["x"][t * TN:(t + 1) * TN, :], [t_xt_read[b]])
        bank = PS[5 + t % 2]
        Q.pe(lambda e, b=b, bank=bank: e.matmul(bank[:, 0:TN], XST[b][:, 0:128], IDN[0:TN, 0:TN], start=True, stop=True, is_transpose=True), [tl, t_con, t_ptfree[t % 2]])
        tt = Q.pe(lambda e, b=b, bank=bank: e.matmul(bank[:, TN:2 * TN], XST[b][:, 128:256], IDN[0:TN, 0:TN], start=True, stop=True, is_transpose=True), last=True)
        t_xt_read[b] = tt
        te = Q.act(lambda e, t=t, bank=bank: e.activation(xTv[:, :, t * TN:(t + 1) * TN], bank[:, 0:2 * TN].rearrange("p (k n) -> p k n", k=2), ACT.Copy), [tt])
        t_ptfree[t % 2] = te
        t_xtw.append(te)
    t_hpfree = [None] * 2
    t_hp = [[None] * NT for _ in range(2)]
    t_raw = []
    for t in range(NT):
        bank = PS[3 + t % 2]
        Q.pe(lambda e, t=t, bank=bank: e.matmul(bank[0:TN, 0:CH], xTv[:, 0, t * TN:(t + 1) * TN], W1S[:, 0, :], start=True, stop=False), [t_xtw[t], t_w1, t_hpfree[t % 2]])
        tm = Q.pe(lambda e, t=t, bank=bank: e.matmul(bank[0:TN, 0:CH], xTv[:, 1, t * TN:(t + 1) * TN], W1S[:, 1, :], start=False, stop=True), last=True)
        te = Q.act(lambda e, t=t, bank=bank: e.activation(HP[0][:, t, :], bank[0:TN, 0:CH], ACT.Copy), [tm])
        t_hpfree[t % 2] = te
        t_raw.append(te)
    t_xt_done = t_raw[-1]

    t_ixp = Q.pe(lambda e: e.matmul(PS[7][0:R, 0:NJ], K("sel85", TN), STF[:], start=True, stop=True), [t_stf, t_con], last=True)
    t_ixf = Q.dve(lambda e: e.tensor_scalar(IXF[:], PS[7][0:R, 0:NJ], K("k8", R), None, op0=ALU.add), [t_ixp])
    t_tsd = []
    t_ixi = Q.dve(lambda e: e.tensor_copy(IXI[:], IXF[:]), [t_ixf])

    for j in range(NJ):
        t_tsd.append(Q.put("gpsimd", lambda e, j=j: e.indirect_dma_start(out=TSD[:, j, :], out_offset=None, in_=A["sd"], in_offset=off(IXI[:, j:j + 1])), [t_ixi], d_tsd[j], 16))

    t_b = None
    for i, n in enumerate(("b1", "b2", "b3", "b4")):
        t_b = loaded(d_b, BB[i][:], A[n].broadcast_to([TN, CH]))
    t_w2 = loaded(d_w2, W2S[:], A["W2"].rearrange("(k p) n -> p k n", p=128))
    for l in range(2):
        loaded(d_wl, WL[l][:, :, 0:CH], A[f"Wl{l + 1}"].rearrange("(k p) n -> p k n", p=128))
        t_wl = loaded(d_wl, WR[l][:, :, 0:CH], A[f"Wr{l + 1}"].rearrange("(k p) n -> p k n", p=128))
        loaded(d_at, ATB[l][:], A[f"att{l + 1}"].broadcast_to([128, CH]))
        t_at = loaded(d_at, ATC[l][:], A[f"att{l + 1}c"])

    t_fld = [None] * NJ
    t_deg = [None] * NJ
    t_ksfree = [None, None]

    def fields(j):
        src, dst, ew = GSD[:, j, 0:ROW], GSD[:, j, ROW:2 * ROW], GEW[:, j, :]
        slo, key, eww = KS[j % 2]
        drel, blk, ge, tmp, one, blk2 = (g[:] for g in GF)
        prev = [t_fields[-1]] if t_fields else []
        t1 = Q.dve(lambda e: e.tensor_scalar(drel, dst, K("v5", TN)[:, j:j + 1], None, op0=ALU.subtract), t_gsd[j] + [t_con] + prev)
        t2 = Q.dve(lambda e: e.tensor_scalar(blk, src, 1.0 / TN, 0.5 / TN - 0.5, op0=ALU.mult, op1=ALU.add), prev)
        t4 = Q.dve(lambda e: e.tensor_scalar(ge, drel, 0.0, None, op0=ALU.is_ge), [t1])
        t2b = Q.dve(lambda e: e.tensor_scalar(tmp, blk, MAGIC, None, op0=ALU.add), [t2])
        t5 = Q.dve(lambda e: e.scalar_tensor_tensor(one, drel, float(GR), ge, op0=ALU.is_lt, op1=ALU.mult, accum_out=VAL[:, j:j + 1]), [t4])
        t3 = Q.dve(lambda e: e.tensor_scalar(blk2, tmp, MAGIC, None, op0=ALU.subtract), [t2b])
        t6 = Q.dve(lambda e: e.tensor_tensor(eww[:], one, ew, op=ALU.mult), [t5, t_ksfree[j % 2]])
        t7 = Q.dve(lambda e: e.scalar_tensor_tensor(slo[:], blk2, -float(TN), src, op0=ALU.mult, op1=ALU.add), [t3])
        t8 = Q.dve(lambda e: e.scalar_tensor_tensor(key[:], blk2, float(GR), drel, op0=ALU.mult, op1=ALU.add), [t3])
        t_fields.append(t8)
        return t6, t7, t8

    t_fields = []

    def degrees(j, t6):
        eww, drel = KS[j % 2][2], GF[0]
        for r in range(GR):
            t_deg[j] = Q.dve(lambda e, r=r: e.scalar_tensor_tensor(GF[2][:] if r % 2 else GF[3][:], drel[:], float(r), eww[:], op0=ALU.is_equal, op1=ALU.mult, accum_out=DEG[:, j, r:r + 1]), [t6, t_deg[j]])
        t_fields.append(t_deg[j])

    def field_transposes(j, t8):
        for half in range(2):
            for f in range(3):
                tp = Q.pe(lambda e, f=f, half=half: e.matmul(PS[7][:, f * TN:(f + 1) * TN], KS[j % 2][f][:, half * 128:(half + 1) * 128], IDN[0:TN, 0:TN], start=True, stop=True, is_transpose=True), [t8, t_ixf, t_fldfree[0]], last=(f == 2))
            order = (0, 1, 2)
            t_fldfree[0] = Q.act(lambda e, half=half: e.activation(FLD[:, j, half, :, :], PS[7][:, 0:3 * TN].rearrange("p (f n) -> p f n", f=3), ACT.Copy), [tp])
        t_fld[j] = t_fldfree[0]
        t_ksfree[j % 2] = tp

    t_fldfree = [None]

    ROWS_AT = [LG + 2 * jj for jj in range(NJ)]
    build_banks = (0, 1, 2)
    t_bank = [None] * 3
    t_oh = [None] * OHW
    ring_free = [[] for _ in range(NRING)]
    t_at_tile = [None] * NT
    quart = [(q * 4, min(4, GPT - q * 4)) for q in range((GPT + 3) // 4)]
    slot_no = [0]
    bank_no = [0]
    d_ad = [cnt(f"d_ad{i}") for i in range(NRING)]

    def build_quartet(t, q):
        g0, ng = quart[q]
        bk = bank_no[0] % 3
        bank_no[0] += 1
        bank = PS[build_banks[bk]]
        for gi in range(ng):
            g = t * GPT + g0 + gi
            j, p = g // TN, g % TN
            for half in range(2):
                o = slot_no[0] % OHW
                slot_no[0] += 1
                put = Q.pool if half and (t not in ROWS_AT or q < 3) else Q.dve
                t1 = put(lambda e, j=j, p=p, half=half, o=o: e.tensor_scalar(OHS[:, o, 0, :], IOTA, FLD[:, j, half, 0, p:p + 1], None, op0=ALU.is_equal), [t_fld[j], t_oh[o], t_uns])
                t2 = Q.dve(lambda e, j=j, p=p, half=half, o=o: e.tensor_scalar(OHS[:, o, 1, :], IOTA, FLD[:, j, half, 1, p:p + 1], FLD[:, j, half, 2, p:p + 1], op0=ALU.is_equal, op1=ALU.mult), [t_fld[j], t_oh[o], t_uns])
                tm = Q.pe(lambda e, gi=gi, half=half, o=o, bank=bank: e.matmul(bank[0:TN, gi * TN:(gi + 1) * TN], OHS[:, o, 0, 0:TN], OHS[:, o, 1, 0:TN], start=(half == 0), stop=(half == 1)), [t1, t2, t_bank[bk]], last=True)
                t_oh[o] = tm
        r = t % NRING
        dst = RING[0:TN, r, :].rearrange("p (s g d) -> p g s d", s=NT, g=GPT)[:, g0:g0 + ng, :, :]
        src = bank[0:TN, 0:ng * TN].rearrange("p (g c) -> p g c", g=ng)[:, :, 0:NT * GR].rearrange("p g (s d) -> p g s d", d=GR)
        alias = [[t_cvt], [t_uns], [t_xt_done], [t_xt_done]][r]
        t_at_tile[t] = Q.act(lambda e: e.activation(dst, src, ACT.Copy), [tm] + ring_free[r] + alias)
        t_bank[bk] = t_at_tile[t]

    t_acc = [None, None]

    def apply_part(t, s0, s1, layer, acc, first_after):
        bank = PS[3 + acc]
        tm = None
        for s in range(s0, s1):
            tm = Q.pe(lambda e, s=s: e.matmul(bank[0:TN, 0:CH], RING[0:TN, t % NRING, s * TN:(s + 1) * TN], HP[layer][:, s, :], start=(s == 0), stop=(s == NT - 1)), [t_hp[layer][s]] + first_after, last=(s == NT - 1))
        return tm

    t_z = [None] * 4
    t_ht = [None, None]
    t_pt = [None]
    t_pm = [None]

    def post1_vec(t, tm, acc):
        z, h = ZB[0], ZB[1]
        t1 = Q.dve(lambda e: e.tensor_tensor(z[:], PS[3 + acc][0:TN, 0:CH], HP[0][:, t, :], op=ALU.add), [tm, t_z[0]])
        t_acc[acc] = t1
        t2 = Q.dve(lambda e: e.scalar_tensor_tensor(z[:], z[:], DIS[:, t:t + 1], BB[0][:], op0=ALU.mult, op1=ALU.add), [t1, t_b])
        t3 = Q.dve(lambda e: e.scalar_tensor_tensor(h[:], z[:], 0.01, z[:], op0=ALU.mult, op1=ALU.max), [t2, t_z[1]])
        t_z[0] = t3
        return t3

    def transposes(src, t_src, k):
        for c in range(2):
            tp = Q.pe(lambda e, c=c: e.matmul(PS[5][:, c * TN:(c + 1) * TN], src[:, c * 128:(c + 1) * 128], IDN[0:TN, 0:TN], start=True, stop=True, is_transpose=True), [t_src, t_pt[0]], last=(c == 1))
        te = Q.act(lambda e: e.activation(HT[k][:], PS[5][:, 0:2 * TN].rearrange("p (k n) -> p k n", k=2), ACT.Copy), [tp, t_ht[k]])
        t_pt[0] = te
        return tp, te

    def post1_mm(t, te, k):
        for c in range(2):
            tm = Q.pe(lambda e, c=c: e.matmul(PS[6][0:TN, 0:CH], HT[k][:, c, :], W2S[:, c, :], start=(c == 0), stop=(c == 1)), [te, t_w2, t_pm[0]], last=(c == 1))
        t_ht[k] = tm
        tv = Q.act(lambda e: e.activation(HP[1][:, t, :], PS[6][0:TN, 0:CH], ACT.Copy, scale=DIS[:, t:t + 1]), [tm] + early_read)
        t_pm[0] = tv
        t_hp[1][t] = tv

    def dis_chain():
        d_deg = cnt("d_deg")
        tw = Q.dma(d_deg, DEGD.rearrange("(j p r) -> p j r", j=NJ, p=TN), DEG[:], list(t_deg))
        tr = Q.dma(d_deg, DGR[:], DEGD.rearrange("(t n) -> t n", t=NT), [tw])
        tp = Q.pe(lambda e: e.matmul(PS[7][0:TN, 0:NT], DGR[:], IDN[0:NT, 0:NT], start=True, stop=True, is_transpose=True), [tr, t_fldfree[0]], last=True)
        t1 = Q.dve(lambda e: e.tensor_scalar(DG[0][:], PS[7][0:TN, 0:NT], 1.0, None, op0=ALU.add), [tp])
        t_fldfree[0] = t1
        t2 = Q.dve(lambda e: e.tensor_scalar(DG[1][:], DG[0][:], 0.0, None, op0=ALU.is_gt), [t1])
        t3 = Q.dve(lambda e: e.tensor_tensor(DG[2][:], DG[0][:], DG[1][:], op=ALU.mult), [t2])
        t4 = Q.dve(lambda e: e.scalar_tensor_tensor(DG[0][:], DG[1][:], -1.0, DG[2][:], op0=ALU.mult, op1=ALU.add), [t3])
        t5 = Q.dve(lambda e: e.tensor_scalar(DG[2][:], DG[0][:], 1.0, None, op0=ALU.add), [t4])
        t6 = Q.act(lambda e: e.activation(DG[0][:], DG[2][:], ACT.Sqrt), [t5])
        t7 = Q.dve(lambda e: e.reciprocal(DG[2][:], DG[0][:]), [t6])
        t8 = Q.dve(lambda e: e.tensor_tensor(DIS[:], DG[2][:], DG[1][:], op=ALU.mult), [t7])
        for t in range(NT):
            t_hp[0][t] = Q.act(lambda e, t=t: e.activation(HP[0][:, t, :], HP[0][:, t, :], ACT.Copy, scale=DIS[:, t:t + 1]), [t8, t_raw[t]])

    early_read = []
    t_row = [None] * NJ
    d_rows = cnt("d_rows")
    t_pfree = [[], []]

    def rows_of_tiles(jj):
        src, dst = TSD[:, jj, 0:ROW], TSD[:, jj, ROW:2 * ROW]
        df, sf, dl, eq, p1, p2, ge = (x[:, :] for x in PF)
        a = list(t_pfree[0])
        t1 = Q.pool(lambda e: e.tensor_copy(df, dst), [t_tsd[jj]] + a)
        t2 = Q.pool(lambda e: e.tensor_copy(sf, src), a)
        t3 = Q.pool(lambda e: e.tensor_scalar(dl, df, K("v125", R)[:, jj:jj + 1], None, op0=ALU.subtract), [t1, t_con])
        t4 = Q.pool(lambda e: e.tensor_tensor(ge[:, 0:ROW - 1], df[:, 1:ROW], df[:, 0:ROW - 1], op=ALU.subtract))
        t5 = Q.pool(lambda e: e.tensor_scalar(p1, df, df[:, 0:1], BIG, op0=ALU.is_equal, op1=ALU.mult))
        t6 = Q.pool(lambda e: e.tensor_scalar(p2, df, df[:, ROW - 1:ROW], BIG, op0=ALU.is_equal, op1=ALU.mult))
        t7 = Q.pool(lambda e: e.tensor_copy(PB[:], dl), [t3])
        t8 = Q.pool(lambda e: e.tensor_scalar(eq[:, 0:ROW - 1], ge[:, 0:ROW - 1], 0.0, BIG, op0=ALU.is_equal, op1=ALU.mult), [t4])
        t10 = Q.pool(lambda e: e.tensor_scalar(PM[:, ROW + 1:2 * ROW + 1], p1, BIG, None, op0=ALU.subtract), [t5])
        t11 = Q.pool(lambda e: e.tensor_scalar(PM[:, 2 * ROW + 1:3 * ROW + 1], p2, BIG, None, op0=ALU.subtract), [t6])
        t8b = Q.pool(lambda e: e.tensor_scalar(PM[:, 1:ROW], eq[:, 0:ROW - 1], BIG, None, op0=ALU.subtract), [t8])
        t9 = Q.pool(lambda e: e.tensor_scalar(LF[:, jj, 0:ROW - 1], eq[:, 0:ROW - 1], -1.0 / BIG, 1.0, op0=ALU.mult, op1=ALU.add))
        t12 = Q.pool(lambda e: e.tensor_copy(FL[0][:, jj:jj + 1], df[:, 0:1]))
        t13 = Q.pool(lambda e: e.tensor_copy(FL[1][:, jj:jj + 1], df[:, ROW - 1:ROW]))
        t14 = Q.pool(lambda e: e.tensor_scalar(ge, dl, 0.0, None, op0=ALU.is_ge), [t3])
        t_row[jj] = t14
        return df, sf, dl, ge, t14

    def columns_of_tiles(jj, df, sf, dl, ge, t14):
        tv = Q.dve(lambda e: e.scalar_tensor_tensor(PX[0:R, :], dl, float(TN), ge, op0=ALU.is_lt, op1=ALU.mult, accum_out=VALT[:, jj:jj + 1]), [t14, t_fields[-1]] + t_pfree[1])
        td = Q.dma(d_rows, DLBD[jj * R:(jj + 1) * R, :], PB[:], [t14, t_pm0])
        td = Q.dma(d_rows, M3D[jj * R:(jj + 1) * R, :], PM[:], [t14])
        for half in range(2):
            for f, x in ((0, sf), (1, dl)):
                tp = Q.pe(lambda e, x=x, f=f, half=half: e.matmul(PS[7][:, (half * 2 + f) * R:(half * 2 + f + 1) * R], x[:, half * 128:(half + 1) * 128], IDN[0:R, 0:R], start=True, stop=True, is_transpose=True), [t14, t_fldfree[0]], last=(half == 1 and f == 1))
        v = PS[7][:, 0:4 * R].rearrange("p (h f n) -> p h f n", h=2, f=2)
        te1 = Q.dve(lambda e: e.tensor_copy(SRCI[:, jj, :, :], v[:, :, 0, :]), [tp])
        te2 = Q.dve(lambda e: e.tensor_copy(DLS[:, jj, :, :], v[:, :, 1, :]))
        t_fldfree[0] = te2
        t_pfree[0] = [tp, tv, td]
        t_pfree[1] = [tv]
        return te2

    def chains_of_rows():
        tp = Q.pe(lambda e: e.matmul(PS[7][0:R, 0:NJ], K("sh85", R), FL[0][:], start=True, stop=True), [t_row[-1], t_fldfree[0]], last=True)
        t1 = Q.dve(lambda e: e.tensor_scalar(FL[2][:], PS[7][0:R, 0:NJ], K("k16", R), None, op0=ALU.add), [tp])
        t2 = Q.dve(lambda e: e.tensor_tensor(FL[3][:], FL[0][:], FL[1][:], op=ALU.is_equal))
        t3 = Q.dve(lambda e: e.tensor_tensor(FL[4][:], FL[2][:], FL[1][:], op=ALU.is_equal), [t1])
        t4 = Q.dve(lambda e: e.tensor_scalar(CS[:, :, 0], FL[3][:], 1.0, BIG, op0=ALU.subtract, op1=ALU.mult), [t2])
        t5 = Q.dve(lambda e: e.tensor_scalar(CS[:, :, 1], FL[4][:], 1.0, BIG, op0=ALU.subtract, op1=ALU.mult), [t3])
        t6 = Q.dve(lambda e: e.tensor_scalar(LF[:, :, ROW - 1], FL[4][:], -1.0, 1.0, op0=ALU.mult, op1=ALU.add), [t3])
        d_cs = cnt("d_cs")
        tw = Q.dma(d_cs, CSD.rearrange("j p c -> p j c"), CS[:], [t5])
        tr = Q.dma(d_cs, CSB[:].rearrange("p n c -> p (n c)"), CSD.rearrange("(o j) p c -> o (j p c)", o=1).broadcast_to([4, 2 * NROW]), [tw])
        t_fldfree[0] = t6
        for jj in range(NJ):
            for half in range(2):
                tq = Q.pe(lambda e, jj=jj, half=half: e.matmul(PS[7][:, half * R:(half + 1) * R], LF[:, jj, half * 128:(half + 1) * 128], IDN[0:R, 0:R], start=True, stop=True, is_transpose=True), [t6, t_fldfree[0]], last=(half == 1))
            t_fldfree[0] = Q.dve(lambda e, jj=jj: e.tensor_copy(LAST[:, jj, :, :], PS[7][:, 0:2 * R].rearrange("p (h n) -> p h n", h=2)), [tq])
        t7 = Q.dve(lambda e: e.memset(CRF[:, 0:1], -BIG))
        t8 = Q.dve(lambda e: e.tensor_copy(CRF[:, 1:1 + NROW], CSB[:, :, 1]), [tr])
        t9 = Q.dve(lambda e: e.tensor_tensor(ARV[:], CSB[:, :, 0], CSB[:, :, 1], op=ALU.add), [tr])
        t10 = Q.dve(lambda e: e.tensor_tensor(AFW[:], CSB[:, :, 0], CRF[:, 0:NROW], op=ALU.add), [t7, t8])
        return t10

    def verdict():
        t1 = Q.dve(lambda e: e.tensor_reduce(STAT[0:TN, 0:1], VAL[:], axis=AX.X, op=ALU.add), [t_fields[-1], t_stat])
        t2 = Q.dve(lambda e: e.tensor_reduce(STAT[0:R, 1:2], VALT[:], axis=AX.X, op=ALU.add), t_pfree[1])
        tp = Q.pe(lambda e: e.matmul(PS[7][0:1, 0:3], K("ones"), STAT[:, 0:3], start=True, stop=True), [t1, t2, t_uns, t_fldfree[0]], last=True)
        t3 = Q.dve(lambda e: e.tensor_scalar(SUMS[:, 0:2], PS[7][0:1, 0:2], float(E), None, op0=ALU.not_equal), [tp])
        t4 = Q.dve(lambda e: e.tensor_scalar(SUMS[:, 2:3], PS[7][0:1, 2:3], 0.0, None, op0=ALU.not_equal))
        t5 = Q.dve(lambda e: e.tensor_reduce(SUMS[:, 4:5], SUMS[:, 0:3], axis=AX.X, op=ALU.max), [t3, t4])
        t_fldfree[0] = t4
        return Q.dve(lambda e: e.tensor_copy(FLAG[:, 0:1], SUMS[:, 4:5]), [t5])

    def attention_weights():
        prev = []
        for l in range(2):
            H = HS[l]
            if H == 4:
                for half in range(2):
                    t = Q.dve(lambda e, l=l, half=half: e.tensor_scalar(AB[l][:, half, :], K("mb"), ATC[l][:, half:half + 1], 0.4, op0=ALU.mult, op1=ALU.mult), [t_at, t_con])
            else:
                t0 = Q.dve(lambda e, l=l: e.memset(AB[l][:], 0.0))
                t = Q.dve(lambda e, l=l: e.tensor_scalar(AB[l][:, :, 0], ATC[l][:], 0.4, None, op0=ALU.mult), [t0, t_at])
            for W in (WL[l], WR[l]):
                at = ATB[l][:].unsqueeze(1).broadcast_to([128, 2, CH])
                t1 = Q.dve(lambda e, W=W, at=at: e.tensor_tensor(ATW[0][:], W[:, :, 0:CH], at, op=ALU.mult), [t_wl, t_at] + prev)
                t2 = Q.dve(lambda e, H=H: e.tensor_reduce(ATR[:, :, 0:H], ATW[0][:].rearrange("p k (h c) -> p k h c", h=H), axis=AX.X, op=ALU.add), [t1] + prev)
                t3 = Q.dve(lambda e, W=W, H=H: e.tensor_scalar(W[:, :, CH:CH + H], ATR[:, :, 0:H], 0.6, None, op0=ALU.mult), [t2])
                prev = [t3]
            t4 = Q.dve(lambda e, l=l: e.tensor_scalar(ATB[l][:], ATB[l][:], 0.4, None, op0=ALU.mult), prev)
            prev = [t4]
        z = Q.dve(lambda e: e.memset(ARX[1][:].bitcast(F32), 0.0))
        return [t4, z]

    PX = GF[5]
    t_pm0 = Q.pool(lambda e: e.memset(PM[:], 0.0))

    pending = list(range(NJ))

    def prepare(j):
        t6, _, t8 = fields(j)
        degrees(j, t6)
        field_transposes(j, t8)
        early_read.append(t_deg[j])

    prepare(pending.pop(0))
    stored = [None] * NRING
    last1 = {}
    t_rows_ready = []
    parts = [round(i * NT / len(quart)) for i in range(len(quart) + 1)]
    for it in range(NT + LG + 2):
        ta = it - LG
        for q in range(len(quart)):
            if it < NT:
                build_quartet(it, q)
            if q == 1 and ta - 1 in last1:
                t_h = post1_vec(ta - 1, last1[ta - 1], (ta - 1) % 2)
            if q == 3 and ta - 1 in last1:
                t_z[1], t_te = transposes(ZB[1], t_h, ta % 2)
            if q == 5 and ta - 1 in last1:
                post1_mm(ta - 1, t_te, ta % 2)
            if 0 <= ta < NT:
                tm = apply_part(ta, parts[q], parts[q + 1], 0, ta % 2, [t_at_tile[ta], t_acc[ta % 2]])
        if it < NT:
            r = it % NRING
            stored[r] = Q.dma(d_ad[r], AD[it], RING[0:TN, r, :], [t_at_tile[it]])
        if 0 <= ta < NT:
            ring_free[ta % NRING] = [tm, stored[ta % NRING]]
            last1[ta] = tm
        if it < LG:
            for j in (pending if it == LG - 1 else pending[:1]):
                prepare(j)
            pending = [] if it == LG - 1 else pending[1:]
        if it == LG - 1:
            dis_chain()
            t_attw = attention_weights()
        if it in ROWS_AT:
            rows = rows_of_tiles(ROWS_AT.index(it))
        if it - 1 in ROWS_AT:
            columns_of_tiles(ROWS_AT.index(it - 1), *rows)
        if it == ROWS_AT[-1] + 2:
            early_read.append(t_row[-1])
            t_chain = chains_of_rows()
            t_flag = verdict()

    order = list(range(NT - NRING, NT)) + list(range(NT - NRING))
    slot = {t: t % NRING for t in order[:NRING]}
    for i in range(NRING, NT):
        slot[order[i]] = slot[order[i - NRING]]
    t_in = {t: t_at_tile[t] for t in order[:NRING]}
    d_xs = [cnt(f"d_xs{i}") for i in range(3)]
    d_xo, d_tab = [cnt(f"d_xo{i}") for i in range(2)], [[cnt(f"d_tab{l}{i}") for i in range(2)] for l in range(2)]
    d_xr = [[cnt(f"d_xro{l}{i}") for i in range(2)] for l in range(2)]
    t_xsfree = [t_xt_read[i] for i in range(3)]
    t_sm = [None, None]
    t_x1 = {}
    t_tab = [[], []]
    t_xro = [{}, {}]
    t_xl, t_xrs = [None, None], [None, None]

    def norm(y, t_y, yc, out, sm, t_sum, free, sq):
        t1 = Q.dve(lambda e: e.tensor_scalar(sm[:, 1:2], sm[:, 0:1], -1.0 / CH, None, op0=ALU.mult), [t_sum])
        t2 = Q.dve(lambda e: e.tensor_scalar(yc, y, sm[:, 1:2], None, op0=ALU.add), [t1, t_y])
        t3 = Q.act(lambda e: e.activation(sq, yc, ACT.Square, accum_out=sm[:, 2:3]), [t2])
        t4 = Q.dve(lambda e: e.tensor_scalar(sm[:, 3:4], sm[:, 2:3], 1.0 / CH, EPS, op0=ALU.mult, op1=ALU.add), [t3])
        t5 = Q.act(lambda e: e.activation(sm[:, 4:5], sm[:, 3:4], ACT.Sqrt), [t4])
        t6 = Q.dve(lambda e: e.reciprocal(sm[:, 5:6], sm[:, 4:5]), [t5])
        return Q.dve(lambda e: e.tensor_scalar(out, yc, sm[:, 5:6], None, op0=ALU.mult), [t6] + free)

    def post2_vec(i, t, tm):
        acc, b = i % 2, i % 3
        sm = SMALL[i % 2]
        z, y, yc, x1 = (ZB[k][:] for k in range(4))
        tl = t_xs[i]
        t1 = Q.dve(lambda e: e.tensor_tensor(z, PS[3 + acc][0:TN, 0:CH], HP[1][:, t, :], op=ALU.add), [tm, t_z[0]])
        t_acc[acc] = t1
        t2 = Q.dve(lambda e: e.scalar_tensor_tensor(y, z, DIS[:, t:t + 1], BB[1][:], op0=ALU.mult, op1=ALU.add), [t1, t_z[1]])
        t3 = Q.dve(lambda e: e.scalar_tensor_tensor(z, y, 1.0, XST[b][:], op0=ALU.mult, op1=ALU.add, accum_out=sm[:, 0:1]), [t2, tl, t_sm[i % 2]])
        t_xsfree[b] = t3
        t4 = norm(z, t3, yc, x1, sm, t3, [t_z[3], t_x1read[0]], y)
        t_z[0] = t_z[1] = t_sm[i % 2] = t4
        t_z[3] = to = Q.dma(d_xo[i % 2], X1D[t * TN:(t + 1) * TN, :], x1, [t4])
        t_x1[t] = to
        return t4

    def tables(l, t, k, t_ht_ready, HTk, M1, M2, XLk, XRk, free1, free2, w, cols):
        H = HS[l]
        for c in range(2):
            tm1 = Q.pe(lambda e, c=c: e.matmul(M1[0:TN, 0:CH + H], HTk[:, c, :], WL[l][:, c, :], start=(c == 0), stop=(c == 1)), [t_ht_ready] + t_attw + free1, last=(c == 1))
        ta = Q.act(lambda e: e.activation(XLk[:, 0:CH + H], M1[0:TN, 0:CH + H], ACT.Copy), [tm1, t_xl[k]] + t_lsf[k])
        td = Q.dma(d_tab[l][k], TAB[l][t * TN:(t + 1) * TN, :], XLk[:, 0:CH + H], [ta])
        t_xl[k] = td
        t_tab[l].append(td)
        yield ta
        for c in range(2):
            tm2 = Q.pe(lambda e, c=c: e.matmul(M2[0:TN, 0:CH + H], HTk[:, c, :], WR[l][:, c, :], start=(c == 0), stop=(c == 1)), free2, last=(c == 1))
        t_ht[k] = tm2
        th = Q.act(lambda e: e.activation(XRk[:, 0:CH].bitcast(F32R), M2[0:TN, 0:CH], ACT.Copy), [tm2, t_xrs[k]])
        th2 = Q.act(lambda e: e.activation(ARX[l][:, t, 0, 0:H], M2[0:TN, CH:CH + H], ACT.Copy))
        yield th2
        tl = Q.dve(lambda e: e.tensor_tensor(XRk[:, CH:2 * CH].bitcast(F32R), M2[0:TN, 0:CH], XRk[:, 0:CH], op=ALU.subtract), [th2])
        tl2 = Q.dve(lambda e: e.tensor_tensor(ARX[l][:, t, 1, 0:H], M2[0:TN, CH:CH + H], ARX[l][:, t, 0, 0:H].bitcast(F32), op=ALU.subtract))
        td = Q.dma(d_xr[l][k], XRD[l][t], XRk[:], [tl])
        t_xrs[k] = td
        t_xro[l][t] = td
        t1 = Q.dve(lambda e: e.tensor_tensor(w[0], M2[0:TN, 0:CH], XLk[:, 0:CH], op=ALU.add), [ta] + cols)
        t2 = Q.dve(lambda e: e.tensor_tensor(LSF[l][:, t, :], M2[0:TN, CH:CH + H], XLk[:, CH:CH + H], op=ALU.add))
        yield t2
        ta2 = Q.act(lambda e: e.activation(w[1], w[0], ACT.Abs), [t1] + cols)
        t3 = Q.dve(lambda e: e.tensor_tensor(w[0], w[1], ATB[l][0:TN, :], op=ALU.mult), [ta2])
        t4 = Q.dve(lambda e: e.tensor_reduce(w[2][:, 0:H], w[0].rearrange("p (h c) -> p h c", h=H), axis=AX.X, op=ALU.add), [t3] + cols)
        t5 = Q.dve(lambda e: e.tensor_tensor(LSF[l][:, t, :], LSF[l][:, t, :], w[2][:, 0:H], op=ALU.add), [t4, t2])
        t_lsf[k] = [t5]
        yield t5

    t_lsf = [[], []]
    t_x1read = [None]
    t_wfree = []
    m_free = [[t_pm[0]], [t_fldfree[0]]]
    W2B = [GF[3][:], GF[4][:], SMALL[0][:, 8:12]]
    cuts = [round(i * NT / 8) for i in range(9)]
    prev = None
    t_xs = {}

    def load_x(i):
        b, t = i % 3, order[i]
        t_xs[i] = Q.dma(d_xs[b], XST[b][:], A["x"][t * TN:(t + 1) * TN, :], [t_xsfree[b]])

    load_x(0)
    for i in range(NT + 1):
        if i < NT:
            t = order[i]
            RT = RING[0:TN, slot[t], :]
        tab = None
        for q in range(8):
            if i < NT:
                for s in range(cuts[q], cuts[q + 1]):
                    tm = Q.pe(lambda e, s=s, RT=RT, i=i: e.matmul(PS[3 + i % 2][0:TN, 0:CH], RT[:, s * TN:(s + 1) * TN], HP[1][:, s, :], start=(s == 0), stop=(s == NT - 1)), [t_in[t], t_hp[1][s], t_acc[i % 2]], last=(s == NT - 1))
            if prev is not None:
                pt, t_v, k = prev
                if q == 3:
                    t_tp, t_te = transposes(ZB[3], t_v, k)
                    t_x1read[0] = t_tp
                if q == 5:
                    tab = tables(0, pt, k, t_te, HT[k], PS[6], PS[7], XL[k], XRS[k], m_free[0], m_free[1], W2B, list(t_wfree))
                    m_free[0] = [next(tab)]
                if q == 6:
                    next(tab)
                if q == 7:
                    m_free[1] = [next(tab)]
                    t_wfree = [next(tab)]
        if i < NT:
            if i + 1 < NT:
                load_x(i + 1)
            if i + NRING < NT:
                nx = order[i + NRING]
                t_in[nx] = Q.dma(d_ad[slot[nx]], RING[0:TN, slot[nx], :], AD[nx], [tm, stored[slot[nx]]])
            t_v = post2_vec(i, t, tm)
            prev = (t, t_v, i % 2)

    gcn_end = [(Q.done[n], Q.done[n].value) for n in ("tensor", "vector", "scalar", "gpsimd")]
    gcn_end += [(c, c.value) for c in d_ad + d_xo + d_tab[0] + d_xr[0] + [d_rows]]
    gcn.close()

    gat = ExitStack()
    ss = lambda name, shape, dt=F32: gat.enter_context(nc.sbuf_tensor(name, shape, dt))
    G = ss("g", [128, RP * 2 * (CH + 8)])
    OHT = [ss(f"oht{i}", [TN, KP * ROW], F32R) for i in range(2)]
    DLB = [ss(f"dlb{i}", [TN, KP * ROW], BF16) for i in range(2)]
    XR = [ss(f"xr{i}", [TN, 2 * CH], F32R) for i in range(2)]
    M3 = [ss(f"m3{i}", [4 * KP, 772], BF16) for i in range(2)]
    NAB = 3
    ABS = [ss(f"abs{i}", [128, 2 * ROW]) for i in range(NAB)]
    NOH = 4
    OH = [ss(f"oh{i}", [128, 2, TN + 1]) for i in range(NOH)]
    LSUM = ss("lsum", [128, 2 * 4 * KP])
    F1 = ss("f1", [4 * KP, ROW])
    F2 = ss("f2", [4 * KP, ROW])
    F3 = ss("f3", [4 * KP, ROW])
    EX = ss("ex", [4 * KP, ROW])
    SGM = ss("sgm", [4 * KP, 2 * KP])
    VW = ss("vw", [4, 2 * KP])
    CC = ss("cc", [4, 2, KP])
    CRL = ss("crl", [4 * KP, 2])
    XLT = [ss(f"xlt{i}", [TN, CH]) for i in range(2)]
    X1T = [ss(f"x1t{i}", [TN, CH]) for i in range(2)]
    SM = [ss(f"sm{i}", [TN, 64]) for i in range(2)]
    O = [ss(f"o{i}", [TN, CH]) for i in range(4)]
    HT2 = [ss(f"ht2{i}", [128, 2, TN]) for i in range(2)]
    XL2 = [ss(f"xl2{i}", [TN, CH + 1]) for i in range(2)]
    XRS2 = [ss(f"xrs2{i}", [TN, 2 * CH]) for i in range(2)]
    W2C = [ss(f"w2c{i}", [TN, CH]) for i in range(2)]
    W2D = ss("w2d", [TN, 4])
    NG5 = 5
    YC = [ss(f"yc{i}", [TN, NG5, CH]) for i in range(2)]
    SSQ = [ss(f"ssq{i}", [TN, 3, NG5]) for i in range(2)]

    d_g = [[cnt(f"d_g{i}{a}") for a in range(2)] for i in range(RP)]
    d_dlb = [cnt(f"d_dlb{i}") for i in range(2)]
    d_xri = [cnt(f"d_xri{i}") for i in range(2)]
    d_m3 = [cnt(f"d_m3{i}") for i in range(2)]
    d_xlt = [cnt(f"d_xlt{i}") for i in range(2)]
    d_x1t = [cnt(f"d_x1t{i}") for i in range(2)]
    d_out = [cnt(f"d_out{i}") for i in range(2)]

    for n in ("sync", "tensor", "vector", "scalar", "gpsimd"):
        Q.put(n, None, gcn_end)
    for k in range(2):
        t_xl[k] = t_xrs[k] = None
        t_lsf[k] = []
    t_ht[0] = t_ht[1] = None

    MT = (0, 1, 2, 7)
    NMT = len(MT)
    LB, BB_, AGG = 3, 4, (5, 6)
    t_mt = [None] * NMT
    t_abs = [None] * NAB
    t_oh2 = [None] * NOH
    t_gfree = [None] * RP
    t_g = {}
    t_oht = {}
    t_ohtfree = [[], []]
    t_dlbfree, t_xrfree, t_m3free = [None, None], [None, None], [None, None]
    t_lfree = [None]
    t_aggfree = [[], []]
    t_bfree = [None]
    t_xltfree, t_x1tfree = [None, None], [None, None]
    t_smfree = [[], []]
    t_o = [None] * 4
    t_cc0 = Q.dve(lambda e: e.memset(CC[:], -BIG))
    t_sgm = [None]
    t_ycfree = [[], []]
    CHUNKS = ((0, 4), (4, 8), (8, 12), (12, 17))

    def attention(l, tab_ready, xr_ready, x1_ready):
        H, HP_ = HS[l], HPN[l]
        KH, GW = KP * H, CH + 2 * H
        C = CH // H
        GV = G[:, 0:RP * 2 * GW].rearrange("p (r a c) -> p r a c", r=RP, a=2)
        sched = {}
        at = lambda it, fn: sched.setdefault(it, []).append(fn)
        t_dlb, t_xri, t_m3, t_xlt, t_x1t = {}, {}, {}, {}, {}

        def load_tile(t):
            b = t % 2
            t_dlb[t] = Q.dma(d_dlb[b], DLB[b][:], DLBD.rearrange("(t k) e -> t (k e)", t=NT)[t:t + 1, :].broadcast_to([TN, KP * ROW]), [t_dlbfree[b]])
            t_xri[t] = Q.dma(d_xri[b], XR[b][:].bitcast(F32), XRD[l][t], [xr_ready[t], t_xrfree[b]])

        def load_masks(t):
            b = t % 2
            for h in range(H):
                t_m3[t] = Q.dma(d_m3[b], M3[b][h * KP:(h + 1) * KP, :], M3D[t * KP:(t + 1) * KP, :], [t_m3free[b]])

        def load_self(t):
            b = t % 2
            t_xlt[t] = Q.dma(d_xlt[b], XLT[b][:], TAB[l][t * TN:(t + 1) * TN, 0:CH], [t_xltfree[b]])
            if l == 1:
                t_x1t[t] = Q.dma(d_x1t[b], X1T[b][:], X1D[t * TN:(t + 1) * TN, :], [t_x1tfree[b]])

        def place(t, k):
            return t // 5, (t % 5) * KP + k

        def gather(q):
            r = q % RP
            j, c = place(q // KP, q % KP)
            t_g[q] = [Q.put("gpsimd", lambda e, a=a: e.indirect_dma_start(out=GV[:, r, a, 0:CH + H], out_offset=None, in_=TAB[l], in_offset=off(SRCI[:, j, a, c:c + 1])), [t_gfree[r]] + (tab_ready if q == 0 else []), d_g[r][a], 16) for a in range(2)]

        def onehot_t(t, n):
            b = t % 2
            lo, hi = CHUNKS[n][0] * ROW, CHUNKS[n][1] * ROW
            tk = Q.dve(lambda e: e.tensor_scalar(OHT[b][:, lo:hi], DLB[b][:, lo:hi], K("pidx", TN), None, op0=ALU.is_equal), [t_dlb[t]] + t_ohtfree[b])
            t_oht[(l, t, n)] = tk
            if n == len(CHUNKS) - 1:
                t_dlbfree[b] = tk

        def expand(q):
            t, k = q // KP, q % KP
            b, r, bank = t % 2, q % RP, PS[MT[q % NMT]]
            n = min(k // 4, 3)
            first = [t_oht[(l, t, n)], t_xri[t], t_mt[q % NMT]]
            for half in range(2):
                for x in range(2):
                    Q.pe(lambda e, half=half, x=x: e.matmul(bank[:, half * ROW:(half + 1) * ROW], XR[b][:, x * CH + half * 128:x * CH + (half + 1) * 128], OHT[b][:, k * ROW:(k + 1) * ROW], start=(half == 0 and x == 0), stop=False, skip_group_check=True), first)
                    first = []
            for half in range(2):
                for a in range(2):
                    tm = Q.pe(lambda e, half=half, a=a: e.matmul(bank[:, half * ROW + a * 128:half * ROW + (a + 1) * 128], GV[:, r, a, half * 128:(half + 1) * 128], IDN, start=False, stop=(half == 1 and a == 1), is_transpose=True, skip_group_check=True), [t_g[q][a]], last=(half == 1 and a == 1))
            if k == KP - 1:
                t_xrfree[b] = tm
            ta = Q.act(lambda e: e.activation(ABS[q % NAB][:], bank[:], ACT.Abs), [tm, t_abs[q % NAB]])
            t_mt[q % NMT] = ta
            return ta

        def logits(q, ta):
            t, k = q // KP, q % KP
            b = t % 2
            first = [ta, t_lfree[0] if k == 0 else None]
            for a in range(2):
                s = 2 * k + a
                oh = OHT[b][:, k * ROW + a * 128:k * ROW + (a + 1) * 128]
                Lc = PS[LB][:, s * HP_:(s + 1) * HP_]
                Q.pe(lambda e, oh=oh, Lc=Lc: e.matmul(Lc, oh, ARX[l][:, t, 0, :], start=True, stop=False, skip_group_check=True), first)
                first = []
                Q.pe(lambda e, oh=oh, Lc=Lc: e.matmul(Lc, oh, ARX[l][:, t, 1, :], start=False, stop=False, skip_group_check=True))
                for half in range(2):
                    out = PS[LB][:, s * HP_ + 2 * half:s * HP_ + 2 * half + 2] if H == 4 else Lc
                    tm = Q.pe(lambda e, a=a, half=half, out=out: e.matmul(out, ABS[q % NAB][:, half * ROW + a * 128:half * ROW + (a + 1) * 128], AB[l][:, half, :], start=False, stop=(half == 1), skip_group_check=True), last=(half == 1 and a == 1))
            t_abs[q % NAB] = tm
            if k == KP - 1:
                t_ohtfree[b] = [tm]
            return tm

        def softmax_rows(t, tl, it):
            b = t % 2
            r0 = (t % 2) * KP
            F, Pm, Sm = M3[b][0:KH, 0:ROW + 1], M3[b][0:KH, ROW + 1:2 * ROW + 1], M3[b][0:KH, 2 * ROW + 1:3 * ROW + 1]
            bank = PS[BB_]
            Lrow = bank[0:KH, 0:ROW]
            S2 = K("sel2", KH)
            j, c0 = place(t, 0)
            st = {}

            def s0():
                L = PS[LB][:, 0:2 * KP * HP_].rearrange("p (k a h) -> p k a h", k=KP, a=2)[:, :, :, 0:H]
                al = GV[:, r0:r0 + KP, :, CH:CH + H]
                out = LSUM[:, 0:2 * KH].rearrange("p (a h k) -> p k a h", a=2, h=H)
                st["l"] = Q.dve(lambda e: e.tensor_tensor(out, L, al, op=ALU.add), [tl, st0[0]])
                t_lfree[0] = st["l"]

            def s1():
                for a in range(2):
                    tp = Q.pe(lambda e, a=a: e.matmul(bank[0:KH, a * 128:(a + 1) * 128], LSUM[:, a * KH:(a + 1) * KH], IDN, start=True, stop=True, is_transpose=True), [st["l"], t_bfree[0]], last=(a == 1))
                st0[0] = tp
                t1 = Q.dve(lambda e: e.tensor_tensor_scan(F1[0:KH, :], F[:, 0:ROW], Lrow, -BIG, op0=ALU.add, op1=ALU.max), [tp, t_m3[t], st1[0]])
                t2 = Q.dve(lambda e: e.tensor_tensor_scan(F2[0:KH, ::-1], F[:, ROW:0:-1], F1[0:KH, ::-1], -BIG, op0=ALU.add, op1=ALU.max), [t1, st1[0]])
                st["g"] = t2
                st["sg"] = Q.dve(lambda e: e.tensor_tensor(SGM[0:KH, :].rearrange("p (x k) -> p x k", x=2), S2.rearrange("p (x k) -> p x k", x=2), F2[0:KH, 0:ROW:ROW - 1].unsqueeze(2).broadcast_to([KH, 2, KP]), op=ALU.mult), [t2, st1[0]])

            def s2():
                chp = bank[0:H, ROW:ROW + 2 * KP]
                tp = Q.pe(lambda e: e.matmul(chp, K("hm", KH)[:, 0:H], SGM[0:KH, :], start=True, stop=True), [st["sg"]], last=True)
                row = slice(t * KP, (t + 1) * KP)
                t1 = Q.dve(lambda e: e.tensor_tensor_scan(VW[0:H, KP:2 * KP], AFW[0:H, row], chp[:, KP:2 * KP], -BIG, op0=ALU.add, op1=ALU.max), [tp, t_chain])
                t2 = Q.dve(lambda e: e.tensor_tensor_scan(VW[0:H, 0:KP][:, ::-1], ARV[0:H, row][:, ::-1], chp[:, 0:KP][:, ::-1], -BIG, op0=ALU.add, op1=ALU.max))
                t3 = Q.dve(lambda e: e.tensor_tensor(CC[0:H, 1, 1:KP], VW[0:H, KP:2 * KP - 1], CRF[0:H, t * KP + 1:(t + 1) * KP], op=ALU.add), [t1, t_cc0, st2[0]])
                st["cc"] = Q.dve(lambda e: e.tensor_tensor(CC[0:H, 0, 0:KP - 1], VW[0:H, 1:KP], CRF[0:H, t * KP + 1:(t + 1) * KP], op=ALU.add), [t2])

            def s3():
                exp_ = bank[0:KH, ROW + 64:ROW + 64 + 2 * KP]
                tp = Q.pe(lambda e: e.matmul(exp_, K("hmt", 4)[0:H, 0:KH], CC[0:H, :, :].rearrange("p x k -> p (x k)"), start=True, stop=True), [st["cc"]], last=True)
                st2[0] = tp
                t1 = Q.dve(lambda e: e.tensor_tensor(SGM[0:KH, :], exp_, S2, op=ALU.mult), [tp])
                t2 = Q.dve(lambda e: e.tensor_reduce(CRL[0:KH, :], SGM[0:KH, :].rearrange("p (x k) -> p x k", x=2), axis=AX.X, op=ALU.add), [t1])
                t3 = Q.dve(lambda e: e.scalar_tensor_tensor(F1[0:KH, :], Pm, CRL[0:KH, 1:2], F2[0:KH, :], op0=ALU.add, op1=ALU.max), [t2])
                t4 = Q.dve(lambda e: e.scalar_tensor_tensor(F3[0:KH, :], Sm, CRL[0:KH, 0:1], F1[0:KH, :], op0=ALU.add, op1=ALU.max), [t3, st3[0]])
                t_m3free[b] = t4
                st["m"] = t4
                t5 = Q.dve(lambda e: e.tensor_tensor(F2[0:KH, :], Lrow, F3[0:KH, :], op=ALU.subtract), [t4])
                st["e"] = Q.act(lambda e: e.activation(EX[0:KH, :], F2[0:KH, :], ACT.Exp), [t5, st3[0]])
                st1[0] = st["e"]

            def s4():
                for x, src in ((0, EX), (1, F3)):
                    for a in range(2):
                        tp = Q.pe(lambda e, x=x, a=a, src=src: e.matmul(bank[:, (2 * x + a) * KH:(2 * x + a + 1) * KH], src[0:KH, a * 128:(a + 1) * 128], IDN[0:KH, 0:KH], start=True, stop=True, is_transpose=True), [st["e"]], last=(x == 1 and a == 1))
                st3[0] = tp
                v = bank[:, 0:4 * KH].rearrange("p (x a h k) -> p x k a h", x=2, a=2, h=H)
                t1 = Q.dve(lambda e: e.tensor_copy(GV[:, r0:r0 + KP, :, CH:CH + H], v[:, 0]), [tp])
                lastv = LAST[:, j, :, c0:c0 + KP].rearrange("p a k -> p k a")
                t2 = Q.dve(lambda e: e.tensor_tensor(GV[:, r0:r0 + KP, :, CH + H:CH + 2 * H], v[:, 1], lastv.unsqueeze(3).broadcast_to([128, KP, 2, H]), op=ALU.mult))
                t_bfree[0] = t2
                t_ex[t] = t2

            for n, f in enumerate((s0, s1, s2, s3, s4)):
                at(it + n, f)

        st0, st1, st2, st3 = [None], [None], [None], [None]
        t_ex = {}

        def combine(q, it):
            t, k = q // KP, q % KP
            r, o = q % RP, q % NOH
            j, c = place(t, k)
            for a in range(2):
                t1 = Q.dve(lambda e, a=a: e.tensor_scalar(OH[o][:, a, :], IOTA, DLS[:, j, a, c:c + 1], None, op0=ALU.is_equal), [t_oh2[o]])
                rows = GV[:, r, a, 0:CH]
                if H == 1:
                    t2 = Q.dve(lambda e, a=a, rows=rows: e.tensor_scalar(rows, rows, GV[:, r, a, CH:CH + 1], None, op0=ALU.mult), [t_ex[t]])
                else:
                    rv = rows.rearrange("p (h c) -> p h c", h=H)
                    t2 = Q.dve(lambda e, a=a, rv=rv: e.tensor_tensor(rv, rv, GV[:, r, a, CH:CH + H].unsqueeze(2).broadcast_to([128, H, C]), op=ALU.mult), [t_ex[t]])
                tm = Q.pe(lambda e, a=a: e.matmul(PS[AGG[t % 2]][0:TN, 0:GW], OH[o][:, a, 0:TN], GV[:, r, a, 0:GW], start=(k == 0 and a == 0), stop=(k == KP - 1 and a == 1)), [t1, t2] + t_aggfree[t % 2], last=(a == 1))
            t_oh2[o] = t_gfree[r] = tm
            if k == KP - 1:
                finish(t, tm, it)

        def finish(t, tm, it):
            b = t % 2
            agg = PS[AGG[b]][0:TN, 0:GW]
            sm = SM[b]
            D, M = agg[:, CH:CH + H], agg[:, CH + H:CH + 2 * H]
            self_ = LSF[l][:, t, :]
            col = lambda n, w=1: sm[:, 4 * n:4 * n + w * H] if w == 1 else sm[:, 4 * n:4 * n + 8]
            e0, mf, mm = sm[:, 0:H], sm[:, 4:4 + H], sm[:, 8:8 + H]
            dd, rs = sm[:, 16:16 + 2 * H], sm[:, 24:24 + 2 * H]
            den, rec, fr = sm[:, 32:32 + H], sm[:, 36:36 + H], sm[:, 40:40 + 2 * H]
            st = {}
            o1, o2, o3, o4 = (x[:] for x in O)

            def f0():
                t1 = Q.dve(lambda e: e.tensor_scalar(e0, D, 0.0, -BIG, op0=ALU.is_equal, op1=ALU.mult), [tm] + t_smfree[b])
                t2 = Q.dve(lambda e: e.tensor_tensor(mf, M, e0, op=ALU.add), [t1])
                t3 = Q.dve(lambda e: e.tensor_tensor(mm, mf, self_, op=ALU.max), [t2])
                t4 = Q.dve(lambda e: e.tensor_tensor(dd[:, 0:H], mf, mm, op=ALU.subtract), [t3])
                t5 = Q.dve(lambda e: e.tensor_tensor(dd[:, H:2 * H], self_, mm, op=ALU.subtract))
                st["x"] = Q.act(lambda e: e.activation(rs, dd, ACT.Exp), [t5])

            def f1():
                t1 = Q.dve(lambda e: e.tensor_tensor(den, D, rs[:, 0:H], op=ALU.mult), [st["x"]])
                t2 = Q.dve(lambda e: e.tensor_tensor(e0, den, rs[:, H:2 * H], op=ALU.add), [t1])
                t3 = Q.dve(lambda e: e.reciprocal(rec, e0), [t2])
                t4 = Q.dve(lambda e: e.tensor_tensor(fr.rearrange("p (x h) -> p x h", x=2), rs.rearrange("p (x h) -> p x h", x=2), rec.unsqueeze(1).broadcast_to([TN, 2, H]), op=ALU.mult), [t3])
                hv = lambda x: x.rearrange("p (h c) -> p h c", h=H)
                st["a"] = Q.dve(lambda e: e.tensor_tensor(hv(o1), hv(agg[:, 0:CH]), fr[:, 0:H].unsqueeze(2).broadcast_to([TN, H, C]), op=ALU.mult), [t4, t_o[0]])
                st["b"] = Q.dve(lambda e: e.tensor_tensor(hv(o2), hv(XLT[b][:]), fr[:, H:2 * H].unsqueeze(2).broadcast_to([TN, H, C]), op=ALU.mult), [t_xlt[t], t_o[1]])
                t_smfree[b] = [st["b"]]
                t_xltfree[b] = st["b"]

            def f2():
                t1 = Q.dve(lambda e: e.tensor_tensor(o3, o1, o2, op=ALU.add), [st["b"], t_o[2]])
                st["o"] = Q.dve(lambda e: e.tensor_tensor(o1, o3, BB[2 + l][:], op=ALU.add), [t1])

            if l == 0:
                def f3():
                    t1 = Q.dve(lambda e: e.tensor_scalar(o2, o1, 0.0, None, op0=ALU.min), [st["o"]])
                    t2 = Q.act(lambda e: e.activation(o3, o2, ACT.Exp), [t1])
                    st["e"] = t2

                def f4():
                    t1 = Q.dve(lambda e: e.scalar_tensor_tensor(o2, o1, 0.0, o3, op0=ALU.max, op1=ALU.add), [st["e"]])
                    st["h"] = Q.dve(lambda e: e.tensor_scalar(o4, o2, -1.0, None, op0=ALU.add), [t1, t_o[3]])
                    t_o[0] = t_o[1] = t_o[2] = st["h"]

                def f5():
                    bank = PS[AGG[b]]
                    for c in range(2):
                        tp = Q.pe(lambda e, c=c: e.matmul(bank[:, c * TN:(c + 1) * TN], o4[:, c * 128:(c + 1) * 128], IDN[0:TN, 0:TN], start=True, stop=True, is_transpose=True), [st["h"]], last=(c == 1))
                    t_o[3] = tp
                    te = Q.act(lambda e: e.activation(HT2[b][:], bank[:, 0:2 * TN].rearrange("p (k n) -> p k n", k=2), ACT.Copy), [tp, t_ht[b]])
                    st["tab"] = tables(1, t, b, te, HT2[b], bank, bank, XL2[b], XRS2[b], [], [], [W2C[0][:], W2C[1][:], W2D], list(t_wfree2))

                def f6():
                    st["m1"] = next(st["tab"])

                def f7():
                    Q.put("tensor", None, [st["m1"]])
                    next(st["tab"])

                def f8():
                    next(st["tab"])

                def f9():
                    t_wfree2[:] = [next(st["tab"])]
                    t_aggfree[b] = list(t_wfree2)

                steps = (f0, f1, f2, f3, f4, f5, f6, f7, f8, f9)
            else:
                g, n = divmod(t, NG5)
                y = g % 2
                yc = YC[y]

                def f3():
                    t1 = Q.dve(lambda e: e.scalar_tensor_tensor(o2, o1, 1.0, X1T[b][:], op0=ALU.mult, op1=ALU.add, accum_out=sm[:, 48:49]), [st["o"], t_x1t[t]])
                    t_x1tfree[b] = t1
                    t2 = Q.dve(lambda e: e.tensor_scalar(sm[:, 49:50], sm[:, 48:49], -1.0 / CH, None, op0=ALU.mult), [t1])
                    t3 = Q.dve(lambda e: e.tensor_scalar(yc[:, n, :], o2, sm[:, 49:50], None, op0=ALU.add), [t2] + t_ycfree[y])
                    t4 = Q.act(lambda e: e.activation(o3, yc[:, n, :], ACT.Square, accum_out=SSQ[y][:, 0, n:n + 1]), [t3])
                    t_o[0] = t_o[1] = t_o[2] = t4
                    t_smfree[b].append(t3)
                    st["n"] = t4
                    t_aggfree[b] = [st["a"]]

                def f4():
                    if n == NG5 - 1 or t == NT - 1:
                        w = n + 1
                        t1 = Q.dve(lambda e: e.tensor_scalar(SSQ[y][:, 1, 0:w], SSQ[y][:, 0, 0:w], 1.0 / CH, EPS, op0=ALU.mult, op1=ALU.add), [st["n"]])
                        t2 = Q.act(lambda e: e.activation(SSQ[y][:, 2, 0:w], SSQ[y][:, 1, 0:w], ACT.Sqrt), [t1])
                        t3 = Q.dve(lambda e: e.reciprocal(SSQ[y][:, 1, 0:w], SSQ[y][:, 2, 0:w]), [t2])
                        for i in range(w):
                            t4 = Q.dve(lambda e, i=i: e.tensor_scalar(yc[:, i, :], yc[:, i, :], SSQ[y][:, 1, i:i + 1], None, op0=ALU.mult), [t3])
                        t0 = t - n
                        td = Q.dma(d_out[y], A["out"][t0 * TN:(t + 1) * TN, :].rearrange("(t p) c -> p t c", p=TN), yc[:, 0:w, :], [t4])
                        t_ycfree[y] = [td]

                steps = (f0, f1, f2, f3, f4)
            for n_, f in enumerate(steps):
                at(it + 1 + n_, f)

        t_wfree2 = []
        LEAD = RP - LAGC
        load_tile(0)
        load_masks(0)
        for n in range(4):
            onehot_t(0, n)
        for q in range(min(LEAD, NP)):
            gather(q)
        t_a = {}
        it = 0
        last = NP + LAGC + 12
        for it in range(last):
            if it < NP:
                t, k = it // KP, it % KP
                if k == 2 and t + 1 < NT:
                    load_tile(t + 1)
                if k == 9 and t + 1 < NT:
                    load_masks(t + 1)
                if k in (4, 8, 12, 15) and t + 1 < NT:
                    onehot_t(t + 1, (4, 8, 12, 15).index(k))
                t_a[it] = expand(it)
            if it >= LAGC + 6 and (it - LAGC - 6) % KP == 0 and (it - LAGC - 6) // KP < NT:
                load_self((it - LAGC - 6) // KP)
            for f in sched.pop(it, []):
                f()
            if 0 <= it - LAGC < NP:
                combine(it - LAGC, it)
            if 0 <= it - 1 < NP:
                tl = logits(it - 1, t_a[it - 1])
                if it % KP == 0:
                    softmax_rows(it // KP - 1, tl, it + 1)
            if LEAD <= it + LEAD < NP and it >= 0:
                gather(it + LEAD)
        assert not sched

    attention(0, t_tab[0], t_xro[0], None)
    attention(1, t_tab[1], t_xro[1], None)

    ended = [(Q.done[n], Q.done[n].value) for n in Q.done] + [(c, c.value) for c in d_out + d_tab[1] + d_xr[1]]
    for n in Q.lists:
        Q.put(n, None, ended)
    gat.close()
    W = {"2": W2S, "l0": WL[0], "r0": WR[0], "l1": WL[1], "r1": WR[1]}
    return ctx, Q, FLAG, general_path(nc, ctx, sem, A, NT, E, PS, IOTA, IDN, K("pidx", TN), W, BB, DIS)


class Serial:

    ENGINES = ("sync", "tensor", "vector", "scalar", "gpsimd")

    def __init__(self, sem):
        self.chain, self.met, self.rows = sem("g_chain"), sem("g_met"), sem("g_rows")
        self.go = {n: sem(f"g_go_{n}") for n in self.ENGINES if n != "gpsimd"}
        self.rounds = []

    def once(self, *steps):
        self.rounds.append((None, steps))

    def loop(self, count, *steps):
        self.rounds.append((count, steps))

    def run(self, name, e, steps, i):
        at = gathered = 0
        for engine, fns in steps:
            if engine == name:
                if at:
                    e.wait_ge(self.chain, at)
                for f in fns:
                    ins = f(e, i)
                    if engine == "sync":
                        ins.then_inc(self.chain, 16)
                if engine == "gpsimd":
                    gathered += 16
                    ins.then_inc(self.rows, 16)
                    e.wait_ge(self.rows, gathered)
                    e.sem_inc(self.chain, 1)
                elif engine != "sync":
                    ins.then_inc(self.chain, 1)
            at += 16 * len(fns) if engine == "sync" else 1
        e.wait_ge(self.chain, at)
        if name == "gpsimd":
            e.wait_ge(self.met, len(self.go))
            e.sem_clear(self.chain)
            if gathered:
                e.dma_reset(range(self.rows.num, self.rows.num + 1))
                e.sem_clear(self.rows)
            e.sem_inc(self.met, -len(self.go))
            for g in self.go.values():
                e.sem_inc(g, 1)
        else:
            e.sem_inc(self.met, 1)
            e.wait_ge(self.go[name], 1)
            e.sem_inc(self.go[name], -1)

    def emit(self, name, e):
        for count, steps in self.rounds:
            if count is None:
                self.run(name, e, steps, None)
            else:
                with e.Fori(0, count) as i:
                    self.run(name, e, steps, i)


def general_path(nc, ctx, sem, A, NT, E, PS, IOTA, IDN, PIDX, W, BB, DIS):
    N = NT * TN
    NR = A["sdr"].shape[0]
    CK = 4
    HS = (4, 1)
    sb = lambda name, shape, dt=F32: ctx.enter_context(nc.sbuf_tensor(f"g_{name}", shape, dt))
    dram = lambda name, shape, dt=F32: nc.dram_tensor(f"g_{name}", shape, dt, kind="Internal").ap()
    S = Serial(sem)
    off = lambda ap: bass.IndirectOffsetOnAxis(ap=ap, axis=0)

    DISD = dram("dis_d", (NT, TN, 1))
    HPD = [dram(f"hp{k}_d", (NT, TN, CH)) for k in range(2)]
    ACCD = dram("acc_d", (NT, TN, CH + 4))
    X1 = dram("x1_d", (NT, TN, CH))
    XLD = [dram(f"xl{l}_d", (NT, TN, CH)) for l in range(2)]
    XRD = [dram(f"xr{l}_d", (N + 1, CH)) for l in range(2)]
    LSD = [dram(f"ls{l}_d", (NT, TN, 4)) for l in range(2)]
    LGE = [dram(f"lge{l}_d", (NR, 128, HS[l])) for l in range(2)]
    LGR = [dram(f"lgr{l}_d", (NR, HS[l], 128)) for l in range(2)]
    MXD = [dram(f"mx{l}_d", (N + 1, 4)) for l in range(2)]

    NIO, OHA = sb("nio", [128, N]), sb("oha", [128, N])
    NID = sb("nid", [TN, NT])
    ATG = [sb(f"atg{l}", [128, CH]) for l in range(2)]
    ACC = sb("acc", [TN, NT, CH + 4])
    DGA = [sb(f"dga{k}", [TN, NT]) for k in range(4)]
    SDI, DF, DC, DI, EWC = sb("sdi", [128, 2], I32), sb("df", [128, 1]), sb("dc", [128, 1]), sb("di", [128, 1], I32), sb("ewc", [128, 1])
    GR, GX, GW_ = sb("gr", [128, CH + 4]), sb("gx", [128, CH]), sb("gw", [128, CH])
    LE, LX, MXG, LER = sb("le", [128, 4]), sb("lx", [128, 4]), sb("mxg", [128, 4]), sb("ler", [4, 128])
    DBI, DBF, MK = sb("dbi", [TN, CK * 128], I32), sb("dbf", [TN, CK * 128]), sb("mk", [TN, CK * 128])
    LB, TMP = sb("lb", [TN, CK * 4 * 128]), sb("tmp", [TN, CK * 4 * 128])
    MXA, LSA, MXT = sb("mxa", [TN, NT, 4]), sb("lsa", [TN, NT, 4]), sb("mxt", [TN, 4])
    DIT = sb("dit", [NT, TN])
    W = {"1": sb("w1", [128, 2, CH]), **W}
    ROWP = sb("rowp", [1, CH])
    BIGR = sb("bigr", [1, 4])
    X, Y, Z, AC, T1, T2 = (sb(n, [TN, CH + 4]) for n in ("x", "y", "z", "ac", "t1", "t2"))
    HT = sb("ht", [128, 2, TN])
    DSC, SM, LST = sb("dsc", [TN, 1]), sb("sm", [TN, 8]), sb("lst", [TN, 4])

    dve = lambda *f: ("vector", f)
    act = lambda *f: ("scalar", f)
    pe = lambda *f: ("tensor", f)
    gather = lambda out, table, idx: ("gpsimd", [lambda e, i: e.indirect_dma_start(out=out, out_offset=None, in_=table, in_offset=off(idx))])
    dma = lambda *f: ("sync", [(lambda e, i, x=x: e.dma_start(*x(i))) for x in f])
    at = lambda arr, i: arr[bass.ds(i, 1)].rearrange("a p c -> (a p) c")
    flat = lambda arr: arr.rearrange("t p c -> (t p) c")
    xv = A["x"].rearrange("(t p) c -> t p c", p=TN)
    ov = A["out"].rearrange("(t p) c -> t p c", p=TN)
    x_, y_, z_, t1_, t2_ = (b[:, 0:CH] for b in (X, Y, Z, T1, T2))

    def project(src, Wm):
        return [pe(*[lambda e, i, c=c: e.matmul(PS[0][:, c * TN:(c + 1) * TN], src[:, c * 128:(c + 1) * 128], IDN[0:TN, 0:TN], start=True, stop=True, is_transpose=True) for c in range(2)]),
                act(lambda e, i: e.activation(HT[:], PS[0][:, 0:2 * TN].rearrange("p (k n) -> p k n", k=2), ACT.Copy)),
                pe(*[lambda e, i, c=c: e.matmul(PS[1][0:TN, 0:CH], HT[:, c, :], Wm[:, c, 0:CH], start=(c == 0), stop=(c == 1)) for c in range(2)])]

    targets = [dma(lambda i: (SDI[:], at(A["sdr"], i))),
               dve(lambda e, i: e.tensor_copy(DF[:], SDI[:, 1:2])),
               dve(lambda e, i: e.tensor_scalar(DC[:], DF[:], float(N), None, op0=ALU.min)),
               dve(lambda e, i: e.tensor_copy(DI[:], DC[:]))]
    onehot = dve(lambda e, i: e.tensor_scalar(OHA[:], NIO[:], DF[:, 0:1], None, op0=ALU.is_equal))

    def aggregate(w):
        steps = []
        for t0 in range(0, NT, 8):
            ts = range(t0, min(t0 + 8, NT))
            steps.append(pe(*[lambda e, i, t=t: e.matmul(PS[t % 8][0:TN, 0:w], OHA[:, t * TN:(t + 1) * TN], GR[:, 0:w], start=True, stop=True) for t in ts]))
            steps.append(dve(*[lambda e, i, t=t: e.tensor_tensor(ACC[:, t, 0:w], ACC[:, t, 0:w], PS[t % 8][0:TN, 0:w], op=ALU.add) for t in ts]))
        return steps

    clear = dve(lambda e, i: e.memset(ACC[:], 0.0))
    keep = dma(lambda i: (ACCD.rearrange("t p c -> p t c"), ACC[:]))

    def weighted(table):
        S.once(clear)
        S.loop(NR, *targets, dma(lambda i: (EWC[:], at(A["ewr"], i))), onehot, gather(GR[:, 0:CH], table, SDI[:, 0:1]),
               dve(lambda e, i: e.tensor_scalar(GR[:, 0:CH], GR[:, 0:CH], EWC[:, 0:1], None, op0=ALU.mult)), *aggregate(CH))
        S.once(keep)

    def normed(src, out):
        return [dve(lambda e, i: e.tensor_scalar(SM[:, 1:2], SM[:, 0:1], -1.0 / CH, None, op0=ALU.mult)),
                dve(lambda e, i: e.tensor_scalar(t1_, src, SM[:, 1:2], None, op0=ALU.add)),
                act(lambda e, i: e.activation(t2_, t1_, ACT.Square, accum_out=SM[:, 2:3])),
                dve(lambda e, i: e.tensor_scalar(SM[:, 3:4], SM[:, 2:3], 1.0 / CH, EPS, op0=ALU.mult, op1=ALU.add)),
                act(lambda e, i: e.activation(SM[:, 4:5], SM[:, 3:4], ACT.Sqrt)),
                dve(lambda e, i: e.reciprocal(SM[:, 5:6], SM[:, 4:5])),
                dve(lambda e, i: e.tensor_scalar(out, t1_, SM[:, 5:6], None, op0=ALU.mult))]

    def logits(l, a, b, p, tmp, out):
        H = HS[l]
        return [dve(lambda e, i: e.tensor_tensor(tmp, a, b, op=ALU.add)),
                dve(lambda e, i: e.scalar_tensor_tensor(b, tmp, 0.2, tmp, op0=ALU.mult, op1=ALU.max)),
                dve(lambda e, i: e.tensor_tensor(tmp, b, ATG[l][0:p, :], op=ALU.mult)),
                dve(lambda e, i: e.tensor_reduce(out[:, 0:H], tmp.rearrange("p (h c) -> p h c", h=H), axis=AX.X, op=ALU.add))]

    def sides(l, src):
        return [*project(src, W[f"l{l}"]), act(lambda e, i: e.activation(t1_, PS[1][0:TN, 0:CH], ACT.Copy)),
                *project(src, W[f"r{l}"]), act(lambda e, i: e.activation(t2_, PS[1][0:TN, 0:CH], ACT.Copy)),
                dma(lambda i: (at(XLD[l], i), t1_), lambda i: (at(XRD[l][0:N].rearrange("(t p) c -> t p c", p=TN), i), t2_)),
                *logits(l, t1_, t2_, TN, y_, LST[:]),
                dma(lambda i: (at(LSD[l], i), LST[:]))]

    S.once(dve(*[lambda e, i, t=t: e.tensor_scalar(NIO[:, t * TN:(t + 1) * TN], IOTA[:, 0:TN], float(t * TN), None, op0=ALU.add) for t in range(NT)],
               *[lambda e, i, t=t: e.tensor_scalar(NID[:, t:t + 1], PIDX, float(t * TN), None, op0=ALU.add) for t in range(NT)],
               lambda e, i: e.memset(DGA[0][:], 0.0), lambda e, i: e.memset(LST[:], 0.0), lambda e, i: e.memset(ROWP[:], 0.0), lambda e, i: e.memset(BIGR[:], BIG)),
           dma(lambda i: (W["1"][:], A["W1"].rearrange("(k p) n -> p k n", p=128)), *[lambda i, l=l: (ATG[l][:], A[f"att{l + 1}"].broadcast_to([128, CH])) for l in range(2)],
               *[lambda i, l=l: (XRD[l][N:N + 1], ROWP[:]) for l in range(2)],
               *[lambda i, l=l: (MXD[l][N:N + 1], BIGR[:]) for l in range(2)]))

    S.loop(NR, *targets, dma(lambda i: (EWC[:], at(A["ewr"], i))), onehot,
           pe(*[lambda e, i, t=t: e.matmul(PS[0][0:TN, t:t + 1], OHA[:, t * TN:(t + 1) * TN], EWC[:], start=True, stop=True) for t in range(NT)]),
           dve(lambda e, i: e.tensor_tensor(DGA[0][:], DGA[0][:], PS[0][0:TN, 0:NT], op=ALU.add)))
    a, b, c, d = (x[:] for x in DGA)
    S.once(dve(lambda e, i: e.tensor_scalar(b, a, 1.0, None, op0=ALU.add)),
           dve(lambda e, i: e.tensor_scalar(c, b, 0.0, None, op0=ALU.is_gt)),
           dve(lambda e, i: e.tensor_tensor(d, b, c, op=ALU.mult)),
           dve(lambda e, i: e.scalar_tensor_tensor(b, c, -1.0, d, op0=ALU.mult, op1=ALU.add)),
           dve(lambda e, i: e.tensor_scalar(d, b, 1.0, None, op0=ALU.add)),
           act(lambda e, i: e.activation(b, d, ACT.Sqrt)),
           dve(lambda e, i: e.reciprocal(d, b)),
           dve(lambda e, i: e.tensor_tensor(DIS[:], d, c, op=ALU.mult)),
           pe(lambda e, i: e.matmul(PS[0][0:NT, 0:TN], DIS[:], IDN[0:TN, 0:TN], start=True, stop=True, is_transpose=True)),
           act(lambda e, i: e.activation(DIT[:], PS[0][0:NT, 0:TN], ACT.Copy)),
           dma(lambda i: (DISD.rearrange("t p c -> t (p c)"), DIT[:])))

    S.loop(NT, dma(lambda i: (x_, at(xv, i)), lambda i: (DSC[:], at(DISD, i))), *project(x_, W["1"]),
           act(lambda e, i: e.activation(y_, PS[1][0:TN, 0:CH], ACT.Copy, scale=DSC[:, 0:1])),
           dma(lambda i: (at(HPD[0], i), y_)))
    weighted(flat(HPD[0]))

    def summed(k):
        return [dma(lambda i: (AC[:], at(ACCD, i)), lambda i: (x_, at(HPD[k], i)), lambda i: (DSC[:], at(DISD, i))),
                dve(lambda e, i: e.tensor_tensor(z_, AC[:, 0:CH], x_, op=ALU.add)),
                dve(lambda e, i: e.scalar_tensor_tensor(y_, z_, DSC[:, 0:1], BB[k][:], op0=ALU.mult, op1=ALU.add))]

    S.loop(NT, *summed(0), dve(lambda e, i: e.scalar_tensor_tensor(z_, y_, 0.01, y_, op0=ALU.mult, op1=ALU.max)), *project(z_, W["2"]),
           act(lambda e, i: e.activation(y_, PS[1][0:TN, 0:CH], ACT.Copy, scale=DSC[:, 0:1])),
           dma(lambda i: (at(HPD[1], i), y_)))
    weighted(flat(HPD[1]))
    S.loop(NT, *summed(1), dma(lambda i: (x_, at(xv, i))),
           dve(lambda e, i: e.scalar_tensor_tensor(z_, y_, 1.0, x_, op0=ALU.mult, op1=ALU.add, accum_out=SM[:, 0:1])),
           *normed(z_, x_), dma(lambda i: (at(X1, i), x_)), *sides(0, x_))

    def layer(l):
        H = HS[l]
        C = CH // H
        hv = lambda v: v.rearrange("p (h c) -> p h c", h=H)
        gr, gx, gw = GR[:, 0:CH], GX[:], GW_[:]
        S.loop(NR, *targets, gather(gr, flat(XLD[l]), SDI[:, 0:1]), gather(gx, XRD[l], DI[:, 0:1]), *logits(l, gr, gx, 128, gw, LE[:]),
               pe(lambda e, i: e.matmul(PS[0][0:H, 0:128], LE[:, 0:H], IDN, start=True, stop=True, is_transpose=True)),
               act(lambda e, i: e.activation(LER[0:H, :], PS[0][0:H, 0:128], ACT.Copy)),
               dma(lambda i: (at(LGE[l], i), LE[:, 0:H]), lambda i: (at(LGR[l], i), LER[0:H, :])))
        S.once(dve(lambda e, i: e.memset(MXA[:], -BIG)))
        lb = LB[:, 0:CK * H * 128].rearrange("p (r h e) -> p r h e", r=CK, h=H)
        tmp = TMP[:, 0:CK * H * 128].rearrange("p (r h e) -> p r h e", r=CK, h=H)
        mk = MK[:].rearrange("p (r o e) -> p r o e", r=CK, o=1).broadcast_to([TN, CK, H, 128])
        largest = []
        for t in range(NT):
            largest += [dve(lambda e, i, t=t: e.tensor_scalar(MK[:], DBF[:], NID[:, t:t + 1], -BIG, op0=ALU.not_equal, op1=ALU.mult)),
                        dve(lambda e, i: e.tensor_tensor(tmp, lb, mk, op=ALU.add)),
                        dve(lambda e, i: e.tensor_reduce(MXT[:, 0:H], tmp.rearrange("p r h e -> p h r e"), axis=AX.XY, op=ALU.max)),
                        dve(lambda e, i, t=t: e.tensor_tensor(MXA[:, t, 0:H], MXA[:, t, 0:H], MXT[:, 0:H], op=ALU.max))]
        S.loop(NR // CK,
               dma(lambda i: (DBI[:], A["dr"][bass.ds(i, 1), :].broadcast_to([TN, CK * 128])),
                   lambda i: (LB[:, 0:CK * H * 128], LGR[l].rearrange("(n r) h e -> n (r h e)", r=CK)[bass.ds(i, 1), :].broadcast_to([TN, CK * H * 128]))),
               dve(lambda e, i: e.tensor_copy(DBF[:], DBI[:])), *largest)
        S.once(dma(lambda i: (LSA[:], LSD[l].rearrange("t p h -> p t h"))),
               dve(lambda e, i: e.tensor_tensor(MXA[:], MXA[:], LSA[:], op=ALU.max)),
               dma(lambda i: (MXD[l][0:N].rearrange("(t p) h -> p t h", p=TN), MXA[:])),
               clear)
        S.loop(NR, *targets, onehot, gather(gr, flat(XLD[l]), SDI[:, 0:1]), gather(MXG[:], MXD[l], DI[:, 0:1]), dma(lambda i: (LE[:, 0:H], at(LGE[l], i))),
               dve(lambda e, i: e.tensor_tensor(LX[:, 0:H], LE[:, 0:H], MXG[:, 0:H], op=ALU.subtract)),
               act(lambda e, i: e.activation(GR[:, CH:CH + H], LX[:, 0:H], ACT.Exp)),
               dve(lambda e, i: e.tensor_tensor(hv(gr), hv(gr), GR[:, CH:CH + H].unsqueeze(2).broadcast_to([128, H, C]), op=ALU.mult)),
               *aggregate(CH + H))
        S.once(keep)
        wide = lambda v: v.unsqueeze(2).broadcast_to([TN, H, C])
        out = [dma(lambda i: (AC[:], at(ACCD, i)), lambda i: (x_, at(XLD[l], i)), lambda i: (LST[:], at(LSD[l], i)),
                   lambda i: (MXT[:], at(MXD[l][0:N].rearrange("(t p) h -> t p h", p=TN), i))),
               dve(lambda e, i: e.tensor_tensor(SM[:, 0:H], LST[:, 0:H], MXT[:, 0:H], op=ALU.subtract)),
               act(lambda e, i: e.activation(SM[:, 4:4 + H], SM[:, 0:H], ACT.Exp)),
               dve(lambda e, i: e.tensor_tensor(SM[:, 0:H], SM[:, 4:4 + H], AC[:, CH:CH + H], op=ALU.add)),
               dve(lambda e, i: e.tensor_tensor(hv(y_), hv(x_), wide(SM[:, 4:4 + H]), op=ALU.mult)),
               dve(lambda e, i: e.reciprocal(LST[:, 0:H], SM[:, 0:H])),
               dve(lambda e, i: e.tensor_tensor(z_, y_, AC[:, 0:CH], op=ALU.add)),
               dve(lambda e, i: e.tensor_tensor(hv(y_), hv(z_), wide(LST[:, 0:H]), op=ALU.mult)),
               dve(lambda e, i: e.tensor_tensor(z_, y_, BB[2 + l][:], op=ALU.add))]
        if l == 0:
            out += [dve(lambda e, i: e.tensor_scalar(y_, z_, 0.0, None, op0=ALU.min)),
                    act(lambda e, i: e.activation(t1_, y_, ACT.Exp)),
                    dve(lambda e, i: e.scalar_tensor_tensor(y_, z_, 0.0, t1_, op0=ALU.max, op1=ALU.add)),
                    dve(lambda e, i: e.tensor_scalar(z_, y_, -1.0, None, op0=ALU.add)), *sides(1, z_)]
        else:
            out += [dma(lambda i: (x_, at(X1, i))),
                    dve(lambda e, i: e.scalar_tensor_tensor(y_, z_, 1.0, x_, op0=ALU.mult, op1=ALU.add, accum_out=SM[:, 0:1])),
                    *normed(y_, x_), dma(lambda i: (at(ov, i), x_))]
        S.loop(NT, *out)

    for l in range(2):
        layer(l)
    return S


def layouts(src, dst, ew, NT, E):
    N = NT * TN
    nb = -(-E // BLK)
    nr = nb + KP * ROW // BLK
    length = (nr + ROW // BLK) * BLK
    cw = -(-E // 128)
    length = max(length, 128 * cw + 1)
    length = -(-length // BLK) * BLK

    def padded(a, value):
        out = np.full(length, value, a.dtype)
        out[:E] = a
        return out

    def fill(a, value):
        out = np.full(-(-E // 512) * 512, value, a.dtype)
        out[:E] = a
        return out.reshape(-1, 128)

    s, d, w = padded(src, 0), padded(dst, N + 875), padded(ew, 0)
    rows = lambda a: [a.reshape(-1, BLK)[m:m + nr] for m in range(ROW // BLK)]
    return {
        "sd": np.ascontiguousarray(np.concatenate(rows(s) + rows(d), axis=1)),
        "ew": np.ascontiguousarray(np.concatenate(rows(w), axis=1)),
        "first": np.ascontiguousarray(d.reshape(-1, BLK)[:nb, 0][None]),
        "sdr": np.stack([fill(src, 0), fill(dst, N + 875)], axis=2),
        "ewr": fill(ew, 0)[:, :, None],
        "dr": fill(dst, N + 875).reshape(-1, 4 * 128),
        "dsort": np.ascontiguousarray(np.concatenate([d[:128 * cw].reshape(128, cw), d[cw:128 * cw + 1:cw][:, None]], axis=1)),
    }


def build(nc, A, NT, E, where):
    ctx, Q, FLAG, general = gnn_program(nc, A, NT, E, where)

    def emit(name, e):
        Q.emit(name, e)
        needed = e.value_load(FLAG[0:1, 0:1], min_val=0, max_val=1)
        with e.If(needed == 1):
            general.emit(name, e)

    with ctx:
        with nc.Block() as block:
            block.sync(lambda e: emit("sync", e))
            block.tensor(lambda e: emit("tensor", e))
            block.vector(lambda e: emit("vector", e))
            block.scalar(lambda e: emit("scalar", e))
            block.gpsimd(lambda e: emit("gpsimd", e))


def kernel(**inputs):
    import concourse.bacc as _bacc
    from concourse.bass_utils import run_bass_kernel_spmd as _run

    a = {k: np.asarray(v) for k, v in inputs.items()}
    NT, E = a["x"].shape[0] // TN, a["src"].shape[0]
    arrays = layouts(a["src"], a["dst"], a["edge_weight"], NT, E)
    arrays["x"] = a["x"]
    arrays["W1"], arrays["W2"] = a["L0_gnn_W1"], a["L0_gnn_W2"]
    for l in (1, 2):
        arrays[f"Wl{l}"], arrays[f"Wr{l}"] = a[f"L1_gnn_Wl{l}"], a[f"L1_gnn_Wr{l}"]
        arrays[f"att{l}"] = a[f"L1_gnn_att{l}"].reshape(1, CH)
        arrays[f"att{l}c"] = a[f"L1_gnn_att{l}"].reshape(2, 128).T
    for i, n in enumerate(("L0_gnn_b1", "L0_gnn_b2", "L1_gnn_b1", "L1_gnn_b2")):
        arrays[f"b{i + 1}"] = a[n].reshape(1, CH)
    arrays["const"], where = shape_constants(NT)
    arrays = {f"in_{k}": np.ascontiguousarray(v) for k, v in arrays.items()}

    nc = _bacc.Bacc("TRN2", target_bir_lowering=False, num_devices=1)
    A = {k[3:]: nc.dram_tensor(k, v.shape, mybir.dt.from_np(v.dtype), kind="ExternalInput").ap() for k, v in arrays.items()}
    A["out"] = nc.dram_tensor("out", (NT * TN, CH), F32, kind="ExternalOutput").ap()
    build(nc, A, NT, E, where)
    r = _run(nc, [arrays], core_ids=[0])
    return r.results[0]["out"]
```

```python
from contextlib import ExitStack

import numpy as np

import concourse.bass as bass
from concourse import mybir
from concourse.alu_op_type import AluOpType as ALU

ACT = mybir.ActivationFunctionType
AX = mybir.AxisListType
F32 = mybir.dt.float32
F32R = mybir.dt.float32r
BF16 = mybir.dt.bfloat16
I32 = mybir.dt.int32

TN = 125
CH = 256
GR = 5
GPT = TN // GR
BLK = 32
ROW = 256
KP = 17
BIG = 2.0 ** 100
MAGIC = 12582912.0
EPS = 1.0e-5
LG = 2
NRING = 4
RP = 2 * KP
BL = 32
WIN = 62
WINS = (0, 31, 63)
CHUNKS = ((0, 4), (4, 8), (8, 12), (12, KP))
LAGC = 24


class Counter:

    def __init__(self, handle):
        self.handle, self.value = handle, 0

    def raised(self, by):
        self.value += by
        return (self, self.value)


class Queues:

    def __init__(self, sem):
        self.lists = {n: [] for n in ("sync", "tensor", "vector", "scalar", "gpsimd")}
        self.done = {n: Counter(sem(f"{n}_done")) for n in ("tensor", "vector", "scalar", "gpsimd")}

    def put(self, engine, fn, after=(), counter=None, by=1):
        token = counter.raised(by) if counter else None
        self.lists[engine].append((fn, [a for a in after if a], counter, by))
        return token

    def pe(self, fn, after=(), last=False):
        return self.put("tensor", fn, after, self.done["tensor"] if last else None)

    def dve(self, fn, after=()):
        return self.put("vector", fn, after, self.done["vector"])

    def act(self, fn, after=()):
        return self.put("scalar", fn, after, self.done["scalar"])

    def pool(self, fn, after=()):
        return self.put("gpsimd", fn, after, self.done["gpsimd"])

    def dma(self, counter, out, in_, after=(), engine="sync"):
        return self.put(engine, lambda e: e.dma_start(out, in_), after, counter, 16)

    def emit(self, engine, e):
        seen = {}
        for fn, after, counter, by in self.lists[engine]:
            for c, value in after:
                if seen.get(c, 0) < value:
                    e.wait_ge(c.handle, value)
                    seen[c] = value
            i = fn(e) if fn else None
            if counter:
                i.then_inc(counter.handle, by)


def place_in_tile(i):
    return 4 * (i % 4) + i // 4 if i < KP - 1 else i


def position(i, h):
    return BL * (i % 4) + 5 * h + i // 4


def reach(E, N):
    degree = max(E / N, 1.0)
    windows, blocks, allowed = [], [], []
    for i in range(KP):
        k = place_in_tile(i)
        spans = []
        for half in range(2):
            e0 = ROW * k + ROW // 2 * half
            lo, hi = (e0 - 2 * BLK) / degree, (e0 + ROW // 2) / degree
            slack = lambda n: 1.0 + 5.0 * np.sqrt(max(min(n, TN), 0.0) / degree)
            lo, hi = lo - slack(lo), hi + slack(hi)
            spans.append((min(max(lo, 0.0), TN - 1.0), min(max(hi, 0.0), TN - 1.0)))
        lo, hi = spans[0][0], spans[1][1]
        w = min(WINS, key=lambda w: max(w - lo, hi - (w + WIN - 1)))
        windows.append(w)
        for lo, hi in spans:
            b0, b1 = int(lo) // BL, int(hi) // BL
            blocks.append((b0, b1))
            allowed.append((max(b0 * BL, w), min((b1 + 1) * BL, w + WIN, TN)))
    return windows, blocks, allowed


def shape_constants(NT, E):
    NJ = NT // 5
    p = np.arange(128, dtype=np.float32)[:, None]
    R = 5 * KP
    rows = np.array([place_in_tile(m % KP) for m in range(128)], np.float32)[:, None]
    number = {place_in_tile(i): i for i in range(KP)}
    windows, blocks, allowed = reach(E, NT * TN)
    parts = {}
    parts["iota"] = np.broadcast_to(np.arange(128, dtype=np.float32), (128, 128))
    parts["ident"] = np.eye(128, dtype=np.float32)
    parts["pidx"] = p
    parts["pwin"] = p % WIN
    parts["v5"] = GR * (np.arange(NJ, dtype=np.float32)[None] * TN + p)
    parts["v125"] = TN * (np.arange(NJ, dtype=np.float32)[None] * 5 + np.floor(p / KP))
    parts["k8"] = (ROW // BLK) * rows
    parts["win"] = np.array([windows[m % KP] for m in range(128)], np.float32)[:, None]
    parts["allow"] = np.array([allowed[2 * (m % KP)] + allowed[2 * (m % KP) + 1] for m in range(128)], np.float32)
    sel = np.zeros((128, R), np.float32)
    for m in range(R):
        sel[GPT * (m // KP), m] = 1
    parts["sel85"] = sel
    sh, order = np.zeros((128, R), np.float32), np.zeros((128, R), np.float32)
    for m in range(R):
        k = place_in_tile(m % KP)
        order[m, m - m % KP + k] = 1
        if k != KP - 1:
            sh[m - m % KP + number[k + 1], m] = 1
    parts["sh85"], parts["order"] = sh, order
    parts["k16"] = -(rows == KP - 1).astype(np.float32)
    s2, hm = np.zeros((128, 2 * KP), np.float32), np.zeros((128, 4), np.float32)
    for i in range(KP):
        for h in range(4):
            s2[position(i, h), place_in_tile(i)] = s2[position(i, h), KP + place_in_tile(i)] = 1
            hm[position(i, h), h] = 1
    parts["sel2"], parts["hm"] = s2, hm
    hmt = np.zeros((128, 128), np.float32)
    hmt[:4, :] = hm.T
    parts["hmt"] = hmt
    mb = np.zeros((128, 2), np.float32)
    mb[:64, 0] = mb[64:, 1] = 1
    parts["mb"] = mb
    parts["ones"] = np.ones((128, 1), np.float32)
    at, where = 0, {}
    for k, v in parts.items():
        where[k] = (at, at + v.shape[1])
        at += v.shape[1]
    return np.ascontiguousarray(np.concatenate(list(parts.values()), axis=1).astype(np.float32)), where


def gnn_program(nc, A, NT, E, where):
    NJ = NT // 5
    N = NT * TN
    R = 5 * KP
    NROW = NT * KP
    NB = A["first"].shape[1]
    CW = A["dsort"].shape[1] - 1
    NP = NT * KP
    SC = NT * TN

    ctx = ExitStack()
    sb = lambda name, shape, dt=F32: ctx.enter_context(nc.sbuf_tensor(name, shape, dt))
    sem = lambda name: ctx.enter_context(nc.semaphore(name))
    dram = lambda name, shape, dt=F32: nc.dram_tensor(name, shape, dt, kind="Internal").ap()
    Q = Queues(sem)
    cnt = lambda name: Counter(sem(name))

    DEGD = dram("deg_d", (N,))
    AD = dram("a_d", (NT, TN, SC))
    X1D = dram("x1_d", (N, CH))
    TAB = [dram("tab1_d", (N, CH + 4)), dram("tab2_d", (N, CH + 1))]
    XRD = [dram(f"xr{l}_d", (NT, TN, 2 * CH)) for l in range(2)]
    CSD = dram("cs_d", (NJ, R, 2))
    M3D = dram("m3_d", (NROW + 3, 772), BF16)
    DLBD = dram("dlb_d", (NROW, ROW), BF16)

    PS = [ctx.enter_context(nc.psum_tensor(f"bank{i}", [128, 512], F32)) for i in range(8)]

    CON = sb("con", [128, A["const"].shape[1]])
    K = lambda name, p=128: CON[0:p, where[name][0]:where[name][1]]
    IOTA = K("iota")[:, 0:TN + 1]
    IDN = K("ident")
    W2S = sb("w2s", [128, 2, CH])
    HS = [4, 1]
    WL = [sb(f"wl{l}", [128, 2, CH + HS[l]]) for l in range(2)]
    WR = [sb(f"wr{l}", [128, 2, CH + HS[l]]) for l in range(2)]
    BB = [sb(f"bb{i}", [TN, CH]) for i in range(4)]
    ATB = [sb(f"atb{l}", [128, CH]) for l in range(2)]
    ATC = [sb(f"atc{l}", [128, 2]) for l in range(2)]
    AZ = [sb(f"az{l}", [128, 2, 4 + BL]) for l in range(2)]
    ARN = [sb(f"arn{l}", [TN, NT, HS[l]]) for l in range(2)]
    LSF = [sb(f"lsf{l}", [TN, NT, HS[l]]) for l in range(2)]
    SRCI = sb("srci", [128, NJ, 2, R], I32)
    DLS = sb("dls", [128, NJ, 2, R])
    LAST = sb("last", [128, NJ, 2, R])
    CRF = sb("crf", [4, 1 + NROW])
    AFW = sb("afw", [4, NROW])
    ARV = sb("arv", [4, NROW])
    DIS = sb("dis", [TN, NT])
    FLAG = sb("flag", [1, 4], I32)

    d_con = cnt("d_con")
    t_con = Q.dma(d_con, CON[:], A["const"])

    def loaded(counter, out, in_, after=(), engine="sync"):
        return Q.dma(counter, out, in_, after, engine)

    gcn = ExitStack()
    sg = lambda name, shape, dt=F32: gcn.enter_context(nc.sbuf_tensor(name, shape, dt))
    HP = [sg(f"hp{i}", [TN, NT, CH]) for i in range(2)]
    RING = sg("ring", [128, NRING, SC])
    FLD = sg("fld", [128, NJ, 2, 3, TN])
    early = HP[1][:].rearrange("p t c -> p (t c)")
    GSD = early[:, 0:2 * ROW * NJ].bitcast(I32).rearrange("p (j c) -> p j c", j=NJ)
    GEW = early[:, 2 * ROW * NJ:3 * ROW * NJ].rearrange("p (j c) -> p j c", j=NJ)
    TSD = early[0:R, 3 * ROW * NJ:5 * ROW * NJ].bitcast(I32).rearrange("p (j c) -> p j c", j=NJ)
    XST = [sg(f"xst{i}", [TN, CH]) for i in range(3)]
    OHW = 12
    OHS = sg("ohs", [128, OHW, 2, TN + 1])
    W1S = sg("w1s", [128, 2, CH])
    CNT = sg("cnt", [TN, NJ])
    CNB = sg("cnb", [TN, NJ])
    STF = sg("stf", [TN, NJ])
    STI = sg("sti", [TN, NJ], I32)
    IXF = sg("ixf", [R, NJ])
    IXI = sg("ixi", [R, NJ], I32)
    GF = [sg(f"gf{i}", [TN, ROW]) for i in range(6)]
    KS = [[sg(f"ks{i}_{j}", [TN, ROW]) for i in range(3)] for j in range(2)]
    DEG = sg("deg", [TN, NJ, GR])
    VAL = sg("val", [TN, NJ])
    DGR = sg("dgr", [NT, TN])
    DG = [sg(f"dg{i}", [TN, NT]) for i in range(3)]
    HT = [sg(f"ht{i}", [128, 2, TN]) for i in range(2)]
    ZB = [sg(f"zb{i}", [TN, CH]) for i in range(4)]
    XL = [sg(f"xl{i}", [TN, CH + 4]) for i in range(2)]
    SMALL = [sg(f"small{i}", [TN, 16]) for i in range(2)]
    XRS = [sg(f"xrs{i}", [TN, 2 * CH]) for i in range(2)]
    PF = [XRS[i // 2][0:R, (i % 2) * CH:(i % 2 + 1) * CH] for i in range(4)] + [sg(f"pf{i}", [R, ROW]) for i in range(4, 7)]
    PB = sg("pb", [R, ROW], BF16)
    PM = sg("pm", [R, 772], BF16)
    LF = sg("lf", [R, NJ, ROW])
    FL = [sg(f"fl{i}", [R, NJ]) for i in range(5)]
    CS = sg("cs", [R, NJ, 2])
    CSB = sg("csb", [4, NROW, 2])
    VALT = sg("valt", [R, 2 * NJ])
    CSP = sg("csp", [R, NJ, 2])
    STAT = sg("stat", [128, 4])
    SUMS = sg("sums", [1, 8])
    DSI = RING[:, 1, SC - CW - 1:SC].bitcast(I32)
    ATW = [sg("atw0", [128, 2, CH])]
    ATR = sg("atr", [128, 2, 4])

    ring_flat = RING[:].rearrange("p r c -> p (r c)")
    FIRST = HP[1][:].rearrange("p t c -> p (t c)")[:, 0:NB]
    FIRSTI = ring_flat[0:TN, 0:NB].bitcast(I32)
    d_sort = cnt("d_sort")
    d_first, d_w1, d_w2, d_b, d_wl, d_at = (cnt(n) for n in ("d_first", "d_w1", "d_w2", "d_b", "d_wl", "d_at"))
    t_first = loaded(d_first, FIRSTI, A["first"][0:1, :].broadcast_to([TN, NB]), engine="scalar")
    t_w1 = loaded(d_w1, W1S[:], A["W1"].rearrange("(k p) n -> p k n", p=128), engine="scalar")
    t_dsi = loaded(d_sort, DSI, A["dsort"], engine="scalar")
    d_x = [cnt(f"d_x{i}") for i in range(3)]
    xTv = ring_flat[:, (NRING - 2) * SC:(NRING - 2) * SC + 2 * N].rearrange("p (k n) -> p k n", k=2)

    t_cvt = Q.dve(lambda e: e.tensor_copy(FIRST, FIRSTI), [t_first])
    junk = OHS[:].rearrange("p a b c -> p (a b c)").bitcast(BF16)
    junk_act = FLD[:].rearrange("p j h f n -> p (j h f n)").bitcast(BF16)
    t_cnt, t_sti = None, []
    t_nv = Q.dve(lambda e: e.tensor_scalar(CNB[:], K("v5", TN), -1.0, 0.5, op0=ALU.mult, op1=ALU.add), [t_con])
    for j in range(NJ):
        if j % 2 == 0:
            t_cnt = Q.dve(lambda e, j=j: e.tensor_scalar(junk[0:TN, 0:NB], FIRST, K("v5", TN)[:, j:j + 1], None, op0=ALU.is_lt, op1=ALU.add, accum_out=CNT[:, j:j + 1]), [t_cvt, t_con, t_cnt])
            t_stf = Q.dve(lambda e, j=j: e.tensor_scalar(STF[:, j:j + 1], CNT[:, j:j + 1], -1.0, 0.0, op0=ALU.add, op1=ALU.max), [t_cnt])
            t_sti.append(Q.dve(lambda e, j=j: e.tensor_copy(STI[:, j:j + 1], STF[:, j:j + 1]), [t_stf]))
        else:
            t_cnta = Q.act(lambda e, j=j: e.activation(junk_act[0:TN, 0:NB], FIRST, ACT.Sign, bias=CNB[:, j:j + 1], accum_out=CNT[:, j:j + 1]), [t_cvt, t_nv] + ([t_cnta] if j > 1 else []))
            t_sti.append(None)
    for j in range(1, NJ, 2):
        t_1 = Q.dve(lambda e, j=j: e.tensor_scalar(STF[:, j:j + 1], CNT[:, j:j + 1], -0.5, NB / 2 - 1.0, op0=ALU.mult, op1=ALU.add), [t_cnta])
        t_stf = Q.dve(lambda e, j=j: e.tensor_scalar(STF[:, j:j + 1], STF[:, j:j + 1], 0.0, None, op0=ALU.max), [t_1])
        t_sti[j] = Q.dve(lambda e, j=j: e.tensor_copy(STI[:, j:j + 1], STF[:, j:j + 1]), [t_stf])
    if NJ == 1:
        t_cnta = t_cvt
    t_stat = Q.dve(lambda e: e.memset(STAT[:], 0.0))
    t_uns = Q.dve(lambda e: e.scalar_tensor_tensor(junk[:, 0:CW], DSI[:, 0:CW], 0.0, DSI[:, 1:CW + 1], op0=ALU.add, op1=ALU.is_gt, accum_out=STAT[:, 2:3]), [t_dsi, t_stat, t_cnt])

    off = lambda ap: bass.IndirectOffsetOnAxis(ap=ap, axis=0)
    d_gsd, d_gew, d_tsd = ([cnt(f"{n}{j}") for j in range(NJ)] for n in ("d_gsd", "d_gew", "d_tsd"))
    t_gsd = []
    for j in range(NJ):
        t_1 = Q.put("gpsimd", lambda e, j=j: e.indirect_dma_start(out=GSD[:, j, :], out_offset=None, in_=A["sd"], in_offset=off(STI[:, j:j + 1])), [t_sti[j], t_cvt, t_cnt, t_cnta], d_gsd[j], 16)
        t_2 = Q.put("gpsimd", lambda e, j=j: e.indirect_dma_start(out=GEW[:, j, :], out_offset=None, in_=A["ew"], in_offset=off(STI[:, j:j + 1])), [], d_gew[j], 16)
        t_gsd.append([t_1, t_2])
    t_xload, t_xt_read = [None] * 3, [None] * 3
    t_xw = []
    t_ptfree = [None, None]
    t_xtw = []
    for t in range(NT):
        b = t % 3
        tl = loaded(d_x[b], XST[b][:], A["x"][t * TN:(t + 1) * TN, :], [t_xt_read[b]])
        bank = PS[5 + t % 2]
        Q.pe(lambda e, b=b, bank=bank: e.matmul(bank[:, 0:TN], XST[b][:, 0:128], IDN[0:TN, 0:TN], start=True, stop=True, is_transpose=True), [tl, t_con, t_ptfree[t % 2]])
        tt = Q.pe(lambda e, b=b, bank=bank: e.matmul(bank[:, TN:2 * TN], XST[b][:, 128:256], IDN[0:TN, 0:TN], start=True, stop=True, is_transpose=True), last=True)
        t_xt_read[b] = tt
        te = Q.act(lambda e, t=t, bank=bank: e.activation(xTv[:, :, t * TN:(t + 1) * TN], bank[:, 0:2 * TN].rearrange("p (k n) -> p k n", k=2), ACT.Copy), [tt])
        t_ptfree[t % 2] = te
        t_xtw.append(te)
    t_hpfree = [None] * 2
    t_hp = [[None] * NT for _ in range(2)]
    t_raw = []
    for t in range(NT):
        bank = PS[3 + t % 2]
        Q.pe(lambda e, t=t, bank=bank: e.matmul(bank[0:TN, 0:CH], xTv[:, 0, t * TN:(t + 1) * TN], W1S[:, 0, :], start=True, stop=False), [t_xtw[t], t_w1, t_hpfree[t % 2]])
        tm = Q.pe(lambda e, t=t, bank=bank: e.matmul(bank[0:TN, 0:CH], xTv[:, 1, t * TN:(t + 1) * TN], W1S[:, 1, :], start=False, stop=True), last=True)
        te = Q.act(lambda e, t=t, bank=bank: e.activation(HP[0][:, t, :], bank[0:TN, 0:CH], ACT.Copy), [tm])
        t_hpfree[t % 2] = te
        t_raw.append(te)
    t_xt_done = t_raw[-1]

    t_ixp = Q.pe(lambda e: e.matmul(PS[7][0:R, 0:NJ], K("sel85", TN), STF[:], start=True, stop=True), [t_stf, t_con], last=True)
    t_ixf = Q.dve(lambda e: e.tensor_scalar(IXF[:], PS[7][0:R, 0:NJ], K("k8", R), None, op0=ALU.add), [t_ixp])
    t_tsd = []
    t_ixi = Q.dve(lambda e: e.tensor_copy(IXI[:], IXF[:]), [t_ixf])

    for j in range(NJ):
        t_tsd.append(Q.put("gpsimd", lambda e, j=j: e.indirect_dma_start(out=TSD[:, j, :], out_offset=None, in_=A["sd"], in_offset=off(IXI[:, j:j + 1])), [t_ixi], d_tsd[j], 16))

    t_b = None
    for i, n in enumerate(("b1", "b2", "b3", "b4")):
        t_b = loaded(d_b, BB[i][:], A[n].broadcast_to([TN, CH]))
    t_w2 = loaded(d_w2, W2S[:], A["W2"].rearrange("(k p) n -> p k n", p=128))
    for l in range(2):
        loaded(d_wl, WL[l][:, :, 0:CH], A[f"Wl{l + 1}"].rearrange("(k p) n -> p k n", p=128))
        t_wl = loaded(d_wl, WR[l][:, :, 0:CH], A[f"Wr{l + 1}"].rearrange("(k p) n -> p k n", p=128))
        loaded(d_at, ATB[l][:], A[f"att{l + 1}"].broadcast_to([128, CH]))
        t_at = loaded(d_at, ATC[l][:], A[f"att{l + 1}c"])

    t_fld = [None] * NJ
    t_deg = [None] * NJ
    t_ksfree = [None, None]

    def fields(j):
        src, dst, ew = GSD[:, j, 0:ROW], GSD[:, j, ROW:2 * ROW], GEW[:, j, :]
        slo, key, eww = KS[j % 2]
        drel, blk, ge, tmp, one, blk2 = (g[:] for g in GF)
        prev = [t_fields[-1]] if t_fields else []
        t1 = Q.dve(lambda e: e.tensor_scalar(drel, dst, K("v5", TN)[:, j:j + 1], None, op0=ALU.subtract), t_gsd[j] + [t_con] + prev)
        t2 = Q.dve(lambda e: e.tensor_scalar(blk, src, 1.0 / TN, 0.5 / TN - 0.5, op0=ALU.mult, op1=ALU.add), prev)
        t4 = Q.dve(lambda e: e.tensor_scalar(ge, drel, 0.0, None, op0=ALU.is_ge), [t1])
        t2b = Q.dve(lambda e: e.tensor_scalar(tmp, blk, MAGIC, None, op0=ALU.add), [t2])
        t5 = Q.dve(lambda e: e.scalar_tensor_tensor(one, drel, float(GR), ge, op0=ALU.is_lt, op1=ALU.mult, accum_out=VAL[:, j:j + 1]), [t4])
        t3 = Q.dve(lambda e: e.tensor_scalar(blk2, tmp, MAGIC, None, op0=ALU.subtract), [t2b])
        t6 = Q.dve(lambda e: e.tensor_tensor(eww[:], one, ew, op=ALU.mult), [t5, t_ksfree[j % 2]])
        t7 = Q.dve(lambda e: e.scalar_tensor_tensor(slo[:], blk2, -float(TN), src, op0=ALU.mult, op1=ALU.add), [t3])
        t8 = Q.dve(lambda e: e.scalar_tensor_tensor(key[:], blk2, float(GR), drel, op0=ALU.mult, op1=ALU.add), [t3])
        t_fields.append(t8)
        return t6, t7, t8

    t_fields = []

    def degrees(j, t6):
        eww, drel = KS[j % 2][2], GF[0]
        for r in range(GR):
            t_deg[j] = Q.dve(lambda e, r=r: e.scalar_tensor_tensor(GF[2][:] if r % 2 else GF[3][:], drel[:], float(r), eww[:], op0=ALU.is_equal, op1=ALU.mult, accum_out=DEG[:, j, r:r + 1]), [t6, t_deg[j]])
        t_fields.append(t_deg[j])

    def field_transposes(j, t8):
        for half in range(2):
            for f in range(3):
                tp = Q.pe(lambda e, f=f, half=half: e.matmul(PS[7][:, f * TN:(f + 1) * TN], KS[j % 2][f][:, half * 128:(half + 1) * 128], IDN[0:TN, 0:TN], start=True, stop=True, is_transpose=True), [t8, t_ixf, t_fldfree[0]], last=(f == 2))
            order = (0, 1, 2)
            t_fldfree[0] = Q.act(lambda e, half=half: e.activation(FLD[:, j, half, :, :], PS[7][:, 0:3 * TN].rearrange("p (f n) -> p f n", f=3), ACT.Copy), [tp])
        t_fld[j] = t_fldfree[0]
        t_ksfree[j % 2] = tp

    t_fldfree = [None]

    ROWS_AT = [LG + 2 * jj for jj in range(NJ)]
    build_banks = (0, 1, 2)
    t_bank = [None] * 3
    t_oh = [None] * OHW
    ring_free = [[] for _ in range(NRING)]
    t_at_tile = [None] * NT
    quart = [(q * 4, min(4, GPT - q * 4)) for q in range((GPT + 3) // 4)]
    slot_no = [0]
    bank_no = [0]
    d_ad = [cnt(f"d_ad{i}") for i in range(NRING)]

    def build_quartet(t, q):
        g0, ng = quart[q]
        bk = bank_no[0] % 3
        bank_no[0] += 1
        bank = PS[build_banks[bk]]
        for gi in range(ng):
            g = t * GPT + g0 + gi
            j, p = g // TN, g % TN
            for half in range(2):
                o = slot_no[0] % OHW
                slot_no[0] += 1
                put = Q.pool if half and (t not in ROWS_AT or q < 3) else Q.dve
                t1 = put(lambda e, j=j, p=p, half=half, o=o: e.tensor_scalar(OHS[:, o, 0, :], IOTA, FLD[:, j, half, 0, p:p + 1], None, op0=ALU.is_equal), [t_fld[j], t_oh[o], t_uns])
                t2 = Q.dve(lambda e, j=j, p=p, half=half, o=o: e.tensor_scalar(OHS[:, o, 1, :], IOTA, FLD[:, j, half, 1, p:p + 1], FLD[:, j, half, 2, p:p + 1], op0=ALU.is_equal, op1=ALU.mult), [t_fld[j], t_oh[o], t_uns])
                tm = Q.pe(lambda e, gi=gi, half=half, o=o, bank=bank: e.matmul(bank[0:TN, gi * TN:(gi + 1) * TN], OHS[:, o, 0, 0:TN], OHS[:, o, 1, 0:TN], start=(half == 0), stop=(half == 1)), [t1, t2, t_bank[bk]], last=True)
                t_oh[o] = tm
        r = t % NRING
        dst = RING[0:TN, r, :].rearrange("p (s g d) -> p g s d", s=NT, g=GPT)[:, g0:g0 + ng, :, :]
        src = bank[0:TN, 0:ng * TN].rearrange("p (g c) -> p g c", g=ng)[:, :, 0:NT * GR].rearrange("p g (s d) -> p g s d", d=GR)
        alias = [[t_cvt], [t_uns], [t_xt_done], [t_xt_done]][r]
        t_at_tile[t] = Q.act(lambda e: e.activation(dst, src, ACT.Copy), [tm] + ring_free[r] + alias)
        t_bank[bk] = t_at_tile[t]

    t_acc = [None, None]

    def apply_part(t, s0, s1, layer, acc, first_after):
        bank = PS[3 + acc]
        tm = None
        for s in range(s0, s1):
            tm = Q.pe(lambda e, s=s: e.matmul(bank[0:TN, 0:CH], RING[0:TN, t % NRING, s * TN:(s + 1) * TN], HP[layer][:, s, :], start=(s == 0), stop=(s == NT - 1)), [t_hp[layer][s]] + first_after, last=(s == NT - 1))
        return tm

    t_z = [None] * 4
    t_ht = [None, None]
    t_pt = [None]
    t_pm = [None]

    def post1_vec(t, tm, acc):
        z, h = ZB[0], ZB[1]
        t1 = Q.dve(lambda e: e.tensor_tensor(z[:], PS[3 + acc][0:TN, 0:CH], HP[0][:, t, :], op=ALU.add), [tm, t_z[0]])
        t_acc[acc] = t1
        t2 = Q.dve(lambda e: e.scalar_tensor_tensor(z[:], z[:], DIS[:, t:t + 1], BB[0][:], op0=ALU.mult, op1=ALU.add), [t1, t_b])
        t3 = Q.dve(lambda e: e.scalar_tensor_tensor(h[:], z[:], 0.01, z[:], op0=ALU.mult, op1=ALU.max), [t2, t_z[1]])
        t_z[0] = t3
        return t3

    def transposes(src, t_src, k):
        for c in range(2):
            tp = Q.pe(lambda e, c=c: e.matmul(PS[5][:, c * TN:(c + 1) * TN], src[:, c * 128:(c + 1) * 128], IDN[0:TN, 0:TN], start=True, stop=True, is_transpose=True), [t_src, t_pt[0]], last=(c == 1))
        te = Q.act(lambda e: e.activation(HT[k][:], PS[5][:, 0:2 * TN].rearrange("p (k n) -> p k n", k=2), ACT.Copy), [tp, t_ht[k]])
        t_pt[0] = te
        return tp, te

    def post1_mm(t, te, k):
        for c in range(2):
            tm = Q.pe(lambda e, c=c: e.matmul(PS[6][0:TN, 0:CH], HT[k][:, c, :], W2S[:, c, :], start=(c == 0), stop=(c == 1)), [te, t_w2, t_pm[0]], last=(c == 1))
        t_ht[k] = tm
        tv = Q.act(lambda e: e.activation(HP[1][:, t, :], PS[6][0:TN, 0:CH], ACT.Copy, scale=DIS[:, t:t + 1]), [tm] + early_read)
        t_pm[0] = tv
        t_hp[1][t] = tv

    def dis_chain():
        d_deg = cnt("d_deg")
        tw = Q.dma(d_deg, DEGD.rearrange("(j p r) -> p j r", j=NJ, p=TN), DEG[:], list(t_deg))
        tr = Q.dma(d_deg, DGR[:], DEGD.rearrange("(t n) -> t n", t=NT), [tw])
        tp = Q.pe(lambda e: e.matmul(PS[7][0:TN, 0:NT], DGR[:], IDN[0:NT, 0:NT], start=True, stop=True, is_transpose=True), [tr, t_fldfree[0]], last=True)
        t1 = Q.dve(lambda e: e.tensor_scalar(DG[0][:], PS[7][0:TN, 0:NT], 1.0, None, op0=ALU.add), [tp])
        t_fldfree[0] = t1
        t2 = Q.dve(lambda e: e.tensor_scalar(DG[1][:], DG[0][:], 0.0, None, op0=ALU.is_gt), [t1])
        t3 = Q.dve(lambda e: e.tensor_tensor(DG[2][:], DG[0][:], DG[1][:], op=ALU.mult), [t2])
        t4 = Q.dve(lambda e: e.scalar_tensor_tensor(DG[0][:], DG[1][:], -1.0, DG[2][:], op0=ALU.mult, op1=ALU.add), [t3])
        t5 = Q.dve(lambda e: e.tensor_scalar(DG[2][:], DG[0][:], 1.0, None, op0=ALU.add), [t4])
        t6 = Q.act(lambda e: e.activation(DG[0][:], DG[2][:], ACT.Sqrt), [t5])
        t7 = Q.dve(lambda e: e.reciprocal(DG[2][:], DG[0][:]), [t6])
        t8 = Q.dve(lambda e: e.tensor_tensor(DIS[:], DG[2][:], DG[1][:], op=ALU.mult), [t7])
        for t in range(NT):
            t_hp[0][t] = Q.act(lambda e, t=t: e.activation(HP[0][:, t, :], HP[0][:, t, :], ACT.Copy, scale=DIS[:, t:t + 1]), [t8, t_raw[t]])

    early_read = []
    t_row = [None] * NJ
    d_rows = cnt("d_rows")
    t_pfree = [[], []]

    def rows_of_tiles(jj):
        src, dst = TSD[:, jj, 0:ROW], TSD[:, jj, ROW:2 * ROW]
        df, sf, dl, eq, p1, p2, ge = (x[:, :] for x in PF)
        a = t_pfree[0] + [t_pad]
        t1 = Q.pool(lambda e: e.tensor_copy(df, dst), [t_tsd[jj]] + a)
        t2 = Q.pool(lambda e: e.tensor_copy(sf, src), a)
        t3 = Q.pool(lambda e: e.tensor_scalar(dl, df, K("v125", R)[:, jj:jj + 1], None, op0=ALU.subtract), [t1, t_con])
        t4 = Q.pool(lambda e: e.tensor_tensor(ge[:, 0:ROW - 1], df[:, 1:ROW], df[:, 0:ROW - 1], op=ALU.subtract))
        t5 = Q.pool(lambda e: e.tensor_scalar(p1, df, df[:, 0:1], BIG, op0=ALU.is_equal, op1=ALU.mult))
        t6 = Q.pool(lambda e: e.tensor_scalar(p2, df, df[:, ROW - 1:ROW], BIG, op0=ALU.is_equal, op1=ALU.mult))
        t7 = Q.pool(lambda e: e.tensor_scalar(PB[:], dl, K("win", R), None, op0=ALU.subtract), [t3])
        t8 = Q.pool(lambda e: e.tensor_scalar(eq[:, 0:ROW - 1], ge[:, 0:ROW - 1], 0.0, BIG, op0=ALU.is_equal, op1=ALU.mult), [t4])
        t10 = Q.pool(lambda e: e.tensor_scalar(PM[:, ROW + 1:2 * ROW + 1], p1, BIG, None, op0=ALU.subtract), [t5])
        t11 = Q.pool(lambda e: e.tensor_scalar(PM[:, 2 * ROW + 1:3 * ROW + 1], p2, BIG, None, op0=ALU.subtract), [t6])
        t8b = Q.pool(lambda e: e.tensor_scalar(PM[:, 1:ROW], eq[:, 0:ROW - 1], BIG, None, op0=ALU.subtract), [t8])
        t9 = Q.pool(lambda e: e.tensor_scalar(LF[:, jj, 0:ROW - 1], eq[:, 0:ROW - 1], -1.0 / BIG, 1.0, op0=ALU.mult, op1=ALU.add))
        t12 = Q.pool(lambda e: e.tensor_copy(FL[0][:, jj:jj + 1], df[:, 0:1]))
        t13 = Q.pool(lambda e: e.tensor_copy(FL[1][:, jj:jj + 1], df[:, ROW - 1:ROW]))
        for half in range(2):
            t14 = Q.pool(lambda e, half=half: e.tensor_scalar(ge[:, half * 128:(half + 1) * 128], dl[:, half * 128:(half + 1) * 128], K("allow", R)[:, 2 * half:2 * half + 1], None, op0=ALU.is_ge), [t3])
        t_row[jj] = t14
        return df, sf, dl, ge, t14

    def columns_of_tiles(jj, df, sf, dl, ge, t14):
        for half in range(2):
            tv = Q.dve(lambda e, half=half: e.scalar_tensor_tensor(PX[0:R, half * 128:(half + 1) * 128], dl[:, half * 128:(half + 1) * 128], K("allow", R)[:, 2 * half + 1:2 * half + 2], ge[:, half * 128:(half + 1) * 128], op0=ALU.is_lt, op1=ALU.mult, accum_out=VALT[:, 2 * jj + half:2 * jj + half + 1]), [t14, t_fields[-1]] + t_pfree[1])
        td = Q.dma(d_rows, DLBD[jj * R:(jj + 1) * R, :], PB[:], [t14, t_pm0])
        td = Q.dma(d_rows, M3D[jj * R:(jj + 1) * R, :], PM[:], [t14])
        for half in range(2):
            for f, x in ((0, sf), (1, dl)):
                tp = Q.pe(lambda e, x=x, f=f, half=half: e.matmul(PS[7][:, (half * 2 + f) * R:(half * 2 + f + 1) * R], x[:, half * 128:(half + 1) * 128], IDN[0:R, 0:R], start=True, stop=True, is_transpose=True), [t14, t_fldfree[0]], last=(half == 1 and f == 1))
        v = PS[7][:, 0:4 * R].rearrange("p (h f n) -> p h f n", h=2, f=2)
        te1 = Q.dve(lambda e: e.tensor_copy(SRCI[:, jj, :, :], v[:, :, 0, :]), [tp])
        te2 = Q.dve(lambda e: e.tensor_copy(DLS[:, jj, :, :], v[:, :, 1, :]))
        t_fldfree[0] = te2
        t_pfree[0] = [tp, tv, td]
        t_pfree[1] = [tv]
        return te2

    def chains_of_rows():
        tp = Q.pe(lambda e: e.matmul(PS[7][0:R, 0:NJ], K("sh85", R), FL[0][:], start=True, stop=True), [t_row[-1], t_fldfree[0]], last=True)
        t1 = Q.dve(lambda e: e.tensor_scalar(FL[2][:], PS[7][0:R, 0:NJ], K("k16", R), None, op0=ALU.add), [tp])
        t2 = Q.dve(lambda e: e.tensor_tensor(FL[3][:], FL[0][:], FL[1][:], op=ALU.is_equal))
        t3 = Q.dve(lambda e: e.tensor_tensor(FL[4][:], FL[2][:], FL[1][:], op=ALU.is_equal), [t1])
        t4 = Q.dve(lambda e: e.tensor_scalar(CS[:, :, 0], FL[3][:], 1.0, BIG, op0=ALU.subtract, op1=ALU.mult), [t2])
        t5 = Q.dve(lambda e: e.tensor_scalar(CS[:, :, 1], FL[4][:], 1.0, BIG, op0=ALU.subtract, op1=ALU.mult), [t3])
        t6 = Q.dve(lambda e: e.tensor_scalar(LF[:, :, ROW - 1], FL[4][:], -1.0, 1.0, op0=ALU.mult, op1=ALU.add), [t3])
        d_cs = cnt("d_cs")
        tq = Q.pe(lambda e: e.matmul(PS[7][0:R, 0:2 * NJ], K("order", R), CS[:].rearrange("p j c -> p (j c)"), start=True, stop=True), [t4, t5, t1], last=True)
        t5b = Q.dve(lambda e: e.tensor_copy(CSP[:].rearrange("p j c -> p (j c)"), PS[7][0:R, 0:2 * NJ]), [tq])
        tw = Q.dma(d_cs, CSD.rearrange("j p c -> p j c"), CSP[:], [t5b])
        tr = Q.dma(d_cs, CSB[:].rearrange("p n c -> p (n c)"), CSD.rearrange("(o j) p c -> o (j p c)", o=1).broadcast_to([4, 2 * NROW]), [tw])
        t_fldfree[0] = t5b
        for jj in range(NJ):
            for half in range(2):
                tq = Q.pe(lambda e, jj=jj, half=half: e.matmul(PS[7][:, half * R:(half + 1) * R], LF[:, jj, half * 128:(half + 1) * 128], IDN[0:R, 0:R], start=True, stop=True, is_transpose=True), [t6, t_fldfree[0]], last=(half == 1))
            t_fldfree[0] = Q.dve(lambda e, jj=jj: e.tensor_copy(LAST[:, jj, :, :], PS[7][:, 0:2 * R].rearrange("p (h n) -> p h n", h=2)), [tq])
        t7 = Q.dve(lambda e: e.memset(CRF[:, 0:1], -BIG))
        t8 = Q.dve(lambda e: e.tensor_copy(CRF[:, 1:1 + NROW], CSB[:, :, 1]), [tr])
        t9 = Q.dve(lambda e: e.tensor_tensor(ARV[:], CSB[:, :, 0], CSB[:, :, 1], op=ALU.add), [tr])
        t10 = Q.dve(lambda e: e.tensor_tensor(AFW[:], CSB[:, :, 0], CRF[:, 0:NROW], op=ALU.add), [t7, t8])
        return t10

    def verdict():
        t1 = Q.dve(lambda e: e.tensor_reduce(STAT[0:TN, 0:1], VAL[:], axis=AX.X, op=ALU.add), [t_fields[-1], t_stat])
        t2 = Q.dve(lambda e: e.tensor_reduce(STAT[0:R, 1:2], VALT[:], axis=AX.X, op=ALU.add), t_pfree[1])
        tp = Q.pe(lambda e: e.matmul(PS[7][0:1, 0:3], K("ones"), STAT[:, 0:3], start=True, stop=True), [t1, t2, t_uns, t_fldfree[0]], last=True)
        t3 = Q.dve(lambda e: e.tensor_scalar(SUMS[:, 0:2], PS[7][0:1, 0:2], float(E), None, op0=ALU.not_equal), [tp])
        t4 = Q.dve(lambda e: e.tensor_scalar(SUMS[:, 2:3], PS[7][0:1, 2:3], 0.0, None, op0=ALU.not_equal))
        t5 = Q.dve(lambda e: e.tensor_reduce(SUMS[:, 4:5], SUMS[:, 0:3], axis=AX.X, op=ALU.max), [t3, t4])
        t_fldfree[0] = t4
        return Q.dve(lambda e: e.tensor_copy(FLAG[:, 0:1], SUMS[:, 4:5]), [t5])

    def attention_weights():
        prev = []
        for l in range(2):
            H = HS[l]
            t0 = Q.dve(lambda e, l=l: e.memset(AZ[l][:], 0.0))
            for half in range(2):
                if H == 1:
                    t = Q.dve(lambda e, l=l, half=half: e.tensor_scalar(AZ[l][:, half, 4:5], ATC[l][:, half:half + 1], 0.4, None, op0=ALU.mult), [t0, t_at])
                else:
                    t = Q.dve(lambda e, l=l, half=half: e.tensor_scalar(AZ[l][:, half, 4 + 10 * half:4 + 10 * half + 6:5], K("mb"), ATC[l][:, half:half + 1], 0.4, op0=ALU.mult, op1=ALU.mult), [t0, t_at, t_con])
            for W in (WL[l], WR[l]):
                at = ATB[l][:].unsqueeze(1).broadcast_to([128, 2, CH])
                t1 = Q.dve(lambda e, W=W, at=at: e.tensor_tensor(ATW[0][:], W[:, :, 0:CH], at, op=ALU.mult), [t_wl, t_at] + prev)
                t2 = Q.dve(lambda e, H=H: e.tensor_reduce(ATR[:, :, 0:H], ATW[0][:].rearrange("p k (h c) -> p k h c", h=H), axis=AX.X, op=ALU.add), [t1] + prev)
                t3 = Q.dve(lambda e, W=W, H=H: e.tensor_scalar(W[:, :, CH:CH + H], ATR[:, :, 0:H], 0.6, None, op0=ALU.mult), [t2])
                prev = [t3]
            t4 = Q.dve(lambda e, l=l: e.tensor_scalar(ATB[l][:], ATB[l][:], 0.4, None, op0=ALU.mult), prev)
            prev = [t4, t]
        return prev

    PX = GF[5]
    t_pm0 = Q.pool(lambda e: e.memset(PM[:], 0.0))
    t_pad = Q.dma(d_rows, M3D[NROW:NROW + 3, :], PM[0:3, :], [t_pm0])

    pending = list(range(NJ))

    def prepare(j):
        t6, _, t8 = fields(j)
        degrees(j, t6)
        field_transposes(j, t8)
        early_read.append(t_deg[j])

    prepare(pending.pop(0))
    stored = [None] * NRING
    last1 = {}
    t_rows_ready = []
    parts = [round(i * NT / len(quart)) for i in range(len(quart) + 1)]
    for it in range(NT + LG + 2):
        ta = it - LG
        for q in range(len(quart)):
            if it < NT:
                build_quartet(it, q)
            if q == 1 and ta - 1 in last1:
                t_h = post1_vec(ta - 1, last1[ta - 1], (ta - 1) % 2)
            if q == 3 and ta - 1 in last1:
                t_z[1], t_te = transposes(ZB[1], t_h, ta % 2)
            if q == 5 and ta - 1 in last1:
                post1_mm(ta - 1, t_te, ta % 2)
            if 0 <= ta < NT:
                tm = apply_part(ta, parts[q], parts[q + 1], 0, ta % 2, [t_at_tile[ta], t_acc[ta % 2]])
        if it < NT:
            r = it % NRING
            stored[r] = Q.dma(d_ad[r], AD[it], RING[0:TN, r, :], [t_at_tile[it]])
        if 0 <= ta < NT:
            ring_free[ta % NRING] = [tm, stored[ta % NRING]]
            last1[ta] = tm
        if it < LG:
            for j in (pending if it == LG - 1 else pending[:1]):
                prepare(j)
            pending = [] if it == LG - 1 else pending[1:]
        if it == LG - 1:
            dis_chain()
            t_attw = attention_weights()
        if it in ROWS_AT:
            rows = rows_of_tiles(ROWS_AT.index(it))
        if it - 1 in ROWS_AT:
            columns_of_tiles(ROWS_AT.index(it - 1), *rows)
        if it == ROWS_AT[-1] + 2:
            early_read.append(t_row[-1])
            t_chain = chains_of_rows()
            t_flag = verdict()

    order = list(range(NT - NRING, NT)) + list(range(NT - NRING))
    slot = {t: t % NRING for t in order[:NRING]}
    for i in range(NRING, NT):
        slot[order[i]] = slot[order[i - NRING]]
    t_in = {t: t_at_tile[t] for t in order[:NRING]}
    d_xs = [cnt(f"d_xs{i}") for i in range(3)]
    d_xo, d_tab = [cnt(f"d_xo{i}") for i in range(2)], [[cnt(f"d_tab{l}{i}") for i in range(2)] for l in range(2)]
    d_xr = [[cnt(f"d_xro{l}{i}") for i in range(2)] for l in range(2)]
    t_xsfree = [t_xt_read[i] for i in range(3)]
    t_sm = [None, None]
    t_x1 = {}
    t_tab = [[], []]
    t_xro = [{}, {}]
    t_xl, t_xrs = [None, None], [None, None]

    def norm(y, t_y, yc, out, sm, t_sum, free, sq):
        t1 = Q.dve(lambda e: e.tensor_scalar(sm[:, 1:2], sm[:, 0:1], -1.0 / CH, None, op0=ALU.mult), [t_sum])
        t2 = Q.dve(lambda e: e.tensor_scalar(yc, y, sm[:, 1:2], None, op0=ALU.add), [t1, t_y])
        t3 = Q.act(lambda e: e.activation(sq, yc, ACT.Square, accum_out=sm[:, 2:3]), [t2])
        t4 = Q.dve(lambda e: e.tensor_scalar(sm[:, 3:4], sm[:, 2:3], 1.0 / CH, EPS, op0=ALU.mult, op1=ALU.add), [t3])
        t5 = Q.act(lambda e: e.activation(sm[:, 4:5], sm[:, 3:4], ACT.Sqrt), [t4])
        t6 = Q.dve(lambda e: e.reciprocal(sm[:, 5:6], sm[:, 4:5]), [t5])
        return Q.dve(lambda e: e.tensor_scalar(out, yc, sm[:, 5:6], None, op0=ALU.mult), [t6] + free)

    def post2_vec(i, t, tm):
        acc, b = i % 2, i % 3
        sm = SMALL[i % 2]
        z, y, yc, x1 = (ZB[k][:] for k in range(4))
        tl = t_xs[i]
        t1 = Q.dve(lambda e: e.tensor_tensor(z, PS[3 + acc][0:TN, 0:CH], HP[1][:, t, :], op=ALU.add), [tm, t_z[0]])
        t_acc[acc] = t1
        t2 = Q.dve(lambda e: e.scalar_tensor_tensor(y, z, DIS[:, t:t + 1], BB[1][:], op0=ALU.mult, op1=ALU.add), [t1, t_z[1]])
        t3 = Q.dve(lambda e: e.scalar_tensor_tensor(z, y, 1.0, XST[b][:], op0=ALU.mult, op1=ALU.add, accum_out=sm[:, 0:1]), [t2, tl, t_sm[i % 2]])
        t_xsfree[b] = t3
        t4 = norm(z, t3, yc, x1, sm, t3, [t_z[3], t_x1read[0]], y)
        t_z[0] = t_z[1] = t_sm[i % 2] = t4
        t_z[3] = to = Q.dma(d_xo[i % 2], X1D[t * TN:(t + 1) * TN, :], x1, [t4])
        t_x1[t] = to
        return t4

    def tables(l, t, k, t_ht_ready, HTk, M1, M2, XLk, XRk, free1, free2, w, cols):
        H = HS[l]
        for c in range(2):
            tm1 = Q.pe(lambda e, c=c: e.matmul(M1[0:TN, 0:CH + H], HTk[:, c, :], WL[l][:, c, :], start=(c == 0), stop=(c == 1)), [t_ht_ready] + t_attw + free1, last=(c == 1))
        ta = Q.act(lambda e: e.activation(XLk[:, 0:CH + H], M1[0:TN, 0:CH + H], ACT.Copy), [tm1, t_xl[k]] + t_lsf[k])
        td = Q.dma(d_tab[l][k], TAB[l][t * TN:(t + 1) * TN, :], XLk[:, 0:CH + H], [ta])
        t_xl[k] = td
        t_tab[l].append(td)
        yield ta
        for c in range(2):
            tm2 = Q.pe(lambda e, c=c: e.matmul(M2[0:TN, 0:CH + H], HTk[:, c, :], WR[l][:, c, :], start=(c == 0), stop=(c == 1)), free2, last=(c == 1))
        t_ht[k] = tm2
        th = Q.act(lambda e: e.activation(XRk[:, 0:CH].bitcast(F32R), M2[0:TN, 0:CH], ACT.Copy), [tm2, t_xrs[k]])
        th2 = Q.act(lambda e: e.activation(ARN[l][:, t, :], M2[0:TN, CH:CH + H], ACT.Copy))
        yield th2
        tl = Q.dve(lambda e: e.tensor_tensor(XRk[:, CH:2 * CH].bitcast(F32R), M2[0:TN, 0:CH], XRk[:, 0:CH], op=ALU.subtract), [th2])
        td = Q.dma(d_xr[l][k], XRD[l][t], XRk[:], [tl])
        t_xrs[k] = td
        t_xro[l][t] = td
        t1 = Q.dve(lambda e: e.tensor_tensor(w[0], M2[0:TN, 0:CH], XLk[:, 0:CH], op=ALU.add), [ta] + cols)
        t2 = Q.dve(lambda e: e.tensor_tensor(LSF[l][:, t, :], M2[0:TN, CH:CH + H], XLk[:, CH:CH + H], op=ALU.add))
        yield t2
        ta2 = Q.act(lambda e: e.activation(w[1], w[0], ACT.Abs), [t1] + cols)
        t3 = Q.dve(lambda e: e.tensor_tensor(w[0], w[1], ATB[l][0:TN, :], op=ALU.mult), [ta2])
        t4 = Q.dve(lambda e: e.tensor_reduce(w[2][:, 0:H], w[0].rearrange("p (h c) -> p h c", h=H), axis=AX.X, op=ALU.add), [t3] + cols)
        t5 = Q.dve(lambda e: e.tensor_tensor(LSF[l][:, t, :], LSF[l][:, t, :], w[2][:, 0:H], op=ALU.add), [t4, t2])
        t_lsf[k] = [t5]
        yield t5

    t_lsf = [[], []]
    t_x1read = [None]
    t_wfree = []
    m_free = [[t_pm[0]], [t_fldfree[0]]]
    W2B = [GF[3][:], GF[4][:], SMALL[0][:, 8:12]]
    cuts = [round(i * NT / 8) for i in range(9)]
    prev = None
    t_xs = {}

    def load_x(i):
        b, t = i % 3, order[i]
        t_xs[i] = Q.dma(d_xs[b], XST[b][:], A["x"][t * TN:(t + 1) * TN, :], [t_xsfree[b]])

    load_x(0)
    for i in range(NT + 1):
        if i < NT:
            t = order[i]
            RT = RING[0:TN, slot[t], :]
        tab = None
        for q in range(8):
            if i < NT:
                for s in range(cuts[q], cuts[q + 1]):
                    tm = Q.pe(lambda e, s=s, RT=RT, i=i: e.matmul(PS[3 + i % 2][0:TN, 0:CH], RT[:, s * TN:(s + 1) * TN], HP[1][:, s, :], start=(s == 0), stop=(s == NT - 1)), [t_in[t], t_hp[1][s], t_acc[i % 2]], last=(s == NT - 1))
            if prev is not None:
                pt, t_v, k = prev
                if q == 3:
                    t_tp, t_te = transposes(ZB[3], t_v, k)
                    t_x1read[0] = t_tp
                if q == 5:
                    tab = tables(0, pt, k, t_te, HT[k], PS[6], PS[7], XL[k], XRS[k], m_free[0], m_free[1], W2B, list(t_wfree))
                    m_free[0] = [next(tab)]
                if q == 6:
                    next(tab)
                if q == 7:
                    m_free[1] = [next(tab)]
                    t_wfree = [next(tab)]
        if i < NT:
            if i + 1 < NT:
                load_x(i + 1)
            if i + NRING < NT:
                nx = order[i + NRING]
                t_in[nx] = Q.dma(d_ad[slot[nx]], RING[0:TN, slot[nx], :], AD[nx], [tm, stored[slot[nx]]])
            t_v = post2_vec(i, t, tm)
            prev = (t, t_v, i % 2)

    gcn_end = [(Q.done[n], Q.done[n].value) for n in ("tensor", "vector", "scalar", "gpsimd")]
    gcn_end += [(c, c.value) for c in d_ad + d_xo + d_tab[0] + d_xr[0] + [d_rows]]
    gcn.close()

    gat = ExitStack()
    ss = lambda name, shape, dt=F32: gat.enter_context(nc.sbuf_tensor(name, shape, dt))
    NCH, CMAX = len(CHUNKS), max(b - a for a, b in CHUNKS)
    G = ss("g", [128, RP * 2 * (CH + 8)])
    NOT = 3
    OHT = [ss(f"oht{i}", [2 * WIN, CMAX * ROW], F32R) for i in range(NOT)]
    DLB = [ss(f"dlb{i}", [2 * WIN, CMAX * ROW], BF16) for i in range(NOT)]
    XR = [ss(f"xr{i}", [2 * WIN, len(WINS), CH], F32R) for i in range(2)]
    M3 = [ss(f"m3{i}", [128, 772], BF16) for i in range(2)]
    NAB = 8
    ABS = [ss(f"abs{i}", [128, 2 * ROW]) for i in range(NAB)]
    NOH = 4 * CMAX
    OH = [ss(f"oh{i}", [128, 3 * BL]) for i in range(NOH)]
    ALB = ss("alb", [128, 2, 128])
    F1, F2, F3, EX = (ss(n, [128, ROW]) for n in ("f1", "f2", "f3", "ex"))
    SGM = ss("sgm", [128, 2 * KP])
    VW = ss("vw", [4, 2 * KP])
    CC = ss("cc", [4, 2, KP])
    CRL = ss("crl", [128, 2])
    XLT = [ss(f"xlt{i}", [TN, CH]) for i in range(2)]
    X1T = [ss(f"x1t{i}", [TN, CH]) for i in range(2)]
    SM = [ss(f"sm{i}", [TN, 64]) for i in range(2)]
    O = [ss(f"o{i}", [TN, CH]) for i in range(4)]
    HT2 = [ss(f"ht2{i}", [128, 2, TN]) for i in range(2)]
    XL2 = [ss(f"xl2{i}", [TN, CH + 1]) for i in range(2)]
    XRS2 = [ss(f"xrs2{i}", [TN, 2 * CH]) for i in range(2)]
    W2C = [ss(f"w2c{i}", [TN, CH]) for i in range(2)]
    W2D = ss("w2d", [TN, 4])
    NG5 = 5
    YC = [ss(f"yc{i}", [TN, NG5, CH]) for i in range(2)]
    SSQ = [ss(f"ssq{i}", [TN, 3, NG5]) for i in range(2)]

    d_g = [[cnt(f"d_g{i}{a}") for a in range(2)] for i in range(RP)]
    d_dlb = [cnt(f"d_dlb{i}") for i in range(NOT)]
    d_xri = [cnt(f"d_xri{i}") for i in range(2)]
    d_m3 = [cnt(f"d_m3{i}") for i in range(2)]
    d_xlt = [cnt(f"d_xlt{i}") for i in range(2)]
    d_x1t = [cnt(f"d_x1t{i}") for i in range(2)]
    d_out = [cnt(f"d_out{i}") for i in range(2)]

    for n in ("sync", "tensor", "vector", "scalar", "gpsimd"):
        Q.put(n, None, gcn_end)
    for k in range(2):
        t_xl[k] = t_xrs[k] = None
        t_lsf[k] = []
    t_ht[0] = t_ht[1] = None

    windows, blocks, _ = reach(E, N)
    MT = (0, 1, 2, 7)
    NMT = len(MT)
    LBK, AGG = (3, 4), (5, 6)
    t_mt = [None] * NMT
    t_abs = [None] * NAB
    t_oh2 = [None] * NOH
    t_gfree = [None] * RP
    t_g = {}
    t_oht = {}
    t_ohtfree, t_dlbfree = [None] * NOT, [None] * NOT
    t_xrfree, t_m3free = [None, None], [None, None]
    t_lfree = [None, None]
    t_aggfree = [[], []]
    t_xltfree, t_x1tfree = [None, None], [None, None]
    t_smfree = [[], []]
    t_o = [None] * 4
    t_cc0 = Q.dve(lambda e: e.memset(CC[:], -BIG))
    for x in (*M3, ALB):
        t_m0 = Q.dve(lambda e, x=x: e.memset(x[:], 0.0))
    t_alb = [t_m0]
    t_ycfree = [[], []]
    oh_no = [0]
    chunk_of = [min(i // 4, NCH - 1) for i in range(KP)]

    def attention(l, tab_ready, xr_ready):
        H = HS[l]
        GW = CH + 2 * H
        C = CH // H
        GV = G[:, 0:RP * 2 * GW].rearrange("p (r a c) -> p r a c", r=RP, a=2)
        sched = {}
        at = lambda it, fn: sched.setdefault(it, []).append(fn)
        t_dlb, t_xri, t_m3, t_xlt, t_x1t, t_mm, t_a, t_ex, t_scaled = ({} for _ in range(9))
        st0, st1, st2, st3 = [None], [None], [None], [None]

        def load_targets(c):
            t, n = divmod(c, NCH)
            a, b = CHUNKS[n]
            t_dlb[c] = Q.dma(d_dlb[c % NOT], DLB[c % NOT][:, 0:(b - a) * ROW], DLBD.rearrange("(t k) e -> t (k e)", t=NT)[t:t + 1, a * ROW:b * ROW].broadcast_to([2 * WIN, (b - a) * ROW]), [t_dlbfree[c % NOT]])

        def load_windows(t):
            b = t % 2
            for w, w0 in enumerate(WINS):
                src = XRD[l][t].rearrange("n (x c) -> x n c", x=2)[:, w0:w0 + WIN, :]
                t_xri[t] = Q.dma(d_xri[b], XR[b][:, w, :].bitcast(F32), src, [xr_ready[t], t_xrfree[b]])

        def load_masks(t):
            b = t % 2
            for g in range(4):
                rows = M3D[t * KP + g:t * KP + g + 17:4, :]
                for h in range(H):
                    t_m3[t] = Q.dma(d_m3[b], M3[b][BL * g + 5 * h:BL * g + 5 * h + 5, :], rows, [t_m3free[b], t_m0])

        def load_self(t):
            b = t % 2
            t_xlt[t] = Q.dma(d_xlt[b], XLT[b][:], TAB[l][t * TN:(t + 1) * TN, 0:CH], [t_xltfree[b]])
            if l == 1:
                t_x1t[t] = Q.dma(d_x1t[b], X1T[b][:], X1D[t * TN:(t + 1) * TN, :], [t_x1tfree[b]])

        def place(t, i):
            return t // 5, (t % 5) * KP + i

        def gather(q):
            r = q % RP
            j, c = place(q // KP, q % KP)
            t_g[q] = [Q.put("gpsimd", lambda e, a=a: e.indirect_dma_start(out=GV[:, r, a, 0:CH + H], out_offset=None, in_=TAB[l], in_offset=off(SRCI[:, j, a, c:c + 1])), [t_gfree[r]] + (tab_ready if q == 0 else []), d_g[r][a], 16) for a in range(2)]

        def onehot_t(c):
            b = c % NOT
            w = (CHUNKS[c % NCH][1] - CHUNKS[c % NCH][0]) * ROW
            t_oht[c] = t_dlbfree[b] = Q.dve(lambda e: e.tensor_scalar(OHT[b][:, 0:w], DLB[b][:, 0:w], K("pwin", 2 * WIN), None, op0=ALU.is_equal), [t_dlb[c], t_ohtfree[b]])

        def expand(q):
            t, i = q // KP, q % KP
            c = t * NCH + chunk_of[i]
            e0 = (i - CHUNKS[chunk_of[i]][0]) * ROW
            w = WINS.index(windows[i])
            b, r, bank = t % 2, q % RP, PS[MT[q % NMT]]
            first = [t_oht[c], t_xri[t], t_mt[q % NMT]]
            for half in range(2):
                tm = Q.pe(lambda e, half=half: e.matmul(bank[:, half * ROW:(half + 1) * ROW], XR[b][:, w, half * 128:(half + 1) * 128], OHT[c % NOT][:, e0:e0 + ROW], start=(half == 0), stop=False, skip_group_check=True), first if half == 0 else [])
            for half in range(2):
                for a in range(2):
                    tm = Q.pe(lambda e, half=half, a=a: e.matmul(bank[:, half * ROW + a * 128:half * ROW + (a + 1) * 128], GV[:, r, a, half * 128:(half + 1) * 128], IDN, start=False, stop=(half == 1 and a == 1), is_transpose=True, skip_group_check=True), [t_g[q][a]], last=(half == 1 and a == 1))
            t_mm[q] = tm
            if i == KP - 1:
                t_xrfree[b] = tm
            if i == CHUNKS[chunk_of[i]][1] - 1:
                t_ohtfree[c % NOT] = tm
            t_a[q] = t_mt[q % NMT] = Q.act(lambda e: e.activation(ABS[q % NAB][:], bank[:], ACT.Abs), [tm, t_abs[q % NAB]])

        def linear(t, q):
            r0 = (t % 2) * KP
            for a in range(2):
                src = GV[:, r0:r0 + 16, a, CH:CH + H].rearrange("p (k g) h -> p g h k", g=4)
                dst = ALB[:, a, :].rearrange("p (g x) -> p g x", g=4)[:, :, 0:20].rearrange("p g (h k) -> p g h k", k=5)[:, :, 0:H, 0:4]
                Q.dve(lambda e, src=src, dst=dst: e.tensor_copy(dst, src), [t_mm[q], t_alb[0]])
            src = GV[:, r0 + 16, :, CH:CH + H]
            dst = ALB[:, :, 4:4 + 5 * H:5]
            return Q.dve(lambda e: e.tensor_copy(dst, src), [t_mm[q], t_alb[0]])

        def logits(c):
            t, n = divmod(c, NCH)
            bank = PS[LBK[t % 2]]
            a, b = CHUNKS[n]
            first = [t_a[t * KP + b - 1], t_lfree[t % 2] if n == 0 else None]
            for i0 in range(a, b, 4):
                for half in range(2):
                    for i in range(i0, min(i0 + 4, b)):
                        g, q = i % 4, t * KP + i
                        tm = Q.pe(lambda e, g=g, i=i, half=half, q=q: e.matmul(bank[BL * g:BL * (g + 1), 0:ROW], AZ[l][:, half, 4 - i // 4:4 - i // 4 + BL], ABS[q % NAB][:, half * ROW:(half + 1) * ROW], start=(i < 4 and half == 0), stop=False, skip_group_check=True), first, last=(i == b - 1 and half == 1))
                        first = []
            for i in range(a, b):
                t_abs[(t * KP + i) % NAB] = tm
            if n == NCH - 1:
                tl = linear(t, t * KP + KP - 1)
                for a in range(2):
                    tm = Q.pe(lambda e, a=a: e.matmul(bank[:, a * 128:(a + 1) * 128], ALB[:, a, :], IDN, start=False, stop=(a == 1), is_transpose=True, skip_group_check=True), [tl], last=(a == 1))
                t_alb[0] = tm
            return tm

        def softmax_rows(t, tl, it):
            b = t % 2
            r0 = (t % 2) * KP
            F, Pm, Sm = M3[b][:, 0:ROW + 1], M3[b][:, ROW + 1:2 * ROW + 1], M3[b][:, 2 * ROW + 1:3 * ROW + 1]
            bank = PS[LBK[b]]
            Lrow = bank[:, 0:ROW]
            S2 = K("sel2")
            j, c0 = place(t, 0)
            st = {}

            def s1():
                t1 = Q.dve(lambda e: e.tensor_tensor_scan(F1[:], F[:, 0:ROW], Lrow, -BIG, op0=ALU.add, op1=ALU.max), [tl, t_m3[t], st1[0]])
                t2 = Q.dve(lambda e: e.tensor_tensor_scan(F2[:, ::-1], F[:, ROW:0:-1], F1[:, ::-1], -BIG, op0=ALU.add, op1=ALU.max), [t1, st1[0]])
                st["g"] = t2
                st["sg"] = Q.dve(lambda e: e.tensor_tensor(SGM[:].rearrange("p (x k) -> p x k", x=2), S2.rearrange("p (x k) -> p x k", x=2), F2[:, 0:ROW:ROW - 1].unsqueeze(2).broadcast_to([128, 2, KP]), op=ALU.mult), [t2, st1[0]])

            def s2():
                chp = bank[0:H, ROW:ROW + 2 * KP]
                tp = Q.pe(lambda e: e.matmul(chp, K("hm")[:, 0:H], SGM[:], start=True, stop=True), [st["sg"]], last=True)
                row = slice(t * KP, (t + 1) * KP)
                t1 = Q.dve(lambda e: e.tensor_tensor_scan(VW[0:H, KP:2 * KP], AFW[0:H, row], chp[:, KP:2 * KP], -BIG, op0=ALU.add, op1=ALU.max), [tp, t_chain])
                t2 = Q.dve(lambda e: e.tensor_tensor_scan(VW[0:H, 0:KP][:, ::-1], ARV[0:H, row][:, ::-1], chp[:, 0:KP][:, ::-1], -BIG, op0=ALU.add, op1=ALU.max))
                t3 = Q.dve(lambda e: e.tensor_tensor(CC[0:H, 1, 1:KP], VW[0:H, KP:2 * KP - 1], CRF[0:H, t * KP + 1:(t + 1) * KP], op=ALU.add), [t1, t_cc0, st2[0]])
                st["cc"] = Q.dve(lambda e: e.tensor_tensor(CC[0:H, 0, 0:KP - 1], VW[0:H, 1:KP], CRF[0:H, t * KP + 1:(t + 1) * KP], op=ALU.add), [t2])

            def s3():
                exp_ = bank[:, ROW + 64:ROW + 64 + 2 * KP]
                tp = Q.pe(lambda e: e.matmul(exp_, K("hmt", 4)[0:H, :], CC[0:H, :, :].rearrange("p x k -> p (x k)"), start=True, stop=True), [st["cc"]], last=True)
                st2[0] = tp
                t1 = Q.dve(lambda e: e.tensor_tensor(SGM[:], exp_, S2, op=ALU.mult), [tp])
                t2 = Q.dve(lambda e: e.tensor_reduce(CRL[:], SGM[:].rearrange("p (x k) -> p x k", x=2), axis=AX.X, op=ALU.add), [t1])
                t3 = Q.dve(lambda e: e.scalar_tensor_tensor(F1[:], Pm, CRL[:, 1:2], F2[:], op0=ALU.add, op1=ALU.max), [t2])
                t4 = Q.dve(lambda e: e.scalar_tensor_tensor(F3[:], Sm, CRL[:, 0:1], F1[:], op0=ALU.add, op1=ALU.max), [t3, st3[0]])
                t_m3free[b] = t4
                t5 = Q.dve(lambda e: e.tensor_tensor(F2[:], Lrow, F3[:], op=ALU.subtract), [t4])
                st["e"] = Q.act(lambda e: e.activation(EX[:], F2[:], ACT.Exp), [t5, st3[0]])
                st1[0] = st["e"]

            def s4():
                for x, src in ((0, EX), (1, F3)):
                    for a in range(2):
                        tp = Q.pe(lambda e, x=x, a=a, src=src: e.matmul(bank[:, (2 * x + a) * 128:(2 * x + a + 1) * 128], src[:, a * 128:(a + 1) * 128], IDN, start=True, stop=True, is_transpose=True), [st["e"]], last=(x == 1 and a == 1))
                st3[0] = tp
                for a in range(2):
                    v = bank[:, a * 128:(a + 1) * 128].rearrange("p (g x) -> p g x", g=4)[:, :, 0:20].rearrange("p g (h k) -> p g h k", k=5)[:, :, 0:H, 0:4]
                    out = GV[:, r0:r0 + 16, a, CH:CH + H].rearrange("p (k g) h -> p g h k", g=4)
                    t1 = Q.dve(lambda e, out=out, v=v: e.tensor_copy(out, v), [tp])
                v = bank[:, 0:256].rearrange("p (a n) -> p a n", a=2)[:, :, 4:4 + 5 * H:5]
                t_ex[t] = Q.dve(lambda e: e.tensor_copy(GV[:, r0 + 16, :, CH:CH + H], v), [tp])

            def s5():
                for a in range(2):
                    v = bank[:, 256 + a * 128:256 + (a + 1) * 128].rearrange("p (g x) -> p g x", g=4)[:, :, 0:20].rearrange("p g (h k) -> p g h k", k=5)[:, :, 0:H, 0:4]
                    out = GV[:, r0:r0 + 16, a, CH + H:CH + 2 * H].rearrange("p (k g) h -> p g h k", g=4)
                    last = LAST[:, j, a, c0:c0 + 16].rearrange("p (k g) -> p g k", g=4).unsqueeze(2).broadcast_to([128, 4, H, 4])
                    t1 = Q.dve(lambda e, out=out, v=v, last=last: e.tensor_tensor(out, v, last, op=ALU.mult), [t_ex[t]])
                v = bank[:, 256:512].rearrange("p (a n) -> p a n", a=2)[:, :, 4:4 + 5 * H:5]
                last = LAST[:, j, :, c0 + 16].unsqueeze(2).broadcast_to([128, 2, H])
                t_lfree[b] = t_ex[t] = Q.dve(lambda e: e.tensor_tensor(GV[:, r0 + 16, :, CH + H:CH + 2 * H], v, last, op=ALU.mult), [t_ex[t]])

            for n, f in enumerate((s1, s2, s3, s4, s5)):
                at(it + n, f)

        def scale(q):
            t, i = q // KP, q % KP
            r = q % RP
            j, c = place(t, i)
            t_scaled[q] = []
            for a in range(2):
                o = oh_no[0] % NOH
                oh_no[0] += 1
                b0, b1 = blocks[2 * i + a]
                w = (b1 - b0 + 1) * BL
                Q.dve(lambda e, a=a, o=o, b0=b0, w=w: e.tensor_scalar(OH[o][:, 0:w], K("iota")[:, b0 * BL:b0 * BL + w], DLS[:, j, a, c:c + 1], None, op0=ALU.is_equal), [t_oh2[o]])
                rows = GV[:, r, a, 0:CH]
                if H == 1:
                    t2 = Q.dve(lambda e, a=a, rows=rows: e.tensor_scalar(rows, rows, GV[:, r, a, CH:CH + 1], None, op0=ALU.mult), [t_ex[t]])
                else:
                    rv = rows.rearrange("p (h c) -> p h c", h=H)
                    t2 = Q.dve(lambda e, a=a, rv=rv: e.tensor_tensor(rv, rv, GV[:, r, a, CH:CH + H].unsqueeze(2).broadcast_to([128, H, C]), op=ALU.mult), [t_ex[t]])
                t_scaled[q].append((o, t2))

        seen_block = {}

        def sums(c):
            t, n = divmod(c, NCH)
            a_, b_ = CHUNKS[n]
            todo = [[] for _ in range(4)]
            for i in range(a_, b_):
                for a in range(2):
                    b0, b1 = blocks[2 * i + a]
                    for blk in range(b0, b1 + 1):
                        todo[blk].append((i, a, blk - b0))
            later = {blk for m in range(n + 1, NCH) for i in range(*CHUNKS[m]) for a in range(2) for blk in range(blocks[2 * i + a][0], blocks[2 * i + a][1] + 1)}
            count = sum(len(x) for x in todo)
            first = [t_scaled[t * KP + b_ - 1][1][1]] + (t_aggfree[t % 2] if n == 0 else [])
            while any(todo):
                for blk in range(4):
                    if not todo[blk]:
                        continue
                    i, a, s = todo[blk].pop(0)
                    count -= 1
                    r = (t * KP + i) % RP
                    o = t_scaled[t * KP + i][a][0]
                    start = seen_block.setdefault((t, blk), True)
                    seen_block[(t, blk)] = False
                    stop = not todo[blk] and blk not in later
                    tm = Q.pe(lambda e, o=o, s=s, r=r, a=a, blk=blk, start=start, stop=stop: e.matmul(PS[AGG[t % 2]][blk * BL:(blk + 1) * BL, 0:GW], OH[o][:, s * BL:(s + 1) * BL], GV[:, r, a, 0:GW], start=start, stop=stop, skip_group_check=True), first, last=(count == 0))
                    first = []
            for i in range(a_, b_):
                q = t * KP + i
                t_gfree[q % RP] = tm
                for o, _ in t_scaled[q]:
                    t_oh2[o] = tm
            return tm

        def finish(t, tm, it):
            b = t % 2
            agg = PS[AGG[b]][0:TN, 0:GW]
            sm = SM[b]
            D, M = agg[:, CH:CH + H], agg[:, CH + H:CH + 2 * H]
            self_ = LSF[l][:, t, :]
            e0, mf, mm = sm[:, 0:H], sm[:, 4:4 + H], sm[:, 8:8 + H]
            dd, rs = sm[:, 16:16 + 2 * H], sm[:, 24:24 + 2 * H]
            den, rec, fr = sm[:, 32:32 + H], sm[:, 36:36 + H], sm[:, 40:40 + 2 * H]
            st = {}
            o1, o2, o3, o4 = (x[:] for x in O)

            def f0():
                t1 = Q.dve(lambda e: e.tensor_scalar(e0, D, 0.0, -BIG, op0=ALU.is_equal, op1=ALU.mult), [tm] + t_smfree[b])
                t2 = Q.dve(lambda e: e.tensor_tensor(mf, M, e0, op=ALU.add), [t1])
                t2 = Q.dve(lambda e: e.tensor_tensor(mf, mf, ARN[l][:, t, :], op=ALU.add), [t2])
                t3 = Q.dve(lambda e: e.tensor_tensor(mm, mf, self_, op=ALU.max), [t2])
                t4 = Q.dve(lambda e: e.tensor_tensor(dd[:, 0:H], mf, mm, op=ALU.subtract), [t3])
                t5 = Q.dve(lambda e: e.tensor_tensor(dd[:, H:2 * H], self_, mm, op=ALU.subtract))
                st["x"] = Q.act(lambda e: e.activation(rs, dd, ACT.Exp), [t5])

            def f1():
                t1 = Q.dve(lambda e: e.tensor_tensor(den, D, rs[:, 0:H], op=ALU.mult), [st["x"]])
                t2 = Q.dve(lambda e: e.tensor_tensor(e0, den, rs[:, H:2 * H], op=ALU.add), [t1])
                t3 = Q.dve(lambda e: e.reciprocal(rec, e0), [t2])
                t4 = Q.dve(lambda e: e.tensor_tensor(fr.rearrange("p (x h) -> p x h", x=2), rs.rearrange("p (x h) -> p x h", x=2), rec.unsqueeze(1).broadcast_to([TN, 2, H]), op=ALU.mult), [t3])
                hv = lambda x: x.rearrange("p (h c) -> p h c", h=H)
                st["a"] = Q.dve(lambda e: e.tensor_tensor(hv(o1), hv(agg[:, 0:CH]), fr[:, 0:H].unsqueeze(2).broadcast_to([TN, H, C]), op=ALU.mult), [t4, t_o[0]])
                st["b"] = Q.dve(lambda e: e.tensor_tensor(hv(o2), hv(XLT[b][:]), fr[:, H:2 * H].unsqueeze(2).broadcast_to([TN, H, C]), op=ALU.mult), [t_xlt[t], t_o[1]])
                t_smfree[b] = [st["b"]]
                t_xltfree[b] = st["b"]

            def f2():
                t1 = Q.dve(lambda e: e.tensor_tensor(o3, o1, o2, op=ALU.add), [st["b"], t_o[2]])
                st["o"] = Q.dve(lambda e: e.tensor_tensor(o1, o3, BB[2 + l][:], op=ALU.add), [t1])

            if l == 0:
                def f3():
                    t1 = Q.dve(lambda e: e.tensor_scalar(o2, o1, 0.0, None, op0=ALU.min), [st["o"]])
                    t2 = Q.act(lambda e: e.activation(o3, o2, ACT.Exp), [t1])
                    st["e"] = t2

                def f4():
                    t1 = Q.dve(lambda e: e.scalar_tensor_tensor(o2, o1, 0.0, o3, op0=ALU.max, op1=ALU.add), [st["e"]])
                    st["h"] = Q.dve(lambda e: e.tensor_scalar(o4, o2, -1.0, None, op0=ALU.add), [t1, t_o[3]])
                    t_o[0] = t_o[1] = t_o[2] = st["h"]

                def f5():
                    bank = PS[AGG[b]]
                    for c in range(2):
                        tp = Q.pe(lambda e, c=c: e.matmul(bank[:, c * TN:(c + 1) * TN], o4[:, c * 128:(c + 1) * 128], IDN[0:TN, 0:TN], start=True, stop=True, is_transpose=True), [st["h"]], last=(c == 1))
                    t_o[3] = tp
                    te = Q.act(lambda e: e.activation(HT2[b][:], bank[:, 0:2 * TN].rearrange("p (k n) -> p k n", k=2), ACT.Copy), [tp, t_ht[b]])
                    st["tab"] = tables(1, t, b, te, HT2[b], bank, bank, XL2[b], XRS2[b], [], [], [W2C[0][:], W2C[1][:], W2D], list(t_wfree2))

                def f6():
                    st["m1"] = next(st["tab"])

                def f7():
                    Q.put("tensor", None, [st["m1"]])
                    next(st["tab"])

                def f8():
                    next(st["tab"])

                def f9():
                    t_wfree2[:] = [next(st["tab"])]
                    t_aggfree[b] = list(t_wfree2)

                steps = (f0, f1, f2, f3, f4, f5, f6, f7, f8, f9)
            else:
                g, n = divmod(t, NG5)
                y = g % 2
                yc = YC[y]

                def f3():
                    t1 = Q.dve(lambda e: e.scalar_tensor_tensor(o2, o1, 1.0, X1T[b][:], op0=ALU.mult, op1=ALU.add, accum_out=sm[:, 48:49]), [st["o"], t_x1t[t]])
                    t_x1tfree[b] = t1
                    t2 = Q.dve(lambda e: e.tensor_scalar(sm[:, 49:50], sm[:, 48:49], -1.0 / CH, None, op0=ALU.mult), [t1])
                    t3 = Q.dve(lambda e: e.tensor_scalar(yc[:, n, :], o2, sm[:, 49:50], None, op0=ALU.add), [t2] + t_ycfree[y])
                    t4 = Q.act(lambda e: e.activation(o3, yc[:, n, :], ACT.Square, accum_out=SSQ[y][:, 0, n:n + 1]), [t3])
                    t_o[0] = t_o[1] = t_o[2] = t4
                    t_smfree[b].append(t3)
                    st["n"] = t4
                    t_aggfree[b] = [st["a"]]

                def f4():
                    if n == NG5 - 1 or t == NT - 1:
                        w = n + 1
                        t1 = Q.dve(lambda e: e.tensor_scalar(SSQ[y][:, 1, 0:w], SSQ[y][:, 0, 0:w], 1.0 / CH, EPS, op0=ALU.mult, op1=ALU.add), [st["n"]])
                        t2 = Q.act(lambda e: e.activation(SSQ[y][:, 2, 0:w], SSQ[y][:, 1, 0:w], ACT.Sqrt), [t1])
                        t3 = Q.dve(lambda e: e.reciprocal(SSQ[y][:, 1, 0:w], SSQ[y][:, 2, 0:w]), [t2])
                        for i in range(w):
                            t4 = Q.dve(lambda e, i=i: e.tensor_scalar(yc[:, i, :], yc[:, i, :], SSQ[y][:, 1, i:i + 1], None, op0=ALU.mult), [t3])
                        t0 = t - n
                        td = Q.dma(d_out[y], A["out"][t0 * TN:(t + 1) * TN, :].rearrange("(t p) c -> p t c", p=TN), yc[:, 0:w, :], [t4])
                        t_ycfree[y] = [td]

                steps = (f0, f1, f2, f3, f4)
            for n_, f in enumerate(steps):
                at(it + 1 + n_, f)

        t_wfree2 = []
        LEAD = RP - LAGC - 6
        for c in range(NOT):
            load_targets(c)
        load_windows(0)
        load_masks(0)
        onehot_t(0)
        load_targets(NOT)
        for q in range(LEAD):
            gather(q)
        due = {}
        it = 0
        while it < NP + LAGC + 8 or sched:
            if it < NP:
                t, i = it // KP, it % KP
                if i == 2 and t + 1 < NT:
                    load_windows(t + 1)
                if i == 9 and t + 1 < NT:
                    load_masks(t + 1)
                n = chunk_of[i]
                c = t * NCH + n
                if i == CHUNKS[n][0] + 1 and c + 1 < NT * NCH:
                    onehot_t(c + 1)
                    if c + 1 + NOT < NT * NCH:
                        load_targets(c + 1 + NOT)
                expand(it)
                if i == CHUNKS[n][1] - 1:
                    due.setdefault(it + 2, []).append(c)
            if it >= LAGC - 2 and (it - LAGC + 2) % KP == 0 and (it - LAGC + 2) // KP < NT:
                load_self((it - LAGC + 2) // KP)
            for f in sched.pop(it, []):
                f()
            if 0 <= it - LAGC < NP:
                scale(it - LAGC)
            for c in due.pop(it, []):
                tl = logits(c)
                if c % NCH == NCH - 1:
                    softmax_rows(c // NCH, tl, it + 1)
            x = it - LAGC - 1
            if 0 <= x < NP and x % KP in [b - 1 for _, b in CHUNKS]:
                tm = sums(x // KP * NCH + chunk_of[x % KP])
                if x % KP == KP - 1:
                    finish(x // KP, tm, it)
            if it + LEAD < NP:
                gather(it + LEAD)
            it += 1

    attention(0, t_tab[0], t_xro[0])
    attention(1, t_tab[1], t_xro[1])

    ended = [(Q.done[n], Q.done[n].value) for n in Q.done] + [(c, c.value) for c in d_out + d_tab[1] + d_xr[1]]
    for n in Q.lists:
        Q.put(n, None, ended)
    gat.close()
    W = {"2": W2S, "l0": WL[0], "r0": WR[0], "l1": WL[1], "r1": WR[1]}
    return ctx, Q, FLAG, general_path(nc, ctx, sem, A, NT, E, PS, IOTA, IDN, K("pidx", TN), W, BB, DIS)


class Serial:

    ENGINES = ("sync", "tensor", "vector", "scalar", "gpsimd")

    def __init__(self, sem):
        self.chain, self.met, self.rows = sem("g_chain"), sem("g_met"), sem("g_rows")
        self.go = {n: sem(f"g_go_{n}") for n in self.ENGINES if n != "gpsimd"}
        self.rounds = []

    def once(self, *steps):
        self.rounds.append((None, steps))

    def loop(self, count, *steps):
        self.rounds.append((count, steps))

    def run(self, name, e, steps, i):
        at = gathered = 0
        for engine, fns in steps:
            if engine == name:
                if at:
                    e.wait_ge(self.chain, at)
                for f in fns:
                    ins = f(e, i)
                    if engine == "sync":
                        ins.then_inc(self.chain, 16)
                if engine == "gpsimd":
                    gathered += 16
                    ins.then_inc(self.rows, 16)
                    e.wait_ge(self.rows, gathered)
                    e.sem_inc(self.chain, 1)
                elif engine != "sync":
                    ins.then_inc(self.chain, 1)
            at += 16 * len(fns) if engine == "sync" else 1
        e.wait_ge(self.chain, at)
        if name == "gpsimd":
            e.wait_ge(self.met, len(self.go))
            e.sem_clear(self.chain)
            if gathered:
                e.dma_reset(range(self.rows.num, self.rows.num + 1))
                e.sem_clear(self.rows)
            e.sem_inc(self.met, -len(self.go))
            for g in self.go.values():
                e.sem_inc(g, 1)
        else:
            e.sem_inc(self.met, 1)
            e.wait_ge(self.go[name], 1)
            e.sem_inc(self.go[name], -1)

    def emit(self, name, e):
        for count, steps in self.rounds:
            if count is None:
                self.run(name, e, steps, None)
            else:
                with e.Fori(0, count) as i:
                    self.run(name, e, steps, i)


def general_path(nc, ctx, sem, A, NT, E, PS, IOTA, IDN, PIDX, W, BB, DIS):
    N = NT * TN
    NR = A["sdr"].shape[0]
    CK = 4
    HS = (4, 1)
    sb = lambda name, shape, dt=F32: ctx.enter_context(nc.sbuf_tensor(f"g_{name}", shape, dt))
    dram = lambda name, shape, dt=F32: nc.dram_tensor(f"g_{name}", shape, dt, kind="Internal").ap()
    S = Serial(sem)
    off = lambda ap: bass.IndirectOffsetOnAxis(ap=ap, axis=0)

    DISD = dram("dis_d", (NT, TN, 1))
    HPD = [dram(f"hp{k}_d", (NT, TN, CH)) for k in range(2)]
    ACCD = dram("acc_d", (NT, TN, CH + 4))
    X1 = dram("x1_d", (NT, TN, CH))
    XLD = [dram(f"xl{l}_d", (NT, TN, CH)) for l in range(2)]
    XRD = [dram(f"xr{l}_d", (N + 1, CH)) for l in range(2)]
    LSD = [dram(f"ls{l}_d", (NT, TN, 4)) for l in range(2)]
    LGE = [dram(f"lge{l}_d", (NR, 128, HS[l])) for l in range(2)]
    LGR = [dram(f"lgr{l}_d", (NR, HS[l], 128)) for l in range(2)]
    MXD = [dram(f"mx{l}_d", (N + 1, 4)) for l in range(2)]

    NIO, OHA = sb("nio", [128, N]), sb("oha", [128, N])
    NID = sb("nid", [TN, NT])
    ATG = [sb(f"atg{l}", [128, CH]) for l in range(2)]
    ACC = sb("acc", [TN, NT, CH + 4])
    DGA = [sb(f"dga{k}", [TN, NT]) for k in range(4)]
    SDI, DF, DC, DI, EWC = sb("sdi", [128, 2], I32), sb("df", [128, 1]), sb("dc", [128, 1]), sb("di", [128, 1], I32), sb("ewc", [128, 1])
    GR, GX, GW_ = sb("gr", [128, CH + 4]), sb("gx", [128, CH]), sb("gw", [128, CH])
    LE, LX, MXG, LER = sb("le", [128, 4]), sb("lx", [128, 4]), sb("mxg", [128, 4]), sb("ler", [4, 128])
    DBI, DBF, MK = sb("dbi", [TN, CK * 128], I32), sb("dbf", [TN, CK * 128]), sb("mk", [TN, CK * 128])
    LB, TMP = sb("lb", [TN, CK * 4 * 128]), sb("tmp", [TN, CK * 4 * 128])
    MXA, LSA, MXT = sb("mxa", [TN, NT, 4]), sb("lsa", [TN, NT, 4]), sb("mxt", [TN, 4])
    DIT = sb("dit", [NT, TN])
    W = {"1": sb("w1", [128, 2, CH]), **W}
    ROWP = sb("rowp", [1, CH])
    BIGR = sb("bigr", [1, 4])
    X, Y, Z, AC, T1, T2 = (sb(n, [TN, CH + 4]) for n in ("x", "y", "z", "ac", "t1", "t2"))
    HT = sb("ht", [128, 2, TN])
    DSC, SM, LST = sb("dsc", [TN, 1]), sb("sm", [TN, 8]), sb("lst", [TN, 4])

    dve = lambda *f: ("vector", f)
    act = lambda *f: ("scalar", f)
    pe = lambda *f: ("tensor", f)
    gather = lambda out, table, idx: ("gpsimd", [lambda e, i: e.indirect_dma_start(out=out, out_offset=None, in_=table, in_offset=off(idx))])
    dma = lambda *f: ("sync", [(lambda e, i, x=x: e.dma_start(*x(i))) for x in f])
    at = lambda arr, i: arr[bass.ds(i, 1)].rearrange("a p c -> (a p) c")
    flat = lambda arr: arr.rearrange("t p c -> (t p) c")
    xv = A["x"].rearrange("(t p) c -> t p c", p=TN)
    ov = A["out"].rearrange("(t p) c -> t p c", p=TN)
    x_, y_, z_, t1_, t2_ = (b[:, 0:CH] for b in (X, Y, Z, T1, T2))

    def project(src, Wm):
        return [pe(*[lambda e, i, c=c: e.matmul(PS[0][:, c * TN:(c + 1) * TN], src[:, c * 128:(c + 1) * 128], IDN[0:TN, 0:TN], start=True, stop=True, is_transpose=True) for c in range(2)]),
                act(lambda e, i: e.activation(HT[:], PS[0][:, 0:2 * TN].rearrange("p (k n) -> p k n", k=2), ACT.Copy)),
                pe(*[lambda e, i, c=c: e.matmul(PS[1][0:TN, 0:CH], HT[:, c, :], Wm[:, c, 0:CH], start=(c == 0), stop=(c == 1)) for c in range(2)])]

    targets = [dma(lambda i: (SDI[:], at(A["sdr"], i))),
               dve(lambda e, i: e.tensor_copy(DF[:], SDI[:, 1:2])),
               dve(lambda e, i: e.tensor_scalar(DC[:], DF[:], float(N), None, op0=ALU.min)),
               dve(lambda e, i: e.tensor_copy(DI[:], DC[:]))]
    onehot = dve(lambda e, i: e.tensor_scalar(OHA[:], NIO[:], DF[:, 0:1], None, op0=ALU.is_equal))

    def aggregate(w):
        steps = []
        for t0 in range(0, NT, 8):
            ts = range(t0, min(t0 + 8, NT))
            steps.append(pe(*[lambda e, i, t=t: e.matmul(PS[t % 8][0:TN, 0:w], OHA[:, t * TN:(t + 1) * TN], GR[:, 0:w], start=True, stop=True) for t in ts]))
            steps.append(dve(*[lambda e, i, t=t: e.tensor_tensor(ACC[:, t, 0:w], ACC[:, t, 0:w], PS[t % 8][0:TN, 0:w], op=ALU.add) for t in ts]))
        return steps

    clear = dve(lambda e, i: e.memset(ACC[:], 0.0))
    keep = dma(lambda i: (ACCD.rearrange("t p c -> p t c"), ACC[:]))

    def weighted(table):
        S.once(clear)
        S.loop(NR, *targets, dma(lambda i: (EWC[:], at(A["ewr"], i))), onehot, gather(GR[:, 0:CH], table, SDI[:, 0:1]),
               dve(lambda e, i: e.tensor_scalar(GR[:, 0:CH], GR[:, 0:CH], EWC[:, 0:1], None, op0=ALU.mult)), *aggregate(CH))
        S.once(keep)

    def normed(src, out):
        return [dve(lambda e, i: e.tensor_scalar(SM[:, 1:2], SM[:, 0:1], -1.0 / CH, None, op0=ALU.mult)),
                dve(lambda e, i: e.tensor_scalar(t1_, src, SM[:, 1:2], None, op0=ALU.add)),
                act(lambda e, i: e.activation(t2_, t1_, ACT.Square, accum_out=SM[:, 2:3])),
                dve(lambda e, i: e.tensor_scalar(SM[:, 3:4], SM[:, 2:3], 1.0 / CH, EPS, op0=ALU.mult, op1=ALU.add)),
                act(lambda e, i: e.activation(SM[:, 4:5], SM[:, 3:4], ACT.Sqrt)),
                dve(lambda e, i: e.reciprocal(SM[:, 5:6], SM[:, 4:5])),
                dve(lambda e, i: e.tensor_scalar(out, t1_, SM[:, 5:6], None, op0=ALU.mult))]

    def logits(l, a, b, p, tmp, out):
        H = HS[l]
        return [dve(lambda e, i: e.tensor_tensor(tmp, a, b, op=ALU.add)),
                dve(lambda e, i: e.scalar_tensor_tensor(b, tmp, 0.2, tmp, op0=ALU.mult, op1=ALU.max)),
                dve(lambda e, i: e.tensor_tensor(tmp, b, ATG[l][0:p, :], op=ALU.mult)),
                dve(lambda e, i: e.tensor_reduce(out[:, 0:H], tmp.rearrange("p (h c) -> p h c", h=H), axis=AX.X, op=ALU.add))]

    def sides(l, src):
        return [*project(src, W[f"l{l}"]), act(lambda e, i: e.activation(t1_, PS[1][0:TN, 0:CH], ACT.Copy)),
                *project(src, W[f"r{l}"]), act(lambda e, i: e.activation(t2_, PS[1][0:TN, 0:CH], ACT.Copy)),
                dma(lambda i: (at(XLD[l], i), t1_), lambda i: (at(XRD[l][0:N].rearrange("(t p) c -> t p c", p=TN), i), t2_)),
                *logits(l, t1_, t2_, TN, y_, LST[:]),
                dma(lambda i: (at(LSD[l], i), LST[:]))]

    S.once(dve(*[lambda e, i, t=t: e.tensor_scalar(NIO[:, t * TN:(t + 1) * TN], IOTA[:, 0:TN], float(t * TN), None, op0=ALU.add) for t in range(NT)],
               *[lambda e, i, t=t: e.tensor_scalar(NID[:, t:t + 1], PIDX, float(t * TN), None, op0=ALU.add) for t in range(NT)],
               lambda e, i: e.memset(DGA[0][:], 0.0), lambda e, i: e.memset(LST[:], 0.0), lambda e, i: e.memset(ROWP[:], 0.0), lambda e, i: e.memset(BIGR[:], BIG)),
           dma(lambda i: (W["1"][:], A["W1"].rearrange("(k p) n -> p k n", p=128)), *[lambda i, l=l: (ATG[l][:], A[f"att{l + 1}"].broadcast_to([128, CH])) for l in range(2)],
               *[lambda i, l=l: (XRD[l][N:N + 1], ROWP[:]) for l in range(2)],
               *[lambda i, l=l: (MXD[l][N:N + 1], BIGR[:]) for l in range(2)]))

    S.loop(NR, *targets, dma(lambda i: (EWC[:], at(A["ewr"], i))), onehot,
           pe(*[lambda e, i, t=t: e.matmul(PS[0][0:TN, t:t + 1], OHA[:, t * TN:(t + 1) * TN], EWC[:], start=True, stop=True) for t in range(NT)]),
           dve(lambda e, i: e.tensor_tensor(DGA[0][:], DGA[0][:], PS[0][0:TN, 0:NT], op=ALU.add)))
    a, b, c, d = (x[:] for x in DGA)
    S.once(dve(lambda e, i: e.tensor_scalar(b, a, 1.0, None, op0=ALU.add)),
           dve(lambda e, i: e.tensor_scalar(c, b, 0.0, None, op0=ALU.is_gt)),
           dve(lambda e, i: e.tensor_tensor(d, b, c, op=ALU.mult)),
           dve(lambda e, i: e.scalar_tensor_tensor(b, c, -1.0, d, op0=ALU.mult, op1=ALU.add)),
           dve(lambda e, i: e.tensor_scalar(d, b, 1.0, None, op0=ALU.add)),
           act(lambda e, i: e.activation(b, d, ACT.Sqrt)),
           dve(lambda e, i: e.reciprocal(d, b)),
           dve(lambda e, i: e.tensor_tensor(DIS[:], d, c, op=ALU.mult)),
           pe(lambda e, i: e.matmul(PS[0][0:NT, 0:TN], DIS[:], IDN[0:TN, 0:TN], start=True, stop=True, is_transpose=True)),
           act(lambda e, i: e.activation(DIT[:], PS[0][0:NT, 0:TN], ACT.Copy)),
           dma(lambda i: (DISD.rearrange("t p c -> t (p c)"), DIT[:])))

    S.loop(NT, dma(lambda i: (x_, at(xv, i)), lambda i: (DSC[:], at(DISD, i))), *project(x_, W["1"]),
           act(lambda e, i: e.activation(y_, PS[1][0:TN, 0:CH], ACT.Copy, scale=DSC[:, 0:1])),
           dma(lambda i: (at(HPD[0], i), y_)))
    weighted(flat(HPD[0]))

    def summed(k):
        return [dma(lambda i: (AC[:], at(ACCD, i)), lambda i: (x_, at(HPD[k], i)), lambda i: (DSC[:], at(DISD, i))),
                dve(lambda e, i: e.tensor_tensor(z_, AC[:, 0:CH], x_, op=ALU.add)),
                dve(lambda e, i: e.scalar_tensor_tensor(y_, z_, DSC[:, 0:1], BB[k][:], op0=ALU.mult, op1=ALU.add))]

    S.loop(NT, *summed(0), dve(lambda e, i: e.scalar_tensor_tensor(z_, y_, 0.01, y_, op0=ALU.mult, op1=ALU.max)), *project(z_, W["2"]),
           act(lambda e, i: e.activation(y_, PS[1][0:TN, 0:CH], ACT.Copy, scale=DSC[:, 0:1])),
           dma(lambda i: (at(HPD[1], i), y_)))
    weighted(flat(HPD[1]))
    S.loop(NT, *summed(1), dma(lambda i: (x_, at(xv, i))),
           dve(lambda e, i: e.scalar_tensor_tensor(z_, y_, 1.0, x_, op0=ALU.mult, op1=ALU.add, accum_out=SM[:, 0:1])),
           *normed(z_, x_), dma(lambda i: (at(X1, i), x_)), *sides(0, x_))

    def layer(l):
        H = HS[l]
        C = CH // H
        hv = lambda v: v.rearrange("p (h c) -> p h c", h=H)
        gr, gx, gw = GR[:, 0:CH], GX[:], GW_[:]
        S.loop(NR, *targets, gather(gr, flat(XLD[l]), SDI[:, 0:1]), gather(gx, XRD[l], DI[:, 0:1]), *logits(l, gr, gx, 128, gw, LE[:]),
               pe(lambda e, i: e.matmul(PS[0][0:H, 0:128], LE[:, 0:H], IDN, start=True, stop=True, is_transpose=True)),
               act(lambda e, i: e.activation(LER[0:H, :], PS[0][0:H, 0:128], ACT.Copy)),
               dma(lambda i: (at(LGE[l], i), LE[:, 0:H]), lambda i: (at(LGR[l], i), LER[0:H, :])))
        S.once(dve(lambda e, i: e.memset(MXA[:], -BIG)))
        lb = LB[:, 0:CK * H * 128].rearrange("p (r h e) -> p r h e", r=CK, h=H)
        tmp = TMP[:, 0:CK * H * 128].rearrange("p (r h e) -> p r h e", r=CK, h=H)
        mk = MK[:].rearrange("p (r o e) -> p r o e", r=CK, o=1).broadcast_to([TN, CK, H, 128])
        largest = []
        for t in range(NT):
            largest += [dve(lambda e, i, t=t: e.tensor_scalar(MK[:], DBF[:], NID[:, t:t + 1], -BIG, op0=ALU.not_equal, op1=ALU.mult)),
                        dve(lambda e, i: e.tensor_tensor(tmp, lb, mk, op=ALU.add)),
                        dve(lambda e, i: e.tensor_reduce(MXT[:, 0:H], tmp.rearrange("p r h e -> p h r e"), axis=AX.XY, op=ALU.max)),
                        dve(lambda e, i, t=t: e.tensor_tensor(MXA[:, t, 0:H], MXA[:, t, 0:H], MXT[:, 0:H], op=ALU.max))]
        S.loop(NR // CK,
               dma(lambda i: (DBI[:], A["dr"][bass.ds(i, 1), :].broadcast_to([TN, CK * 128])),
                   lambda i: (LB[:, 0:CK * H * 128], LGR[l].rearrange("(n r) h e -> n (r h e)", r=CK)[bass.ds(i, 1), :].broadcast_to([TN, CK * H * 128]))),
               dve(lambda e, i: e.tensor_copy(DBF[:], DBI[:])), *largest)
        S.once(dma(lambda i: (LSA[:], LSD[l].rearrange("t p h -> p t h"))),
               dve(lambda e, i: e.tensor_tensor(MXA[:], MXA[:], LSA[:], op=ALU.max)),
               dma(lambda i: (MXD[l][0:N].rearrange("(t p) h -> p t h", p=TN), MXA[:])),
               clear)
        S.loop(NR, *targets, onehot, gather(gr, flat(XLD[l]), SDI[:, 0:1]), gather(MXG[:], MXD[l], DI[:, 0:1]), dma(lambda i: (LE[:, 0:H], at(LGE[l], i))),
               dve(lambda e, i: e.tensor_tensor(LX[:, 0:H], LE[:, 0:H], MXG[:, 0:H], op=ALU.subtract)),
               act(lambda e, i: e.activation(GR[:, CH:CH + H], LX[:, 0:H], ACT.Exp)),
               dve(lambda e, i: e.tensor_tensor(hv(gr), hv(gr), GR[:, CH:CH + H].unsqueeze(2).broadcast_to([128, H, C]), op=ALU.mult)),
               *aggregate(CH + H))
        S.once(keep)
        wide = lambda v: v.unsqueeze(2).broadcast_to([TN, H, C])
        out = [dma(lambda i: (AC[:], at(ACCD, i)), lambda i: (x_, at(XLD[l], i)), lambda i: (LST[:], at(LSD[l], i)),
                   lambda i: (MXT[:], at(MXD[l][0:N].rearrange("(t p) h -> t p h", p=TN), i))),
               dve(lambda e, i: e.tensor_tensor(SM[:, 0:H], LST[:, 0:H], MXT[:, 0:H], op=ALU.subtract)),
               act(lambda e, i: e.activation(SM[:, 4:4 + H], SM[:, 0:H], ACT.Exp)),
               dve(lambda e, i: e.tensor_tensor(SM[:, 0:H], SM[:, 4:4 + H], AC[:, CH:CH + H], op=ALU.add)),
               dve(lambda e, i: e.tensor_tensor(hv(y_), hv(x_), wide(SM[:, 4:4 + H]), op=ALU.mult)),
               dve(lambda e, i: e.reciprocal(LST[:, 0:H], SM[:, 0:H])),
               dve(lambda e, i: e.tensor_tensor(z_, y_, AC[:, 0:CH], op=ALU.add)),
               dve(lambda e, i: e.tensor_tensor(hv(y_), hv(z_), wide(LST[:, 0:H]), op=ALU.mult)),
               dve(lambda e, i: e.tensor_tensor(z_, y_, BB[2 + l][:], op=ALU.add))]
        if l == 0:
            out += [dve(lambda e, i: e.tensor_scalar(y_, z_, 0.0, None, op0=ALU.min)),
                    act(lambda e, i: e.activation(t1_, y_, ACT.Exp)),
                    dve(lambda e, i: e.scalar_tensor_tensor(y_, z_, 0.0, t1_, op0=ALU.max, op1=ALU.add)),
                    dve(lambda e, i: e.tensor_scalar(z_, y_, -1.0, None, op0=ALU.add)), *sides(1, z_)]
        else:
            out += [dma(lambda i: (x_, at(X1, i))),
                    dve(lambda e, i: e.scalar_tensor_tensor(y_, z_, 1.0, x_, op0=ALU.mult, op1=ALU.add, accum_out=SM[:, 0:1])),
                    *normed(y_, x_), dma(lambda i: (at(ov, i), x_))]
        S.loop(NT, *out)

    for l in range(2):
        layer(l)
    return S


def layouts(src, dst, ew, NT, E):
    N = NT * TN
    nb = -(-E // BLK)
    nr = nb + KP * ROW // BLK
    length = (nr + ROW // BLK) * BLK
    cw = -(-E // 128)
    length = max(length, 128 * cw + 1)
    length = -(-length // BLK) * BLK

    def padded(a, value):
        out = np.full(length, value, a.dtype)
        out[:E] = a
        return out

    def fill(a, value):
        out = np.full(-(-E // 512) * 512, value, a.dtype)
        out[:E] = a
        return out.reshape(-1, 128)

    s, d, w = padded(src, 0), padded(dst, N + 875), padded(ew, 0)
    rows = lambda a: [a.reshape(-1, BLK)[m:m + nr] for m in range(ROW // BLK)]
    return {
        "sd": np.ascontiguousarray(np.concatenate(rows(s) + rows(d), axis=1)),
        "ew": np.ascontiguousarray(np.concatenate(rows(w), axis=1)),
        "first": np.ascontiguousarray(d.reshape(-1, BLK)[:nb, 0][None]),
        "sdr": np.stack([fill(src, 0), fill(dst, N + 875)], axis=2),
        "ewr": fill(ew, 0)[:, :, None],
        "dr": fill(dst, N + 875).reshape(-1, 4 * 128),
        "dsort": np.ascontiguousarray(np.concatenate([d[:128 * cw].reshape(128, cw), d[cw:128 * cw + 1:cw][:, None]], axis=1)),
    }


def build(nc, A, NT, E, where):
    ctx, Q, FLAG, general = gnn_program(nc, A, NT, E, where)

    def emit(name, e):
        Q.emit(name, e)
        needed = e.value_load(FLAG[0:1, 0:1], min_val=0, max_val=1)
        with e.If(needed == 1):
            general.emit(name, e)

    with ctx:
        with nc.Block() as block:
            block.sync(lambda e: emit("sync", e))
            block.tensor(lambda e: emit("tensor", e))
            block.vector(lambda e: emit("vector", e))
            block.scalar(lambda e: emit("scalar", e))
            block.gpsimd(lambda e: emit("gpsimd", e))


def kernel(**inputs):
    import concourse.bacc as _bacc
    from concourse.bass_utils import run_bass_kernel_spmd as _run

    a = {k: np.asarray(v) for k, v in inputs.items()}
    NT, E = a["x"].shape[0] // TN, a["src"].shape[0]
    arrays = layouts(a["src"], a["dst"], a["edge_weight"], NT, E)
    arrays["x"] = a["x"]
    arrays["W1"], arrays["W2"] = a["L0_gnn_W1"], a["L0_gnn_W2"]
    for l in (1, 2):
        arrays[f"Wl{l}"], arrays[f"Wr{l}"] = a[f"L1_gnn_Wl{l}"], a[f"L1_gnn_Wr{l}"]
        arrays[f"att{l}"] = a[f"L1_gnn_att{l}"].reshape(1, CH)
        arrays[f"att{l}c"] = a[f"L1_gnn_att{l}"].reshape(2, 128).T
    for i, n in enumerate(("L0_gnn_b1", "L0_gnn_b2", "L1_gnn_b1", "L1_gnn_b2")):
        arrays[f"b{i + 1}"] = a[n].reshape(1, CH)
    arrays["const"], where = shape_constants(NT, E)
    arrays = {f"in_{k}": np.ascontiguousarray(v) for k, v in arrays.items()}

    nc = _bacc.Bacc("TRN2", target_bir_lowering=False, num_devices=1)
    A = {k[3:]: nc.dram_tensor(k, v.shape, mybir.dt.from_np(v.dtype), kind="ExternalInput").ap() for k, v in arrays.items()}
    A["out"] = nc.dram_tensor("out", (NT * TN, CH), F32, kind="ExternalOutput").ap()
    build(nc, A, NT, E, where)
    r = _run(nc, [arrays], core_ids=[0])
    return r.results[0]["out"]
```

```python
from contextlib import ExitStack

import numpy as np

import concourse.bass as bass
from concourse import mybir
from concourse.alu_op_type import AluOpType as ALU

ACT = mybir.ActivationFunctionType
AX = mybir.AxisListType
F32 = mybir.dt.float32
F32R = mybir.dt.float32r
BF16 = mybir.dt.bfloat16
I32 = mybir.dt.int32

TN = 125
CH = 256
GR = 5
GPT = TN // GR
BLK = 32
ROW = 256
KP = 17
MARGIN = 28
BIG = 2.0 ** 100
MAGIC = 12582912.0
EPS = 1.0e-5
LG = 1
DIS_AT = 21
X_FIRST = 2
AHEAD_AT = 16
AHEAD_BY = 2
POST_AT = (7, 15, 21)
ATTW_AT = 3
ROWS_FROM = 1
XBLK_AT = (2, 4, 6, 8, 10)
FIELDS_AT = (8, 11, 14, 17, 20)
NRING = 4
RP = 2 * KP
BL = 32
WIN = 62
WINS = (0, 31, 63)
CHUNKS = ((0, 4), (4, 8), (8, 12), (12, KP))
LAGC = 22
HOT_RATE = 3
HOT_AT = 4
LAST_RATE = 4
LAST_LAG = 1
LAST_BY = ("vsvgvg", "svsvgs")


class Counter:

    def __init__(self, handle):
        self.handle, self.value = handle, 0

    def raised(self, by):
        self.value += by
        return (self, self.value)


class Queues:

    def __init__(self, sem):
        self.lists = {n: [] for n in ("sync", "tensor", "vector", "scalar", "gpsimd")}
        self.done = {n: Counter(sem(f"{n}_done")) for n in ("tensor", "vector", "scalar", "gpsimd")}

    def put(self, engine, fn, after=(), counter=None, by=1):
        token = counter.raised(by) if counter else None
        self.lists[engine].append((fn, [a for a in after if a], counter, by))
        return token

    def pe(self, fn, after=(), last=False):
        return self.put("tensor", fn, after, self.done["tensor"] if last else None)

    def dve(self, fn, after=()):
        return self.put("vector", fn, after, self.done["vector"])

    def act(self, fn, after=()):
        return self.put("scalar", fn, after, self.done["scalar"])

    def pool(self, fn, after=()):
        return self.put("gpsimd", fn, after, self.done["gpsimd"])

    def dma(self, counter, out, in_, after=(), engine="sync"):
        return self.put(engine, lambda e: e.dma_start(out, in_), after, counter, 16)

    def emit(self, engine, e):
        seen = {}
        for fn, after, counter, by in self.lists[engine]:
            for c, value in after:
                if seen.get(c, 0) < value:
                    e.wait_ge(c.handle, value)
                    seen[c] = value
            i = fn(e) if fn else None
            if counter:
                i.then_inc(counter.handle, by)


def latest(tokens):
    top = {}
    for c, v in tokens:
        top[c] = max(v, top.get(c, 0))
    return list(top.items())


def place_in_tile(i):
    return 4 * (i % 4) + i // 4 if i < KP - 1 else i


def position(i, h):
    return BL * (i % 4) + 5 * h + i // 4


def reach(E, N):
    degree = max(E / N, 1.0)
    windows, blocks, allowed = [], [], []
    for i in range(KP):
        k = place_in_tile(i)
        spans = []
        for half in range(2):
            e0 = ROW * k + ROW // 2 * half
            lo, hi = (e0 - 2 * BLK) / degree, (e0 + ROW // 2) / degree
            slack = lambda n: 1.0 + 5.0 * np.sqrt(max(min(n, TN), 0.0) / degree)
            lo, hi = lo - slack(lo), hi + slack(hi)
            spans.append((min(max(lo, 0.0), TN - 1.0), min(max(hi, 0.0), TN - 1.0)))
        lo, hi = spans[0][0], spans[1][1]
        w = min(WINS, key=lambda w: max(w - lo, hi - (w + WIN - 1)))
        windows.append(w)
        for lo, hi in spans:
            b0, b1 = int(lo) // BL, int(hi) // BL
            blocks.append((b0, b1))
            allowed.append((max(b0 * BL, w), min((b1 + 1) * BL, w + WIN, TN)))
    return windows, blocks, allowed


def shape_constants(NT, E):
    NJ = NT // 5
    p = np.arange(128, dtype=np.float32)[:, None]
    R = 5 * KP
    rows = np.array([place_in_tile(m % KP) for m in range(128)], np.float32)[:, None]
    number = {place_in_tile(i): i for i in range(KP)}
    windows, blocks, allowed = reach(E, NT * TN)
    parts = {}
    parts["iota"] = np.broadcast_to(np.arange(128, dtype=np.float32), (128, 128))
    parts["ident"] = np.eye(128, dtype=np.float32)
    parts["pidx"] = p
    parts["pwin"] = p % WIN
    parts["v5"] = GR * (np.arange(NJ, dtype=np.float32)[None] * TN + p)
    parts["v125"] = TN * (np.arange(NJ, dtype=np.float32)[None] * 5 + np.floor(p / KP))
    parts["k8"] = (ROW // BLK) * rows
    parts["win"] = np.array([windows[m % KP] for m in range(128)], np.float32)[:, None]
    parts["allow"] = np.array([allowed[2 * (m % KP)] + allowed[2 * (m % KP) + 1] for m in range(128)], np.float32)
    sel = np.zeros((128, R), np.float32)
    for m in range(R):
        sel[GPT * (m // KP), m] = 1
    parts["sel85"] = sel
    sh, order = np.zeros((128, R), np.float32), np.zeros((128, R), np.float32)
    for m in range(R):
        k = place_in_tile(m % KP)
        order[m, m - m % KP + k] = 1
        if k != KP - 1:
            sh[m - m % KP + number[k + 1], m] = 1
    parts["sh85"], parts["order"] = sh, order
    parts["k16"] = -(rows == KP - 1).astype(np.float32)
    s2, hm = np.zeros((128, 2 * KP), np.float32), np.zeros((128, 4), np.float32)
    for i in range(KP):
        for h in range(4):
            s2[position(i, h), place_in_tile(i)] = s2[position(i, h), KP + place_in_tile(i)] = 1
            hm[position(i, h), h] = 1
    parts["sel2"], parts["hm"] = s2, hm
    hmt = np.zeros((128, 128), np.float32)
    hmt[:4, :] = hm.T
    parts["hmt"] = hmt
    mb = np.zeros((128, 2), np.float32)
    mb[:64, 0] = mb[64:, 1] = 1
    parts["mb"] = mb
    parts["group"] = (p % GPT == np.arange(GPT)).astype(np.float32)
    parts["tile"] = (p // GPT == np.arange(5)).astype(np.float32)
    parts["ones"] = np.ones((128, 1), np.float32)
    at, where = 0, {}
    for k, v in parts.items():
        where[k] = (at, at + v.shape[1])
        at += v.shape[1]
    return np.ascontiguousarray(np.concatenate(list(parts.values()), axis=1).astype(np.float32)), where


def gnn_program(nc, A, NT, E, where):
    NJ = NT // 5
    N = NT * TN
    R = 5 * KP
    NROW = NT * KP
    FROM = (0, int((128 - BLK - MARGIN) * N / E))
    NB = A["first"].shape[1]
    CW = A["dsort"].shape[1] - 1
    NP = NT * KP
    SC = NT * TN

    ctx = ExitStack()
    sb = lambda name, shape, dt=F32: ctx.enter_context(nc.sbuf_tensor(name, shape, dt))
    sem = lambda name: ctx.enter_context(nc.semaphore(name))
    dram = lambda name, shape, dt=F32: nc.dram_tensor(name, shape, dt, kind="Internal").ap()
    Q = Queues(sem)
    cnt = lambda name: Counter(sem(name))

    AD = dram("a_d", (NT, TN, SC))
    X1D = dram("x1_d", (N, CH))
    TAB = [dram("tab1_d", (N, CH + 4)), dram("tab2_d", (N, CH + 1))]
    XRD = [dram(f"xr{l}_d", (NT, TN, 2 * CH)) for l in range(2)]
    CSD = dram("cs_d", (NJ, R, 2))
    M3D = dram("m3_d", (NROW + 3, 772), BF16)
    DLBD = dram("dlb_d", (NROW, ROW), BF16)

    PS = [ctx.enter_context(nc.psum_tensor(f"bank{i}", [128, 512], F32)) for i in range(8)]

    CON = sb("con", [128, A["const"].shape[1]])
    K = lambda name, p=128: CON[0:p, where[name][0]:where[name][1]]
    IOTA = K("iota")[:, 0:TN + 1]
    IDN = K("ident")
    W2S = sb("w2s", [128, 2, CH])
    HS = [4, 1]
    WL = [sb(f"wl{l}", [128, 2, CH + HS[l]]) for l in range(2)]
    WR = [sb(f"wr{l}", [128, 2, CH + HS[l]]) for l in range(2)]
    BB = [sb(f"bb{i}", [TN, CH]) for i in range(4)]
    ATB = [sb(f"atb{l}", [128, CH]) for l in range(2)]
    ATC = [sb(f"atc{l}", [128, 2]) for l in range(2)]
    AZ = [sb(f"az{l}", [128, 2, 4 + BL]) for l in range(2)]
    ARN = [sb(f"arn{l}", [TN, NT, HS[l]]) for l in range(2)]
    LSF = [sb(f"lsf{l}", [TN, NT, HS[l]]) for l in range(2)]
    SRCI = sb("srci", [128, NJ, 2, R], I32)
    DLS = sb("dls", [128, NJ, 2, R])
    LAST = sb("last", [128, NJ, 2, R])
    CRF = sb("crf", [4, 1 + NROW])
    AFW = sb("afw", [4, NROW])
    ARV = sb("arv", [4, NROW])
    DIS = sb("dis", [TN, NT])
    FLAG = sb("flag", [1, 4], I32)

    d_con = cnt("d_con")
    t_con = Q.dma(d_con, CON[:], A["const"])

    def loaded(counter, out, in_, after=(), engine="sync"):
        return Q.dma(counter, out, in_, after, engine)

    gcn = ExitStack()
    sg = lambda name, shape, dt=F32: gcn.enter_context(nc.sbuf_tensor(name, shape, dt))
    HP = [sg(f"hp{i}", [TN, NT, CH]) for i in range(2)]
    RING = sg("ring", [128, NRING, SC])
    FLD = sg("fld", [128, NJ, 2, 3, TN])
    early = HP[1][:].rearrange("p t c -> p (t c)")
    GSD = early[:, 0:2 * ROW * NJ].bitcast(I32).rearrange("p (j c) -> p j c", j=NJ)
    GEW = early[:, 2 * ROW * NJ:3 * ROW * NJ].rearrange("p (j c) -> p j c", j=NJ)
    XST = [sg(f"xst{i}", [TN, CH]) for i in range(3)]
    OHW = 12
    OHS = sg("ohs", [128, OHW, 2, TN + 1])
    TSD = FLD[:].rearrange("p j h f n -> p (j h f n)")[0:R, 0:2 * ROW * NJ].bitcast(I32).rearrange("p (j c) -> p j c", j=NJ)
    W1S = sg("w1s", [128, 2, CH])
    CNT = sg("cnt", [TN, NJ])
    CNB = sg("cnb", [TN, NJ])
    STF = sg("stf", [TN, NJ])
    STI = sg("sti", [TN, NJ], I32)
    IXF = sg("ixf", [R, NJ])
    IXI = sg("ixi", [R, NJ], I32)
    GF = [sg(f"gf{i}", [TN, ROW]) for i in range(6)]
    KS = [[sg(f"ks{i}_{j}", [TN, ROW]) for i in range(3)] for j in range(2)]
    DEG = sg("deg", [TN, NJ, GR])
    VAL = sg("val", [TN, NJ])
    DG = [sg(f"dg{i}", [TN, NT]) for i in range(3)]
    HT = [sg(f"ht{i}", [128, 2, TN]) for i in range(2)]
    ZB = [sg(f"zb{i}", [TN, CH]) for i in range(4)]
    XL = [sg(f"xl{i}", [TN, CH + 4]) for i in range(2)]
    SMALL = [sg(f"small{i}", [TN, 16]) for i in range(2)]
    XRS = [sg(f"xrs{i}", [TN, 2 * CH]) for i in range(2)]
    PF = [OHS[:].rearrange("p a b c -> p (a b c)")[0:R, i * ROW:(i + 1) * ROW] for i in range(7)]
    PB = sg("pb", [R, ROW], BF16)
    PM = sg("pm", [R, 772], BF16)
    LF = sg("lf", [R, NJ, ROW])
    FL = [sg(f"fl{i}", [R, NJ]) for i in range(5)]
    CS = sg("cs", [R, NJ, 2])
    CSB = sg("csb", [4, NROW, 2])
    VALT = sg("valt", [R, 2 * NJ])
    CSP = sg("csp", [R, NJ, 2])
    STAT = sg("stat", [128, 4])
    SUMS = sg("sums", [1, 8])
    DSI = RING[:, 1, SC - CW - 1:SC].bitcast(I32)
    ATW = [sg("atw0", [128, 2, CH])]
    ATR = sg("atr", [128, 2, 4])

    ring_flat = RING[:].rearrange("p r c -> p (r c)")
    FIRST = ring_flat[0:TN, 0:NB].bitcast(I32)
    d_first, d_sort, d_w1, d_w2, d_b, d_wl, d_at = (cnt(n) for n in ("d_first", "d_sort", "d_w1", "d_w2", "d_b", "d_wl", "d_at"))
    t_first = loaded(d_first, FIRST, A["first"][0:1, :].broadcast_to([TN, NB]), engine="scalar")
    t_w1 = loaded(d_w1, W1S[:], A["W1"].rearrange("(k p) n -> p k n", p=128))
    d_x = [cnt(f"d_x{i}") for i in range(NJ)]
    t_xin = []

    def load_x_early(j, after):
        t_xin.append(loaded(d_x[j], HP[0][:, 5 * j:5 * j + 5, :], A["x"][5 * j * TN:5 * (j + 1) * TN, :].rearrange("(t p) c -> p t c", p=TN), after))

    for j in range(min(X_FIRST, NJ)):
        load_x_early(j, [t_first])

    junk = OHS[:].rearrange("p a b c -> p (a b c)").bitcast(BF16)
    junk_act = FLD[:].rearrange("p j h f n -> p (j h f n)").bitcast(BF16)
    t_nv = Q.dve(lambda e: e.tensor_scalar(CNB[:], K("v5", TN), -1.0, 0.5, op0=ALU.mult, op1=ALU.add), [t_con])
    t_cnt, t_cnta, t_sti = None, None, [None] * NJ
    for j in range(1, NJ, 2):
        t_cnta = Q.act(lambda e, j=j: e.activation(junk_act[0:TN, 0:NB], FIRST, ACT.Sign, bias=CNB[:, j:j + 1], accum_out=CNT[:, j:j + 1]), [t_first, t_nv, t_cnta])
        t_sti[j] = t_cnta
    for j in range(0, NJ, 2):
        t_cnt = Q.dve(lambda e, j=j: e.tensor_scalar(junk[0:TN, 0:NB], FIRST, K("v5", TN)[:, j:j + 1], None, op0=ALU.is_lt, op1=ALU.add, accum_out=CNT[:, j:j + 1]), [t_first, t_con, t_cnt])
        t_stf = Q.dve(lambda e, j=j: e.tensor_scalar(STF[:, j:j + 1], CNT[:, j:j + 1], -1.0, 0.0, op0=ALU.add, op1=ALU.max), [t_cnt])
        t_sti[j] = Q.dve(lambda e, j=j: e.tensor_copy(STI[:, j:j + 1], STF[:, j:j + 1]), [t_stf])
        if j + 1 < NJ:
            t_1 = Q.dve(lambda e, j=j + 1: e.tensor_scalar(STF[:, j:j + 1], CNT[:, j:j + 1], -0.5, NB / 2 - 1.0, op0=ALU.mult, op1=ALU.add), [t_sti[j + 1]])
            t_stf = Q.dve(lambda e, j=j + 1: e.tensor_scalar(STF[:, j:j + 1], STF[:, j:j + 1], 0.0, None, op0=ALU.max), [t_1])
            t_sti[j + 1] = Q.dve(lambda e, j=j + 1: e.tensor_copy(STI[:, j:j + 1], STF[:, j:j + 1]), [t_stf])
    t_counted = [t_cnt, t_cnta]
    for j in range(X_FIRST, NJ):
        load_x_early(j, [t_sti[min(X_FIRST, NJ - 1)]])
    t_dsi = loaded(d_sort, DSI, A["dsort"])

    off = lambda ap: bass.IndirectOffsetOnAxis(ap=ap, axis=0)
    t_root = Q.act(lambda e: e.activation(DG[0][:, 0:1], K("ones", TN), ACT.Sqrt), [t_con])
    d_gsd, d_gew, d_tsd = ([cnt(f"{n}{j}") for j in range(NJ)] for n in ("d_gsd", "d_gew", "d_tsd"))
    t_gsd = []
    for j in range(NJ):
        t_1 = Q.put("gpsimd", lambda e, j=j: e.indirect_dma_start(out=GSD[:, j, :], out_offset=None, in_=A["sd"], in_offset=off(STI[:, j:j + 1])), [t_sti[j]], d_gsd[j], 16)
        t_2 = Q.put("gpsimd", lambda e, j=j: e.indirect_dma_start(out=GEW[:, j, :], out_offset=None, in_=A["ew"], in_offset=off(STI[:, j:j + 1])), [], d_gew[j], 16)
        t_gsd.append([t_1, t_2])

    t_blk = []

    def source_blocks(j):
        b = XB[j][:]
        t_1 = Q.act(lambda e: e.activation(b, GSD[:, j, 0:ROW], ACT.Copy, scale=1.0 / TN, bias=0.5 / TN - 0.5), t_gsd[j])
        t_2 = Q.act(lambda e: e.activation(b, b, ACT.Copy, bias=MAGIC), [t_1])
        t_blk.append(Q.act(lambda e: e.activation(b, b, ACT.Copy, bias=-MAGIC), [t_2]))

    XB = [XST[0], XST[1], XST[2], ZB[0], ZB[1]]

    t_fld = [None] * NJ
    t_deg = [None] * NJ
    t_ksfree = [None, None]

    def fields(j):
        src, dst, ew = GSD[:, j, 0:ROW], GSD[:, j, ROW:2 * ROW], GEW[:, j, :]
        slo, key, eww = KS[j % 2]
        drel, ge, one = (GF[i][:] for i in (0, 2, 4))
        blk = XB[j][:]
        prev = [t_fields[-1]] if t_fields else []
        t1 = Q.dve(lambda e: e.tensor_scalar(drel, dst, K("v5", TN)[:, j:j + 1], None, op0=ALU.subtract), t_gsd[j] + [t_con] + prev)
        t7 = Q.dve(lambda e: e.scalar_tensor_tensor(slo[:], blk, -float(TN), src, op0=ALU.mult, op1=ALU.add), [t_blk[j], t_ksfree[j % 2]])
        for half in range(2):
            t4 = Q.dve(lambda e, half=half: e.tensor_scalar(ge[:, half * 128:(half + 1) * 128], drel[:, half * 128:(half + 1) * 128], float(FROM[half]), None, op0=ALU.is_ge), [t1])
        t8 = Q.dve(lambda e: e.scalar_tensor_tensor(key[:], drel, float(NT), blk, op0=ALU.mult, op1=ALU.add))
        t5 = Q.dve(lambda e: e.scalar_tensor_tensor(one, drel, float(GR), ge, op0=ALU.is_lt, op1=ALU.mult, accum_out=VAL[:, j:j + 1]), [t4])
        t6 = Q.dve(lambda e: e.tensor_tensor(eww[:], one, ew, op=ALU.mult), [t5])
        t_fields.append(t6)
        return t6, t7, t6

    t_fields = []
    early_read = []

    def degrees(j, t6):
        eww, drel = KS[j % 2][2], GF[0]
        for r in range(GR):
            t_deg[j] = Q.dve(lambda e, r=r: e.scalar_tensor_tensor(GF[1 + r][:], drel[:], float(r), eww[:], op0=ALU.is_equal, op1=ALU.mult, accum_out=DEG[:, j, r:r + 1]), [t6])
        t_fields.append(t_deg[j])

    def field_transposes(j, t8):
        for half in range(2):
            for f in range(3):
                tp = Q.pe(lambda e, f=f, half=half: e.matmul(PS[7][:, f * TN:(f + 1) * TN], KS[j % 2][f][:, half * 128:(half + 1) * 128], IDN[0:TN, 0:TN], start=True, stop=True, is_transpose=True), [t8, t_fldfree[0]], last=(f == 2))
            t_fldfree[0] = Q.act(lambda e, half=half: e.activation(FLD[:, j, half, :, :], PS[7][:, 0:3 * TN].rearrange("p (f n) -> p f n", f=3), ACT.Copy), [tp])
        t_fld[j] = t_fldfree[0]
        t_ksfree[j % 2] = tp

    SPR = [x[0:TN, k, :] for x in HT for k in range(2)] + [ZB[2][:, 0:TN]]
    t_spread = []

    def spread(j):
        t_spread.append(Q.dve(lambda e: e.tensor_tensor(SPR[j].rearrange("p (g r) -> p g r", r=GR), K("group", TN).unsqueeze(2).broadcast_to([TN, GPT, GR]), DEG[:, j, :].unsqueeze(1).broadcast_to([TN, GPT, GR]), op=ALU.mult), [t_deg[j]]))

    def inverse_roots():
        for j in range(NJ):
            tp = Q.pe(lambda e, j=j: e.matmul(PS[7][0:TN, 5 * j:5 * j + 5], SPR[j], K("tile", TN), start=True, stop=True), [t_spread[j], t_fldfree[0]], last=(j == NJ - 1))
        v = PS[7][0:TN, 0:NT]
        t1 = Q.dve(lambda e: e.tensor_scalar(DG[0][:], v, 1.0, None, op0=ALU.add), [tp, t_root])
        t2 = Q.dve(lambda e: e.tensor_scalar(DG[1][:], v, 1.0, 0.0, op0=ALU.add, op1=ALU.is_le))
        t_fldfree[0] = t2
        t3 = Q.dve(lambda e: e.scalar_tensor_tensor(DG[2][:], DG[0][:], 0.0, DG[1][:], op0=ALU.max, op1=ALU.add), [t2])
        t4 = Q.act(lambda e: e.activation(DG[1][:], DG[2][:], ACT.Sqrt), [t3])
        t5 = Q.dve(lambda e: e.reciprocal(DG[2][:], DG[1][:]), [t4])
        return Q.dve(lambda e: e.scalar_tensor_tensor(DIS[:], DG[0][:], 0.0, DG[2][:], op0=ALU.is_gt, op1=ALU.mult), [t5])

    t_fldfree = [None]

    xTv = ring_flat[:, (NRING - 2) * SC:(NRING - 2) * SC + 2 * N].rearrange("p (k n) -> p k n", k=2)
    t_ptfree, t_hpfree = [None, None], [None, None]
    t_hp = [[None] * NT for _ in range(2)]
    t_raw, t_xtw, t_dis = [], [], None
    ahead = [0]
    build_banks = (0, 1, 2)
    t_bank = [None] * 3
    t_oh = [None] * OHW
    ring_free = [[] for _ in range(NRING)]
    t_at_tile = [None] * NT
    quart = [(q * 4, min(4, GPT - q * 4)) for q in range((GPT + 3) // 4)]
    slot_no = [0]
    bank_no = [0]
    d_ad = [cnt(f"d_ad{i}") for i in range(NRING)]

    def build_group(t, gg):
        g0, ng = quart[gg // 4]
        gi, g = gg - g0, t * GPT + gg
        if gi == 0:
            bank_no[0] += 1
        bk = bank_no[0] % 3
        bank = PS[build_banks[bk]]
        j, p = g // TN, g % TN
        for half in range(2):
            o = slot_no[0] % OHW
            slot_no[0] += 1
            put = Q.pool if half else Q.dve
            c0, c1 = FROM[half] * NT, GR * NT
            t1 = put(lambda e, half=half, o=o: e.tensor_scalar(OHS[:, o, 0, :], IOTA, FLD[:, j, half, 0, p:p + 1], None, op0=ALU.is_equal), [t_fld[j], t_oh[o]])
            t2 = Q.dve(lambda e, half=half, o=o, c0=c0: e.tensor_scalar(OHS[:, o, 1, 0:c1 - c0], IOTA[:, c0:c1], FLD[:, j, half, 1, p:p + 1], FLD[:, j, half, 2, p:p + 1], op0=ALU.is_equal, op1=ALU.mult), [t_fld[j], t_oh[o]])
            tm = Q.pe(lambda e, half=half, o=o, c0=c0: e.matmul(bank[0:TN, gi * TN + c0:gi * TN + c1], OHS[:, o, 0, 0:TN], OHS[:, o, 1, 0:c1 - c0], start=(half == 0), stop=(half == 1), skip_group_check=True), [t1, t2, t_bank[bk]], last=True)
            t_oh[o] = tm
        if gi < ng - 1:
            return
        r = t % NRING
        dst = RING[0:TN, r, :].rearrange("p (s g d) -> p g s d", s=NT, g=GPT)[:, g0:g0 + ng, :, :]
        src = bank[0:TN, 0:ng * TN].rearrange("p (g c) -> p g c", g=ng)[:, :, 0:NT * GR].rearrange("p g (d s) -> p g s d", d=GR)
        alias = t_counted if r == 0 else t_counted + [t_uns] if r == 1 else [t_xt_done]
        t_at_tile[t] = t_bank[bk] = Q.act(lambda e: e.activation(dst, src, ACT.Copy), [tm] + ring_free[r] + alias)

    for t in range(NT + 1):
        if t < NT:
            bank = PS[5 + t % 2]
            for c in range(2):
                tt = Q.pe(lambda e, t=t, c=c, bank=bank: e.matmul(bank[:, c * TN:(c + 1) * TN], HP[0][:, t, c * 128:(c + 1) * 128], IDN[0:TN, 0:TN], start=True, stop=True, is_transpose=True), [t_xin[t // 5], t_con, t_ptfree[t % 2]], last=(c == 1))
            t_ptfree[t % 2] = Q.act(lambda e, t=t, bank=bank: e.activation(xTv[:, :, t * TN:(t + 1) * TN], bank[:, 0:2 * TN].rearrange("p (k n) -> p k n", k=2), ACT.Copy), [tt])
            t_xtw.append(t_ptfree[t % 2])
        if t:
            u = t - 1
            bank = PS[3 + u % 2]
            for c in range(2):
                tm = Q.pe(lambda e, u=u, c=c, bank=bank: e.matmul(bank[0:TN, 0:CH], xTv[:, c, u * TN:(u + 1) * TN], W1S[:, c, :], start=(c == 0), stop=(c == 1)), [t_xtw[u], t_w1, t_hpfree[u % 2]], last=(c == 1))
            if t_dis is None:
                t_hpfree[u % 2] = Q.act(lambda e, u=u, bank=bank: e.activation(HP[0][:, u, :], bank[0:TN, 0:CH], ACT.Copy), [tm])
            else:
                t_hp[0][u] = t_hpfree[u % 2] = Q.act(lambda e, u=u, bank=bank: e.activation(HP[0][:, u, :], bank[0:TN, 0:CH], ACT.Copy, scale=DIS[:, u:u + 1]), [tm, t_dis])
            t_raw.append(t_hpfree[u % 2])
        for j in range(NJ):
            if t == min(XBLK_AT[j], NT):
                source_blocks(j)
            if t == min(FIELDS_AT[j], NT):
                t6, _, t8 = fields(j)
                degrees(j, t6)
                field_transposes(j, t8)
                early_read.append(t_deg[j])
                spread(j)
        if t == min(DIS_AT, NT):
            t_dis = inverse_roots()
        if t >= AHEAD_AT and t % AHEAD_BY == 0 and NT >= 10:
            build_group(0, ahead[0])
            ahead[0] += 1
    t_xt_done = t_raw[-1]
    for t in range(NT):
        if t_hp[0][t] is None:
            t_hp[0][t] = Q.act(lambda e, t=t: e.activation(HP[0][:, t, :], HP[0][:, t, :], ACT.Copy, scale=DIS[:, t:t + 1]), [t_dis, t_raw[t]])

    t_b = None
    for i, n in enumerate(("b1", "b2", "b3", "b4")):
        t_b = loaded(d_b, BB[i][:], A[n].broadcast_to([TN, CH]))
    t_w2 = loaded(d_w2, W2S[:], A["W2"].rearrange("(k p) n -> p k n", p=128))
    for l in range(2):
        loaded(d_wl, WL[l][:, :, 0:CH], A[f"Wl{l + 1}"].rearrange("(k p) n -> p k n", p=128))
        t_wl = loaded(d_wl, WR[l][:, :, 0:CH], A[f"Wr{l + 1}"].rearrange("(k p) n -> p k n", p=128))
        loaded(d_at, ATB[l][:], A[f"att{l + 1}"].broadcast_to([128, CH]))
        t_at = loaded(d_at, ATC[l][:], A[f"att{l + 1}c"])

    t_acc = [None, None]

    def apply_part(t, s0, s1, layer, acc, first_after):
        bank = PS[3 + acc]
        tm = None
        for s in range(s0, s1):
            tm = Q.pe(lambda e, s=s: e.matmul(bank[0:TN, 0:CH], RING[0:TN, t % NRING, s * TN:(s + 1) * TN], HP[layer][:, s, :], start=(s == 0), stop=(s == NT - 1)), [t_hp[layer][s]] + first_after, last=(s == NT - 1))
        return tm

    t_z = [None] * 4
    t_ht = [None, None]
    t_pt = [None]
    t_pm = [None]

    def post1_vec(t, tm, acc):
        z, h = ZB[0], ZB[1]
        t1 = Q.dve(lambda e: e.tensor_tensor(z[:], PS[3 + acc][0:TN, 0:CH], HP[0][:, t, :], op=ALU.add), [tm, t_z[0]])
        t_acc[acc] = t1
        t2 = Q.dve(lambda e: e.scalar_tensor_tensor(z[:], z[:], DIS[:, t:t + 1], BB[0][:], op0=ALU.mult, op1=ALU.add), [t1, t_b])
        t3 = Q.dve(lambda e: e.scalar_tensor_tensor(h[:], z[:], 0.01, z[:], op0=ALU.mult, op1=ALU.max), [t2, t_z[1]])
        t_z[0] = t3
        return t3

    def transposes(src, t_src, k):
        for c in range(2):
            tp = Q.pe(lambda e, c=c: e.matmul(PS[5][:, c * TN:(c + 1) * TN], src[:, c * 128:(c + 1) * 128], IDN[0:TN, 0:TN], start=True, stop=True, is_transpose=True), [t_src, t_pt[0]], last=(c == 1))
        te = Q.act(lambda e: e.activation(HT[k][:], PS[5][:, 0:2 * TN].rearrange("p (k n) -> p k n", k=2), ACT.Copy), [tp, t_ht[k]])
        t_pt[0] = te
        return tp, te

    def post1_mm(t, te, k):
        for c in range(2):
            tm = Q.pe(lambda e, c=c: e.matmul(PS[6][0:TN, 0:CH], HT[k][:, c, :], W2S[:, c, :], start=(c == 0), stop=(c == 1)), [te, t_w2, t_pm[0]], last=(c == 1))
        t_ht[k] = tm
        tv = Q.act(lambda e: e.activation(HP[1][:, t, :], PS[6][0:TN, 0:CH], ACT.Copy, scale=DIS[:, t:t + 1]), [tm] + early_read)
        t_pm[0] = tv
        t_hp[1][t] = tv

    t_row = [None] * NJ
    d_rows = cnt("d_rows")
    t_pfree = [[], []]
    t_rb = [None]

    rows, chains = {}, []

    def rows_of_tiles(jj):
        src, dst = TSD[:, jj, 0:ROW], TSD[:, jj, ROW:2 * ROW]
        df, sf, dl, eq, p1, p2, ge = (x[:, :] for x in PF)
        a = t_pfree[0] + [t_pad]
        t1 = Q.pool(lambda e: e.tensor_copy(df, dst), [t_tsd[jj]] + a)
        yield
        t2 = Q.pool(lambda e: e.tensor_copy(sf, src), a)
        yield
        t3 = Q.pool(lambda e: e.tensor_scalar(dl, df, K("v125", R)[:, jj:jj + 1], None, op0=ALU.subtract), [t1, t_con])
        yield
        t4 = Q.pool(lambda e: e.tensor_tensor(ge[:, 0:ROW - 1], df[:, 1:ROW], df[:, 0:ROW - 1], op=ALU.subtract))
        yield
        t5 = Q.pool(lambda e: e.tensor_scalar(p1, df, df[:, 0:1], BIG, op0=ALU.is_equal, op1=ALU.mult))
        yield
        t6 = Q.pool(lambda e: e.tensor_scalar(p2, df, df[:, ROW - 1:ROW], BIG, op0=ALU.is_equal, op1=ALU.mult))
        yield
        t7 = Q.pool(lambda e: e.tensor_scalar(PB[:], dl, K("win", R), None, op0=ALU.subtract), [t3])
        yield
        t8 = Q.pool(lambda e: e.tensor_scalar(eq[:, 0:ROW - 1], ge[:, 0:ROW - 1], 0.0, BIG, op0=ALU.is_equal, op1=ALU.mult), [t4])
        yield
        t10 = Q.pool(lambda e: e.tensor_scalar(PM[:, ROW + 1:2 * ROW + 1], p1, BIG, None, op0=ALU.subtract), [t5])
        yield
        t11 = Q.pool(lambda e: e.tensor_scalar(PM[:, 2 * ROW + 1:3 * ROW + 1], p2, BIG, None, op0=ALU.subtract), [t6])
        yield
        t8b = Q.pool(lambda e: e.tensor_scalar(PM[:, 1:ROW], eq[:, 0:ROW - 1], BIG, None, op0=ALU.subtract), [t8])
        yield
        t9 = Q.pool(lambda e: e.tensor_scalar(LF[:, jj, 0:ROW - 1], eq[:, 0:ROW - 1], -1.0 / BIG, 1.0, op0=ALU.mult, op1=ALU.add))
        yield
        t12 = Q.pool(lambda e: e.tensor_copy(FL[0][:, jj:jj + 1], df[:, 0:1]))
        yield
        t13 = Q.pool(lambda e: e.tensor_copy(FL[1][:, jj:jj + 1], df[:, ROW - 1:ROW]))
        yield
        for half in range(2):
            t14 = Q.pool(lambda e, half=half: e.tensor_scalar(ge[:, half * 128:(half + 1) * 128], dl[:, half * 128:(half + 1) * 128], K("allow", R)[:, 2 * half:2 * half + 1], None, op0=ALU.is_ge), [t3])
        yield
        t_row[jj] = t14
        rows[jj] = (df, sf, dl, ge, t14)

    def columns_of_tiles(jj, df, sf, dl, ge, t14):
        for half in range(2):
            tv = Q.dve(lambda e, half=half: e.scalar_tensor_tensor(PX[0:R, half * 128:(half + 1) * 128], dl[:, half * 128:(half + 1) * 128], K("allow", R)[:, 2 * half + 1:2 * half + 2], ge[:, half * 128:(half + 1) * 128], op0=ALU.is_lt, op1=ALU.mult, accum_out=VALT[:, 2 * jj + half:2 * jj + half + 1]), [t14, t_fields[-1]] + t_pfree[1])
        td = Q.dma(d_rows, DLBD[jj * R:(jj + 1) * R, :], PB[:], [t14, t_pm0])
        td = Q.dma(d_rows, M3D[jj * R:(jj + 1) * R, :], PM[:], [t14])
        for half in range(2):
            for f, x in ((0, sf), (1, dl)):
                tp = Q.pe(lambda e, x=x, f=f, half=half: e.matmul(PS[0][:, (half * 2 + f) * R:(half * 2 + f + 1) * R], x[:, half * 128:(half + 1) * 128], IDN[0:R, 0:R], start=True, stop=True, is_transpose=True), [t14, t_rb[0]], last=(half == 1 and f == 1))
        v = PS[0][:, 0:4 * R].rearrange("p (h f n) -> p h f n", h=2, f=2)
        te1 = Q.dve(lambda e: e.tensor_copy(SRCI[:, jj, :, :], v[:, :, 0, :]), [tp])
        te2 = Q.dve(lambda e: e.tensor_copy(DLS[:, jj, :, :], v[:, :, 1, :]))
        t_rb[0] = te2
        t_pfree[0] = [tp, tv, td]
        t_pfree[1] = [tv]
        return te2

    def idle(n):
        for _ in range(n):
            yield

    def chains_of_rows():
        tp = Q.pe(lambda e: e.matmul(PS[0][0:R, 0:NJ], K("sh85", R), FL[0][:], start=True, stop=True), [t_row[-1], t_rb[0]], last=True)
        yield
        t1 = Q.dve(lambda e: e.tensor_scalar(FL[2][:], PS[0][0:R, 0:NJ], K("k16", R), None, op0=ALU.add), [tp])
        t2 = Q.dve(lambda e: e.tensor_tensor(FL[3][:], FL[0][:], FL[1][:], op=ALU.is_equal))
        t3 = Q.dve(lambda e: e.tensor_tensor(FL[4][:], FL[2][:], FL[1][:], op=ALU.is_equal), [t1])
        t4 = Q.dve(lambda e: e.tensor_scalar(CS[:, :, 0], FL[3][:], 1.0, BIG, op0=ALU.subtract, op1=ALU.mult), [t2])
        t5 = Q.dve(lambda e: e.tensor_scalar(CS[:, :, 1], FL[4][:], 1.0, BIG, op0=ALU.subtract, op1=ALU.mult), [t3])
        t6 = Q.dve(lambda e: e.tensor_scalar(LF[:, :, ROW - 1], FL[4][:], -1.0, 1.0, op0=ALU.mult, op1=ALU.add), [t3])
        yield
        yield
        d_cs = cnt("d_cs")
        yield from idle(6)
        tq = Q.pe(lambda e: e.matmul(PS[0][0:R, 0:2 * NJ], K("order", R), CS[:].rearrange("p j c -> p (j c)"), start=True, stop=True), [t4, t5, t1], last=True)
        yield
        t5b = Q.dve(lambda e: e.tensor_copy(CSP[:].rearrange("p j c -> p (j c)"), PS[0][0:R, 0:2 * NJ]), [tq])
        tw = Q.dma(d_cs, CSD.rearrange("j p c -> p j c"), CSP[:], [t5b])
        tr = Q.dma(d_cs, CSB[:].rearrange("p n c -> p (n c)"), CSD.rearrange("(o j) p c -> o (j p c)", o=1).broadcast_to([4, 2 * NROW]), [tw])
        t_rb[0] = t5b
        yield from idle(6)
        t_last = [t_rb[0], None, None]
        for jj in range(NJ):
            for half in range(2):
                tq = Q.pe(lambda e, jj=jj, half=half: e.matmul(PS[jj % 3][:, half * R:(half + 1) * R], LF[:, jj, half * 128:(half + 1) * 128], IDN[0:R, 0:R], start=True, stop=True, is_transpose=True), [t6, t_last[jj % 3]], last=(half == 1))
            yield from idle(2)
            t_last[jj % 3] = Q.dve(lambda e, jj=jj: e.tensor_copy(LAST[:, jj, :, :], PS[jj % 3][:, 0:2 * R].rearrange("p (h n) -> p h n", h=2)), [tq])
        t_rb[0] = t_last[0]
        t7 = Q.dve(lambda e: e.memset(CRF[:, 0:1], -BIG))
        t8 = Q.dve(lambda e: e.tensor_copy(CRF[:, 1:1 + NROW], CSB[:, :, 1]), [tr])
        t9 = Q.dve(lambda e: e.tensor_tensor(ARV[:], CSB[:, :, 0], CSB[:, :, 1], op=ALU.add), [tr])
        t10 = Q.dve(lambda e: e.tensor_tensor(AFW[:], CSB[:, :, 0], CRF[:, 0:NROW], op=ALU.add), [t7, t8])
        chains.append(t10)

    def verdict():
        t1 = Q.dve(lambda e: e.tensor_reduce(STAT[0:TN, 0:1], VAL[:], axis=AX.X, op=ALU.add), [t_fields[-1], t_stat])
        t2 = Q.dve(lambda e: e.tensor_reduce(STAT[0:R, 1:2], VALT[:], axis=AX.X, op=ALU.add), t_pfree[1])
        yield from idle(6)
        tp = Q.pe(lambda e: e.matmul(PS[0][0:1, 0:3], K("ones"), STAT[:, 0:3], start=True, stop=True), [t1, t2, t_uns, t_rb[0]], last=True)
        yield
        t3 = Q.dve(lambda e: e.tensor_scalar(SUMS[:, 0:2], PS[0][0:1, 0:2], float(E), None, op0=ALU.not_equal), [tp])
        t4 = Q.dve(lambda e: e.tensor_scalar(SUMS[:, 2:3], PS[0][0:1, 2:3], 0.0, None, op0=ALU.not_equal))
        t5 = Q.dve(lambda e: e.tensor_reduce(SUMS[:, 4:5], SUMS[:, 0:3], axis=AX.X, op=ALU.max), [t3, t4])
        t_rb[0] = t4
        chains.append(Q.dve(lambda e: e.tensor_copy(FLAG[:, 0:1], SUMS[:, 4:5]), [t5]))

    def attention_weights(ready):
        prev = []
        for l in range(2):
            H = HS[l]
            t0 = Q.dve(lambda e, l=l: e.memset(AZ[l][:], 0.0))
            yield
            for half in range(2):
                if H == 1:
                    t = Q.dve(lambda e, l=l, half=half: e.tensor_scalar(AZ[l][:, half, 4:5], ATC[l][:, half:half + 1], 0.4, None, op0=ALU.mult), [t0, t_at])
                else:
                    t = Q.dve(lambda e, l=l, half=half: e.tensor_scalar(AZ[l][:, half, 4 + 10 * half:4 + 10 * half + 6:5], K("mb"), ATC[l][:, half:half + 1], 0.4, op0=ALU.mult, op1=ALU.mult), [t0, t_at, t_con])
                yield
            for W in (WL[l], WR[l]):
                at = ATB[l][:].unsqueeze(1).broadcast_to([128, 2, CH])
                t1 = Q.dve(lambda e, W=W, at=at: e.tensor_tensor(ATW[0][:], W[:, :, 0:CH], at, op=ALU.mult), [t_wl, t_at] + prev)
                yield
                t2 = Q.dve(lambda e, H=H: e.tensor_reduce(ATR[:, :, 0:H], ATW[0][:].rearrange("p k (h c) -> p k h c", h=H), axis=AX.X, op=ALU.add), [t1] + prev)
                yield
                t3 = Q.dve(lambda e, W=W, H=H: e.tensor_scalar(W[:, :, CH:CH + H], ATR[:, :, 0:H], 0.6, None, op0=ALU.mult), [t2])
                prev = [t3]
                yield
            t4 = Q.dve(lambda e, l=l: e.tensor_scalar(ATB[l][:], ATB[l][:], 0.4, None, op0=ALU.mult), prev)
            prev = [t4, t]
            yield
        ready.extend(prev)

    PX = GF[5]
    t_pm0 = Q.pool(lambda e: e.memset(PM[:], 0.0))
    t_pad = Q.dma(d_rows, M3D[NROW:NROW + 3, :], PM[0:3, :], [t_pm0])

    t_z[0] = t_z[1] = t_fields[-1]
    t_stat = Q.dve(lambda e: e.memset(STAT[:], 0.0))
    t_uns = Q.dve(lambda e: e.scalar_tensor_tensor(ring_flat[:, 2 * SC - 2 * CW:2 * SC - CW].bitcast(BF16)[:, 0:CW], DSI[:, 0:CW], 0.0, DSI[:, 1:CW + 1], op0=ALU.add, op1=ALU.is_gt, accum_out=STAT[:, 2:3]), [t_dsi, t_stat, t_cnt])
    t_ixp = Q.pe(lambda e: e.matmul(PS[7][0:R, 0:NJ], K("sel85", TN), STF[:], start=True, stop=True), [t_stf, t_con, t_fldfree[0]], last=True)
    t_ixf = Q.dve(lambda e: e.tensor_scalar(IXF[:], PS[7][0:R, 0:NJ], K("k8", R), None, op0=ALU.add), [t_ixp])
    t_fldfree[0] = t_ixf
    t_ixi = Q.dve(lambda e: e.tensor_copy(IXI[:], IXF[:]), [t_ixf])
    t_tsd = []

    stored = [None] * NRING
    last1 = {}
    t_attw = []
    more_weights = attention_weights(t_attw)
    parts = [round(i * NT / GPT) for i in range(GPT + 1)]
    for it in range(NT + LG + 2):
        ta = it - LG
        for gg in range(GPT):
            if ahead[0] <= it * GPT + gg < NT * GPT:
                build_group(it, gg)
            if (it * GPT + gg) % 4 == 3 and it >= ATTW_AT:
                next(more_weights, None)
            if gg == POST_AT[0] and ta - 1 in last1:
                t_h = post1_vec(ta - 1, last1[ta - 1], (ta - 1) % 2)
            if gg == POST_AT[1] and ta - 1 in last1:
                t_z[1], t_te = transposes(ZB[1], t_h, ta % 2)
            if gg == POST_AT[2] and ta - 1 in last1:
                post1_mm(ta - 1, t_te, ta % 2)
            if 0 <= ta < NT and parts[gg] < parts[gg + 1]:
                tm = apply_part(ta, parts[gg], parts[gg + 1], 0, ta % 2, [t_at_tile[ta], t_acc[ta % 2]])
        if it < NT:
            r = it % NRING
            stored[r] = Q.dma(d_ad[r], AD[it], RING[0:TN, r, :], [t_at_tile[it]])
        if 0 <= ta < NT:
            ring_free[ta % NRING] = [tm, stored[ta % NRING]]
            last1[ta] = tm
    for _ in more_weights:
        pass
    t_built = t_oh[(slot_no[0] - 1) % OHW]
    for j in range(NJ):
        t_tsd.append(Q.put("gpsimd", lambda e, j=j: e.indirect_dma_start(out=TSD[:, j, :], out_offset=None, in_=A["sd"], in_offset=off(IXI[:, j:j + 1])), [t_ixi, t_built], d_tsd[j], 16))

    def edge_rows():
        t_rb[0] = t_built
        for j in range(NJ):
            yield from rows_of_tiles(j)
            yield from idle(5)
            columns_of_tiles(j, *rows[j])
            yield
        yield from idle(6)
        yield from chains_of_rows()
        yield from verdict()

    order = list(range(NT - NRING, NT)) + list(range(NT - NRING))
    slot = {t: t % NRING for t in order[:NRING]}
    for i in range(NRING, NT):
        slot[order[i]] = slot[order[i - NRING]]
    t_in = {t: t_at_tile[t] for t in order[:NRING]}
    d_xs = [cnt(f"d_xs{i}") for i in range(3)]
    d_xo, d_tab = [cnt(f"d_xo{i}") for i in range(2)], [[cnt(f"d_tab{l}{i}") for i in range(2)] for l in range(2)]
    d_xr = [[cnt(f"d_xro{l}{i}") for i in range(2)] for l in range(2)]
    t_xsfree = [t_fields[-1]] * 3
    t_sm = [None, None]
    t_x1 = {}
    t_tab = [[], []]
    t_xro = [{}, {}]
    t_xl, t_xrs = [None, None], [None, None]

    def norm(y, t_y, yc, out, sm, t_sum, free, sq):
        t1 = Q.dve(lambda e: e.tensor_scalar(sm[:, 1:2], sm[:, 0:1], -1.0 / CH, None, op0=ALU.mult), [t_sum])
        t2 = Q.dve(lambda e: e.tensor_scalar(yc, y, sm[:, 1:2], None, op0=ALU.add), [t1, t_y])
        t3 = Q.act(lambda e: e.activation(sq, yc, ACT.Square, accum_out=sm[:, 2:3]), [t2])
        t4 = Q.dve(lambda e: e.tensor_scalar(sm[:, 3:4], sm[:, 2:3], 1.0 / CH, EPS, op0=ALU.mult, op1=ALU.add), [t3])
        t5 = Q.act(lambda e: e.activation(sm[:, 4:5], sm[:, 3:4], ACT.Sqrt), [t4])
        t6 = Q.dve(lambda e: e.reciprocal(sm[:, 5:6], sm[:, 4:5]), [t5])
        return Q.dve(lambda e: e.tensor_scalar(out, yc, sm[:, 5:6], None, op0=ALU.mult), [t6] + free)

    def post2_vec(i, t, tm):
        acc, b = i % 2, i % 3
        sm = SMALL[i % 2]
        z, y, yc, x1 = (ZB[k][:] for k in range(4))
        tl = t_xs[i]
        t1 = Q.dve(lambda e: e.tensor_tensor(z, PS[3 + acc][0:TN, 0:CH], HP[1][:, t, :], op=ALU.add), [tm, t_z[0]])
        t_acc[acc] = t1
        t2 = Q.dve(lambda e: e.scalar_tensor_tensor(y, z, DIS[:, t:t + 1], BB[1][:], op0=ALU.mult, op1=ALU.add), [t1, t_z[1]])
        t3 = Q.dve(lambda e: e.scalar_tensor_tensor(z, y, 1.0, XST[b][:], op0=ALU.mult, op1=ALU.add, accum_out=sm[:, 0:1]), [t2, tl, t_sm[i % 2]])
        t_xsfree[b] = t3
        t4 = norm(z, t3, yc, x1, sm, t3, [t_z[3], t_x1read[0]], y)
        t_z[0] = t_z[1] = t_sm[i % 2] = t4
        t_z[3] = to = Q.dma(d_xo[i % 2], X1D[t * TN:(t + 1) * TN, :], x1, [t4])
        t_x1[t] = to
        return t4

    def tables(l, t, k, t_ht_ready, HTk, M1, M2, XLk, XRk, free1, free2, w, cols):
        H = HS[l]
        for c in range(2):
            tm1 = Q.pe(lambda e, c=c: e.matmul(M1[0:TN, 0:CH + H], HTk[:, c, :], WL[l][:, c, :], start=(c == 0), stop=(c == 1)), [t_ht_ready] + t_attw + free1, last=(c == 1))
        ta = Q.act(lambda e: e.activation(XLk[:, 0:CH + H], M1[0:TN, 0:CH + H], ACT.Copy), [tm1, t_xl[k]] + t_lsf[k])
        td = Q.dma(d_tab[l][k], TAB[l][t * TN:(t + 1) * TN, :], XLk[:, 0:CH + H], [ta])
        t_xl[k] = td
        t_tab[l].append(td)
        yield ta
        for c in range(2):
            tm2 = Q.pe(lambda e, c=c: e.matmul(M2[0:TN, 0:CH + H], HTk[:, c, :], WR[l][:, c, :], start=(c == 0), stop=(c == 1)), free2, last=(c == 1))
        t_ht[k] = tm2
        th = Q.act(lambda e: e.activation(XRk[:, 0:CH].bitcast(F32R), M2[0:TN, 0:CH], ACT.Copy), [tm2, t_xrs[k]])
        th2 = Q.act(lambda e: e.activation(ARN[l][:, t, :], M2[0:TN, CH:CH + H], ACT.Copy))
        yield th2
        tl = Q.dve(lambda e: e.tensor_tensor(XRk[:, CH:2 * CH].bitcast(F32R), M2[0:TN, 0:CH], XRk[:, 0:CH], op=ALU.subtract), [th2])
        td = Q.dma(d_xr[l][k], XRD[l][t], XRk[:], [tl])
        t_xrs[k] = td
        t_xro[l][t] = td
        t1 = Q.dve(lambda e: e.tensor_tensor(w[0], M2[0:TN, 0:CH], XLk[:, 0:CH], op=ALU.add), [ta] + cols)
        t2 = Q.dve(lambda e: e.tensor_tensor(LSF[l][:, t, :], M2[0:TN, CH:CH + H], XLk[:, CH:CH + H], op=ALU.add))
        yield t2
        ta2 = Q.act(lambda e: e.activation(w[1], w[0], ACT.Abs), [t1] + cols)
        t3 = Q.dve(lambda e: e.tensor_tensor(w[0], w[1], ATB[l][0:TN, :], op=ALU.mult), [ta2])
        t4 = Q.dve(lambda e: e.tensor_reduce(w[2][:, 0:H], w[0].rearrange("p (h c) -> p h c", h=H), axis=AX.X, op=ALU.add), [t3] + cols)
        t5 = Q.dve(lambda e: e.tensor_tensor(LSF[l][:, t, :], LSF[l][:, t, :], w[2][:, 0:H], op=ALU.add), [t4, t2])
        t_lsf[k] = [t5]
        yield t5

    t_lsf = [[], []]
    t_x1read = [None]
    t_wfree = []
    m_free = [[t_pm[0]], [t_fldfree[0]]]
    W2B = [GF[3][:], GF[4][:], SMALL[0][:, 8:12]]
    cuts = [round(i * NT / 8) for i in range(9)]
    prev = None
    more_rows = edge_rows()
    t_xs = {}

    def load_x(i):
        b, t = i % 3, order[i]
        t_xs[i] = Q.dma(d_xs[b], XST[b][:], A["x"][t * TN:(t + 1) * TN, :], [t_xsfree[b]])

    load_x(0)
    for i in range(NT + 1):
        if i < NT:
            t = order[i]
            RT = RING[0:TN, slot[t], :]
        tab = None
        for q in range(8):
            if i >= ROWS_FROM:
                next(more_rows, None)
            if i < NT:
                for s in range(cuts[q], cuts[q + 1]):
                    tm = Q.pe(lambda e, s=s, RT=RT, i=i: e.matmul(PS[3 + i % 2][0:TN, 0:CH], RT[:, s * TN:(s + 1) * TN], HP[1][:, s, :], start=(s == 0), stop=(s == NT - 1)), [t_in[t], t_hp[1][s], t_acc[i % 2]], last=(s == NT - 1))
            if prev is not None:
                pt, t_v, k = prev
                if q == 3:
                    t_tp, t_te = transposes(ZB[3], t_v, k)
                    t_x1read[0] = t_tp
                if q == 5:
                    tab = tables(0, pt, k, t_te, HT[k], PS[6], PS[7], XL[k], XRS[k], m_free[0], m_free[1], W2B, list(t_wfree))
                    m_free[0] = [next(tab)]
                if q == 6:
                    next(tab)
                if q == 7:
                    m_free[1] = [next(tab)]
                    t_wfree = [next(tab)]
        if i < NT:
            if i + 1 < NT:
                load_x(i + 1)
            if i + NRING < NT:
                nx = order[i + NRING]
                t_in[nx] = Q.dma(d_ad[slot[nx]], RING[0:TN, slot[nx], :], AD[nx], [tm, stored[slot[nx]]])
            t_v = post2_vec(i, t, tm)
            prev = (t, t_v, i % 2)

    for _ in more_rows:
        pass
    t_chain, t_flag = chains

    gcn_end = [(Q.done[n], Q.done[n].value) for n in ("tensor", "vector", "scalar", "gpsimd")]
    ring_end = [tm] + t_acc + [(c, c.value) for c in d_ad]
    gcn_end += [(c, c.value) for c in d_ad + d_xo + d_tab[0] + d_xr[0] + [d_rows]]
    gcn.close()

    gat = ExitStack()
    ss = lambda name, shape, dt=F32: gat.enter_context(nc.sbuf_tensor(name, shape, dt))
    windows, blocks, _ = reach(E, N)
    NCH, CMAX = len(CHUNKS), max(b - a for a, b in CHUNKS)
    G = ss("g", [128, RP * 2 * (CH + 8)])
    NOT = 3
    OHT = [ss(f"oht{i}", [2 * WIN, CMAX * ROW], F32R) for i in range(NOT)]
    DLB = [ss(f"dlb{i}", [2 * WIN, CMAX * ROW], BF16) for i in range(NOT)]
    XR = [ss(f"xr{i}", [2 * WIN, len(WINS), CH], F32R) for i in range(2)]
    M3 = [ss(f"m3{i}", [128, 772], BF16) for i in range(2)]
    NAB = 8
    ABS = [ss(f"abs{i}", [128, 2 * ROW]) for i in range(NAB)]
    NOH = 2 * KP + 4 * CMAX
    OH = [ss(f"oh{i}", [128, BL * max(b1 - b0 + 1 for b0, b1 in blocks)]) for i in range(NOH)]
    ALB = ss("alb", [128, 2, 128])
    F1, F2, F3, EX = (ss(n, [128, ROW]) for n in ("f1", "f2", "f3", "ex"))
    SGM = ss("sgm", [128, 2 * KP])
    VW = ss("vw", [4, 2 * KP])
    CC = ss("cc", [4, 2, KP])
    CRL = ss("crl", [128, 2])
    XLT = [ss(f"xlt{i}", [TN, CH]) for i in range(2)]
    X1T = [ss(f"x1t{i}", [TN, CH]) for i in range(2)]
    SM = [ss(f"sm{i}", [TN, 64]) for i in range(2)]
    O = [ss(f"o{i}", [TN, CH]) for i in range(4)]
    HT2 = [ss(f"ht2{i}", [128, 2, TN]) for i in range(2)]
    XL2 = [ss(f"xl2{i}", [TN, CH + 1]) for i in range(2)]
    XRS2 = [ss(f"xrs2{i}", [TN, 2 * CH]) for i in range(2)]
    W2C = [ss(f"w2c{i}", [TN, CH]) for i in range(2)]
    W2D = ss("w2d", [TN, 4])
    NG5 = 5
    YC = [ss(f"yc{i}", [TN, NG5, CH]) for i in range(2)]
    SSQ = [ss(f"ssq{i}", [TN, 3, NG5]) for i in range(2)]

    d_g = [[cnt(f"d_g{i}{a}") for a in range(2)] for i in range(RP)]
    d_dlb = [cnt(f"d_dlb{i}") for i in range(NOT)]
    d_xri = [cnt(f"d_xri{i}") for i in range(2)]
    d_m3 = [cnt(f"d_m3{i}") for i in range(2)]
    d_xlt = [cnt(f"d_xlt{i}") for i in range(2)]
    d_x1t = [cnt(f"d_x1t{i}") for i in range(2)]
    d_out = [cnt(f"d_out{i}") for i in range(2)]

    for n in ("sync", "tensor", "vector", "scalar"):
        Q.put(n, None, gcn_end)
    Q.put("gpsimd", None, ring_end if RP * 2 * (CH + 8) <= 2 * NT * CH + NRING * SC else gcn_end)
    for k in range(2):
        t_xl[k] = t_xrs[k] = None
        t_lsf[k] = []
    t_ht[0] = t_ht[1] = None

    MT = (0, 1, 2, 7)
    NMT = len(MT)
    LBK, AGG = (3, 4), (5, 6)
    t_mt = [None] * NMT
    t_abs = [None] * NAB
    t_oh2 = [None] * NOH
    t_gfree = [None] * RP
    t_g = {}
    t_oht = {}
    t_ohtfree, t_dlbfree = [None] * NOT, [None] * NOT
    t_xrfree, t_m3free = [None, None], [None, None]
    t_lfree = [None, None]
    t_aggfree = [[], []]
    t_xltfree, t_x1tfree = [None, None], [None, None]
    t_smfree = [[], []]
    t_o = [None] * 4
    t_cc0 = Q.dve(lambda e: e.memset(CC[:], -BIG))
    for x in (*M3, ALB):
        t_m0 = Q.dve(lambda e, x=x: e.memset(x[:], 0.0))
    t_alb = [t_m0]
    t_ycfree = [[], []]
    oh_no = [0]
    oh_used = set()
    chunk_of = [min(i // 4, NCH - 1) for i in range(KP)]

    def attention(l, tab_ready, xr_ready):
        H = HS[l]
        GW = CH + 2 * H
        C = CH // H
        GV = G[:, 0:RP * 2 * GW].rearrange("p (r a c) -> p r a c", r=RP, a=2)
        sched = {}
        at = lambda it, fn: sched.setdefault(it, []).append(fn)
        t_dlb, t_xri, t_m3, t_xlt, t_x1t, t_mm, t_a, t_ex, t_hot, t_scaled = ({} for _ in range(10))
        st0, st1, st2, st3 = [None], [None], [None], [None]

        def load_targets(c):
            t, n = divmod(c, NCH)
            a, b = CHUNKS[n]
            t_dlb[c] = Q.dma(d_dlb[c % NOT], DLB[c % NOT][:, 0:(b - a) * ROW], DLBD.rearrange("(t k) e -> t (k e)", t=NT)[t:t + 1, a * ROW:b * ROW].broadcast_to([2 * WIN, (b - a) * ROW]), [t_dlbfree[c % NOT]])

        def load_windows(t):
            b = t % 2
            for w, w0 in enumerate(WINS):
                src = XRD[l][t].rearrange("n (x c) -> x n c", x=2)[:, w0:w0 + WIN, :]
                t_xri[t] = Q.dma(d_xri[b], XR[b][:, w, :].bitcast(F32), src, [xr_ready[t], t_xrfree[b]])

        def load_masks(t):
            b = t % 2
            for g in range(4):
                rows = M3D[t * KP + g:t * KP + g + 17:4, :]
                for h in range(H):
                    t_m3[t] = Q.dma(d_m3[b], M3[b][BL * g + 5 * h:BL * g + 5 * h + 5, :], rows, [t_m3free[b], t_m0])

        def load_self(t):
            b = t % 2
            t_xlt[t] = Q.dma(d_xlt[b], XLT[b][:], TAB[l][t * TN:(t + 1) * TN, 0:CH], [t_xltfree[b]])
            if l == 1:
                t_x1t[t] = Q.dma(d_x1t[b], X1T[b][:], X1D[t * TN:(t + 1) * TN, :], [t_x1tfree[b]])

        def place(t, i):
            return t // 5, (t % 5) * KP + i

        def gather(q):
            r = q % RP
            j, c = place(q // KP, q % KP)
            t_g[q] = [Q.put("gpsimd", lambda e, a=a: e.indirect_dma_start(out=GV[:, r, a, 0:CH + H], out_offset=None, in_=TAB[l], in_offset=off(SRCI[:, j, a, c:c + 1])), [t_gfree[r]] + (tab_ready if q == 0 else []), d_g[r][a], 16) for a in range(2)]

        def onehot_t(c):
            b = c % NOT
            w = (CHUNKS[c % NCH][1] - CHUNKS[c % NCH][0]) * ROW
            t_oht[c] = t_dlbfree[b] = Q.dve(lambda e: e.tensor_scalar(OHT[b][:, 0:w], DLB[b][:, 0:w], K("pwin", 2 * WIN), None, op0=ALU.is_equal), [t_dlb[c], t_ohtfree[b]])

        def expand(q):
            t, i = q // KP, q % KP
            c = t * NCH + chunk_of[i]
            e0 = (i - CHUNKS[chunk_of[i]][0]) * ROW
            w = WINS.index(windows[i])
            b, r, bank = t % 2, q % RP, PS[MT[q % NMT]]
            first = [t_oht[c], t_xri[t], t_mt[q % NMT]]
            for half in range(2):
                tm = Q.pe(lambda e, half=half: e.matmul(bank[:, half * ROW:(half + 1) * ROW], XR[b][:, w, half * 128:(half + 1) * 128], OHT[c % NOT][:, e0:e0 + ROW], start=(half == 0), stop=False, skip_group_check=True), first if half == 0 else [])
            for half in range(2):
                for a in range(2):
                    tm = Q.pe(lambda e, half=half, a=a: e.matmul(bank[:, half * ROW + a * 128:half * ROW + (a + 1) * 128], GV[:, r, a, half * 128:(half + 1) * 128], IDN, start=False, stop=(half == 1 and a == 1), is_transpose=True, skip_group_check=True), [t_g[q][a]], last=(half == 1 and a == 1))
            t_mm[q] = tm
            if i == KP - 1:
                t_xrfree[b] = tm
            if i == CHUNKS[chunk_of[i]][1] - 1:
                t_ohtfree[c % NOT] = tm
            t_a[q] = t_mt[q % NMT] = Q.act(lambda e: e.activation(ABS[q % NAB][:], bank[:], ACT.Abs), [tm, t_abs[q % NAB]])

        def linear(t, q):
            r0 = (t % 2) * KP
            for a in range(2):
                src = GV[:, r0:r0 + 16, a, CH:CH + H].rearrange("p (k g) h -> p g h k", g=4)
                dst = ALB[:, a, :].rearrange("p (g x) -> p g x", g=4)[:, :, 0:20].rearrange("p g (h k) -> p g h k", k=5)[:, :, 0:H, 0:4]
                Q.dve(lambda e, src=src, dst=dst: e.tensor_copy(dst, src), [t_mm[q], t_alb[0]])
            src = GV[:, r0 + 16, :, CH:CH + H]
            dst = ALB[:, :, 4:4 + 5 * H:5]
            return Q.dve(lambda e: e.tensor_copy(dst, src), [t_mm[q], t_alb[0]])

        def logits(c):
            t, n = divmod(c, NCH)
            bank = PS[LBK[t % 2]]
            a, b = CHUNKS[n]
            first = [t_a[t * KP + b - 1], t_lfree[t % 2] if n == 0 else None]
            for i0 in range(a, b, 4):
                for half in range(2):
                    for i in range(i0, min(i0 + 4, b)):
                        g, q = i % 4, t * KP + i
                        tm = Q.pe(lambda e, g=g, i=i, half=half, q=q: e.matmul(bank[BL * g:BL * (g + 1), 0:ROW], AZ[l][:, half, 4 - i // 4:4 - i // 4 + BL], ABS[q % NAB][:, half * ROW:(half + 1) * ROW], start=(i < 4 and half == 0), stop=False, skip_group_check=True), first, last=(i == b - 1 and half == 1))
                        first = []
            for i in range(a, b):
                t_abs[(t * KP + i) % NAB] = tm
            if n == NCH - 1:
                tl = linear(t, t * KP + KP - 1)
                for a in range(2):
                    tm = Q.pe(lambda e, a=a: e.matmul(bank[:, a * 128:(a + 1) * 128], ALB[:, a, :], IDN, start=False, stop=(a == 1), is_transpose=True, skip_group_check=True), [tl], last=(a == 1))
                t_alb[0] = tm
            return tm

        def softmax_rows(t, tl, it):
            b = t % 2
            r0 = (t % 2) * KP
            F, Pm, Sm = M3[b][:, 0:ROW + 1], M3[b][:, ROW + 1:2 * ROW + 1], M3[b][:, 2 * ROW + 1:3 * ROW + 1]
            bank = PS[LBK[b]]
            Lrow = bank[:, 0:ROW]
            S2 = K("sel2")
            j, c0 = place(t, 0)
            st = {}

            def s1():
                t1 = Q.dve(lambda e: e.tensor_tensor_scan(F1[:], F[:, 0:ROW], Lrow, -BIG, op0=ALU.add, op1=ALU.max), [tl, t_m3[t], st1[0]])
                t2 = Q.dve(lambda e: e.tensor_tensor_scan(F2[:, ::-1], F[:, ROW:0:-1], F1[:, ::-1], -BIG, op0=ALU.add, op1=ALU.max), [t1, st1[0]])
                st["g"] = t2
                st["sg"] = Q.dve(lambda e: e.tensor_tensor(SGM[:].rearrange("p (x k) -> p x k", x=2), S2.rearrange("p (x k) -> p x k", x=2), F2[:, 0:ROW:ROW - 1].unsqueeze(2).broadcast_to([128, 2, KP]), op=ALU.mult), [t2, st1[0]])

            def s2():
                chp = bank[0:H, ROW:ROW + 2 * KP]
                tp = Q.pe(lambda e: e.matmul(chp, K("hm")[:, 0:H], SGM[:], start=True, stop=True), [st["sg"]], last=True)
                row = slice(t * KP, (t + 1) * KP)
                t1 = Q.dve(lambda e: e.tensor_tensor_scan(VW[0:H, KP:2 * KP], AFW[0:H, row], chp[:, KP:2 * KP], -BIG, op0=ALU.add, op1=ALU.max), [tp, t_chain])
                t2 = Q.dve(lambda e: e.tensor_tensor_scan(VW[0:H, 0:KP][:, ::-1], ARV[0:H, row][:, ::-1], chp[:, 0:KP][:, ::-1], -BIG, op0=ALU.add, op1=ALU.max))
                t3 = Q.dve(lambda e: e.tensor_tensor(CC[0:H, 1, 1:KP], VW[0:H, KP:2 * KP - 1], CRF[0:H, t * KP + 1:(t + 1) * KP], op=ALU.add), [t1, t_cc0, st2[0]])
                st["cc"] = Q.dve(lambda e: e.tensor_tensor(CC[0:H, 0, 0:KP - 1], VW[0:H, 1:KP], CRF[0:H, t * KP + 1:(t + 1) * KP], op=ALU.add), [t2])

            def s3():
                exp_ = bank[:, ROW + 64:ROW + 64 + 2 * KP]
                tp = Q.pe(lambda e: e.matmul(exp_, K("hmt", 4)[0:H, :], CC[0:H, :, :].rearrange("p x k -> p (x k)"), start=True, stop=True), [st["cc"]], last=True)
                st2[0] = tp
                t1 = Q.dve(lambda e: e.tensor_tensor(SGM[:], exp_, S2, op=ALU.mult), [tp])
                t2 = Q.dve(lambda e: e.tensor_reduce(CRL[:], SGM[:].rearrange("p (x k) -> p x k", x=2), axis=AX.X, op=ALU.add), [t1])
                t3 = Q.dve(lambda e: e.scalar_tensor_tensor(F1[:], Pm, CRL[:, 1:2], F2[:], op0=ALU.add, op1=ALU.max), [t2])
                t4 = Q.dve(lambda e: e.scalar_tensor_tensor(F3[:], Sm, CRL[:, 0:1], F1[:], op0=ALU.add, op1=ALU.max), [t3, st3[0]])
                t_m3free[b] = t4
                t5 = Q.dve(lambda e: e.tensor_tensor(F2[:], Lrow, F3[:], op=ALU.subtract), [t4])
                st["e"] = Q.act(lambda e: e.activation(EX[:], F2[:], ACT.Exp), [t5, st3[0]])
                st1[0] = st["e"]

            def s4():
                for x, src in ((0, EX), (1, F3)):
                    for a in range(2):
                        tp = Q.pe(lambda e, x=x, a=a, src=src: e.matmul(bank[:, (2 * x + a) * 128:(2 * x + a + 1) * 128], src[:, a * 128:(a + 1) * 128], IDN, start=True, stop=True, is_transpose=True), [st["e"]], last=(x == 1 and a == 1))
                st3[0] = tp
                for a in range(2):
                    v = bank[:, a * 128:(a + 1) * 128].rearrange("p (g x) -> p g x", g=4)[:, :, 0:20].rearrange("p g (h k) -> p g h k", k=5)[:, :, 0:H, 0:4]
                    out = GV[:, r0:r0 + 16, a, CH:CH + H].rearrange("p (k g) h -> p g h k", g=4)
                    t1 = Q.dve(lambda e, out=out, v=v: e.tensor_copy(out, v), [tp])
                v = bank[:, 0:256].rearrange("p (a n) -> p a n", a=2)[:, :, 4:4 + 5 * H:5]
                t_ex[t] = Q.dve(lambda e: e.tensor_copy(GV[:, r0 + 16, :, CH:CH + H], v), [tp])

            def s5():
                for a in range(2):
                    v = bank[:, 256 + a * 128:256 + (a + 1) * 128].rearrange("p (g x) -> p g x", g=4)[:, :, 0:20].rearrange("p g (h k) -> p g h k", k=5)[:, :, 0:H, 0:4]
                    out = GV[:, r0:r0 + 16, a, CH + H:CH + 2 * H].rearrange("p (k g) h -> p g h k", g=4)
                    last = LAST[:, j, a, c0:c0 + 16].rearrange("p (k g) -> p g k", g=4).unsqueeze(2).broadcast_to([128, 4, H, 4])
                    t1 = Q.dve(lambda e, out=out, v=v, last=last: e.tensor_tensor(out, v, last, op=ALU.mult), [t_ex[t]])
                v = bank[:, 256:512].rearrange("p (a n) -> p a n", a=2)[:, :, 4:4 + 5 * H:5]
                last = LAST[:, j, :, c0 + 16].unsqueeze(2).broadcast_to([128, 2, H])
                t_lfree[b] = t_ex[t] = Q.dve(lambda e: e.tensor_tensor(GV[:, r0 + 16, :, CH + H:CH + 2 * H], v, last, op=ALU.mult), [t_ex[t]])

            for n, f in ((0, s1), (0, s2), (1, s3), (2, s4), (2, s5)):
                at(it + n, f)

        def onehots(q):
            t, i = q // KP, q % KP
            j, c = place(t, i)
            t_hot[q] = []
            for a in range(2):
                o = oh_no[0] % NOH
                oh_no[0] += 1
                assert o not in oh_used
                oh_used.add(o)
                b0, b1 = blocks[2 * i + a]
                w = (b1 - b0 + 1) * BL
                t1 = Q.dve(lambda e, a=a, o=o, b0=b0, w=w: e.tensor_scalar(OH[o][:, 0:w], K("iota")[:, b0 * BL:b0 * BL + w], DLS[:, j, a, c:c + 1], None, op0=ALU.is_equal), [t_oh2[o]])
                t_hot[q].append((o, t1))

        def scale(q):
            t, i = q // KP, q % KP
            r = q % RP
            j, c = place(t, i)
            if q not in t_hot:
                onehots(q)
            t_scaled[q] = []
            for a in range(2):
                o, t1 = t_hot[q][a]
                rows = GV[:, r, a, 0:CH]
                n = 2 * (q - NP + LAGC) + a
                by = LAST_BY[l][n % len(LAST_BY[l])] if n >= 0 else "v"
                put = Q.pool if by == "g" else Q.dve
                if by == "s":
                    for h in range(H):
                        t2 = Q.act(lambda e, a=a, h=h, rows=rows: e.activation(rows[:, h * C:(h + 1) * C], rows[:, h * C:(h + 1) * C], ACT.Copy, scale=GV[:, r, a, CH + h:CH + h + 1]), [t_ex[t]])
                elif H == 1:
                    t2 = put(lambda e, a=a, rows=rows: e.tensor_scalar(rows, rows, GV[:, r, a, CH:CH + 1], None, op0=ALU.mult), [t_ex[t]])
                else:
                    rv = rows.rearrange("p (h c) -> p h c", h=H)
                    t2 = put(lambda e, a=a, rv=rv: e.tensor_tensor(rv, rv, GV[:, r, a, CH:CH + H].unsqueeze(2).broadcast_to([128, H, C]), op=ALU.mult), [t_ex[t]])
                t_scaled[q].append((o, [t1, t2]))

        seen_block = {}

        def sums(c):
            t, n = divmod(c, NCH)
            a_, b_ = CHUNKS[n]
            todo = [[] for _ in range(4)]
            for i in range(a_, b_):
                for a in range(2):
                    b0, b1 = blocks[2 * i + a]
                    for blk in range(b0, b1 + 1):
                        todo[blk].append((i, a, blk - b0))
            later = {blk for m in range(n + 1, NCH) for i in range(*CHUNKS[m]) for a in range(2) for blk in range(blocks[2 * i + a][0], blocks[2 * i + a][1] + 1)}
            count = sum(len(x) for x in todo)
            first = latest([x for i in range(a_, b_) for _, ts in t_scaled[t * KP + i] for x in ts]) + (t_aggfree[t % 2] if n == 0 else [])
            while any(todo):
                for blk in range(4):
                    if not todo[blk]:
                        continue
                    i, a, s = todo[blk].pop(0)
                    count -= 1
                    r = (t * KP + i) % RP
                    o = t_scaled[t * KP + i][a][0]
                    start = seen_block.setdefault((t, blk), True)
                    seen_block[(t, blk)] = False
                    stop = not todo[blk] and blk not in later
                    tm = Q.pe(lambda e, o=o, s=s, r=r, a=a, blk=blk, start=start, stop=stop: e.matmul(PS[AGG[t % 2]][blk * BL:(blk + 1) * BL, 0:GW], OH[o][:, s * BL:(s + 1) * BL], GV[:, r, a, 0:GW], start=start, stop=stop, skip_group_check=True), first, last=(count == 0))
                    first = []
            for i in range(a_, b_):
                q = t * KP + i
                t_gfree[q % RP] = tm
                for o, _ in t_scaled[q]:
                    t_oh2[o] = tm
                    oh_used.remove(o)
            return tm

        def finish(t, tm, it):
            b = t % 2
            agg = PS[AGG[b]][0:TN, 0:GW]
            sm = SM[b]
            D, M = agg[:, CH:CH + H], agg[:, CH + H:CH + 2 * H]
            self_ = LSF[l][:, t, :]
            e0, mf, mm = sm[:, 0:H], sm[:, 4:4 + H], sm[:, 8:8 + H]
            dd, rs = sm[:, 16:16 + 2 * H], sm[:, 24:24 + 2 * H]
            den, rec, fr = sm[:, 32:32 + H], sm[:, 36:36 + H], sm[:, 40:40 + 2 * H]
            st = {}
            o1, o2, o3, o4 = (x[:] for x in O)

            def f0():
                t1 = Q.dve(lambda e: e.tensor_scalar(e0, D, 0.0, -BIG, op0=ALU.is_equal, op1=ALU.mult), [tm] + t_smfree[b])
                t2 = Q.dve(lambda e: e.tensor_tensor(mf, M, e0, op=ALU.add), [t1])
                t2 = Q.dve(lambda e: e.tensor_tensor(mf, mf, ARN[l][:, t, :], op=ALU.add), [t2])
                t3 = Q.dve(lambda e: e.tensor_tensor(mm, mf, self_, op=ALU.max), [t2])
                t4 = Q.dve(lambda e: e.tensor_tensor(dd[:, 0:H], mf, mm, op=ALU.subtract), [t3])
                t5 = Q.dve(lambda e: e.tensor_tensor(dd[:, H:2 * H], self_, mm, op=ALU.subtract))
                st["x"] = Q.act(lambda e: e.activation(rs, dd, ACT.Exp), [t5])
                if l == 1 and t == NT - 1:
                    Q.act(lambda e: e.activation(sm[:, 50:51], K("ones", TN), ACT.Sqrt), [t_con])

            def f1():
                t1 = Q.dve(lambda e: e.tensor_tensor(den, D, rs[:, 0:H], op=ALU.mult), [st["x"]])
                t2 = Q.dve(lambda e: e.tensor_tensor(e0, den, rs[:, H:2 * H], op=ALU.add), [t1])
                t3 = Q.dve(lambda e: e.reciprocal(rec, e0), [t2])
                t4 = Q.dve(lambda e: e.tensor_tensor(fr.rearrange("p (x h) -> p x h", x=2), rs.rearrange("p (x h) -> p x h", x=2), rec.unsqueeze(1).broadcast_to([TN, 2, H]), op=ALU.mult), [t3])
                hv = lambda x: x.rearrange("p (h c) -> p h c", h=H)
                st["a"] = Q.dve(lambda e: e.tensor_tensor(hv(o1), hv(agg[:, 0:CH]), fr[:, 0:H].unsqueeze(2).broadcast_to([TN, H, C]), op=ALU.mult), [t4, t_o[0]])
                st["b"] = Q.dve(lambda e: e.tensor_tensor(hv(o2), hv(XLT[b][:]), fr[:, H:2 * H].unsqueeze(2).broadcast_to([TN, H, C]), op=ALU.mult), [t_xlt[t], t_o[1]])
                t_smfree[b] = [st["b"]]
                t_xltfree[b] = st["b"]

            def f2():
                t1 = Q.dve(lambda e: e.tensor_tensor(o3, o1, o2, op=ALU.add), [st["b"], t_o[2]])
                st["o"] = Q.dve(lambda e: e.tensor_tensor(o1, o3, BB[2 + l][:], op=ALU.add), [t1])

            if l == 0:
                def f3():
                    t1 = Q.dve(lambda e: e.tensor_scalar(o2, o1, 0.0, None, op0=ALU.min), [st["o"]])
                    t2 = Q.act(lambda e: e.activation(o3, o2, ACT.Exp), [t1])
                    st["e"] = t2

                def f4():
                    t1 = Q.dve(lambda e: e.scalar_tensor_tensor(o2, o1, 0.0, o3, op0=ALU.max, op1=ALU.add), [st["e"]])
                    st["h"] = Q.dve(lambda e: e.tensor_scalar(o4, o2, -1.0, None, op0=ALU.add), [t1, t_o[3]])
                    t_o[0] = t_o[1] = t_o[2] = st["h"]

                def f5():
                    bank = PS[AGG[b]]
                    for c in range(2):
                        tp = Q.pe(lambda e, c=c: e.matmul(bank[:, c * TN:(c + 1) * TN], o4[:, c * 128:(c + 1) * 128], IDN[0:TN, 0:TN], start=True, stop=True, is_transpose=True), [st["h"]], last=(c == 1))
                    t_o[3] = tp
                    te = Q.act(lambda e: e.activation(HT2[b][:], bank[:, 0:2 * TN].rearrange("p (k n) -> p k n", k=2), ACT.Copy), [tp, t_ht[b]])
                    st["tab"] = tables(1, t, b, te, HT2[b], bank, bank, XL2[b], XRS2[b], [], [], [W2C[0][:], W2C[1][:], W2D], list(t_wfree2))

                def f6():
                    st["m1"] = next(st["tab"])

                def f7():
                    Q.put("tensor", None, [st["m1"]])
                    next(st["tab"])

                def f8():
                    next(st["tab"])

                def f9():
                    t_wfree2[:] = [next(st["tab"])]
                    t_aggfree[b] = list(t_wfree2)

                steps = (f0, f1, f2, f3, f4, f5, f6, f7, f8, f9)
            else:
                g, n = divmod(t, NG5) if t < NT - 1 else ((NT - 2) // NG5 + 1, 0)
                y = g % 2
                yc = YC[y]

                def f3():
                    t1 = Q.dve(lambda e: e.scalar_tensor_tensor(o2, o1, 1.0, X1T[b][:], op0=ALU.mult, op1=ALU.add, accum_out=sm[:, 48:49]), [st["o"], t_x1t[t]])
                    t_x1tfree[b] = t1
                    t2 = Q.dve(lambda e: e.tensor_scalar(sm[:, 49:50], sm[:, 48:49], -1.0 / CH, None, op0=ALU.mult), [t1])
                    t3 = Q.dve(lambda e: e.tensor_scalar(yc[:, n, :], o2, sm[:, 49:50], None, op0=ALU.add), [t2] + t_ycfree[y])
                    t4 = Q.act(lambda e: e.activation(o3, yc[:, n, :], ACT.Square, accum_out=SSQ[y][:, 0, n:n + 1]), [t3])
                    t_o[0] = t_o[1] = t_o[2] = t4
                    t_smfree[b].append(t3)
                    st["n"] = t4
                    t_aggfree[b] = [st["a"]]

                def f4():
                    if n == NG5 - 1 or t >= NT - 2:
                        w = n + 1
                        t1 = Q.dve(lambda e: e.tensor_scalar(SSQ[y][:, 1, 0:w], SSQ[y][:, 0, 0:w], 1.0 / CH, EPS, op0=ALU.mult, op1=ALU.add), [st["n"]])
                        t2 = Q.act(lambda e: e.activation(SSQ[y][:, 2, 0:w], SSQ[y][:, 1, 0:w], ACT.Sqrt), [t1])
                        t3 = Q.dve(lambda e: e.reciprocal(SSQ[y][:, 1, 0:w], SSQ[y][:, 2, 0:w]), [t2])
                        for i in range(w):
                            t4 = Q.dve(lambda e, i=i: e.tensor_scalar(yc[:, i, :], yc[:, i, :], SSQ[y][:, 1, i:i + 1], None, op0=ALU.mult), [t3])
                        t0 = t - n
                        td = Q.dma(d_out[y], A["out"][t0 * TN:(t + 1) * TN, :].rearrange("(t p) c -> p t c", p=TN), yc[:, 0:w, :], [t4])
                        t_ycfree[y] = [td]

                steps = (f0, f1, f2, f3, f4)
            for n_, f in enumerate(steps):
                at(it + 1 + n_, f)

        t_wfree2 = []
        LEAD = RP - LAGC - 6
        for c in range(NOT):
            load_targets(c)
        load_windows(0)
        load_masks(0)
        onehot_t(0)
        load_targets(NOT)
        for q in range(LEAD):
            gather(q)
        due, sums_due = {}, {}

        def due_logits(it):
            for c in due.pop(it, []):
                tl = logits(c)
                if c % NCH == NCH - 1:
                    softmax_rows(c // NCH, tl, it + 1)

        it = scaled = 0
        while it < NP or scaled < NP or sums_due or sched:
            if it < NP:
                t, i = it // KP, it % KP
                if i == 2 and t + 1 < NT:
                    load_windows(t + 1)
                if i == 9 and t + 1 < NT:
                    load_masks(t + 1)
                n = chunk_of[i]
                c = t * NCH + n
                if i == CHUNKS[n][0] + 1 and c + 1 < NT * NCH:
                    onehot_t(c + 1)
                    if c + 1 + NOT < NT * NCH:
                        load_targets(c + 1 + NOT)
                expand(it)
                if i == CHUNKS[n][1] - 1:
                    due.setdefault(it + 1, []).append(c)
            if it >= LAGC - 2 and (it - LAGC + 2) % KP == 0 and (it - LAGC + 2) // KP < NT:
                load_self((it - LAGC + 2) // KP)
            for f in sched.pop(it, []):
                f()
            if it >= NP:
                due_logits(it)
            if it >= NP - HOT_AT:
                for x in list(range(NP - KP, NP))[HOT_RATE * (it - NP + HOT_AT):HOT_RATE * (it - NP + HOT_AT + 1)]:
                    onehots(x)
            for _ in range(0 if it < LAGC else LAST_RATE if it >= NP + LAGC - KP else 1):
                if scaled < NP:
                    scale(scaled)
                    if scaled % KP in [b - 1 for _, b in CHUNKS]:
                        sums_due.setdefault(it + (LAST_LAG if it >= NP + LAGC - KP else 2), []).append(scaled)
                    scaled += 1
            if it < NP:
                due_logits(it)
            for x in sums_due.pop(it, []):
                tm = sums(x // KP * NCH + chunk_of[x % KP])
                if x % KP == KP - 1:
                    finish(x // KP, tm, it)
            if it + LEAD < NP:
                gather(it + LEAD)
            it += 1

    attention(0, t_tab[0], t_xro[0])
    attention(1, t_tab[1], t_xro[1])

    ended = [(Q.done[n], Q.done[n].value) for n in Q.done] + [(c, c.value) for c in d_out + d_tab[1] + d_xr[1]]
    for n in Q.lists:
        Q.put(n, None, ended)
    gat.close()
    W = {"2": W2S, "l0": WL[0], "r0": WR[0], "l1": WL[1], "r1": WR[1]}
    return ctx, Q, FLAG, general_path(nc, ctx, sem, A, NT, E, PS, IOTA, IDN, K("pidx", TN), W, BB, DIS)


class Serial:

    ENGINES = ("sync", "tensor", "vector", "scalar", "gpsimd")

    def __init__(self, sem):
        self.chain, self.met, self.rows = sem("g_chain"), sem("g_met"), sem("g_rows")
        self.go = {n: sem(f"g_go_{n}") for n in self.ENGINES if n != "gpsimd"}
        self.rounds = []

    def once(self, *steps):
        self.rounds.append((None, steps))

    def loop(self, count, *steps):
        self.rounds.append((count, steps))

    def run(self, name, e, steps, i):
        at = gathered = 0
        for engine, fns in steps:
            if engine == name:
                if at:
                    e.wait_ge(self.chain, at)
                for f in fns:
                    ins = f(e, i)
                    if engine == "sync":
                        ins.then_inc(self.chain, 16)
                if engine == "gpsimd":
                    gathered += 16
                    ins.then_inc(self.rows, 16)
                    e.wait_ge(self.rows, gathered)
                    e.sem_inc(self.chain, 1)
                elif engine != "sync":
                    ins.then_inc(self.chain, 1)
            at += 16 * len(fns) if engine == "sync" else 1
        e.wait_ge(self.chain, at)
        if name == "gpsimd":
            e.wait_ge(self.met, len(self.go))
            e.sem_clear(self.chain)
            if gathered:
                e.dma_reset(range(self.rows.num, self.rows.num + 1))
                e.sem_clear(self.rows)
            e.sem_inc(self.met, -len(self.go))
            for g in self.go.values():
                e.sem_inc(g, 1)
        else:
            e.sem_inc(self.met, 1)
            e.wait_ge(self.go[name], 1)
            e.sem_inc(self.go[name], -1)

    def emit(self, name, e):
        for count, steps in self.rounds:
            if count is None:
                self.run(name, e, steps, None)
            else:
                with e.Fori(0, count) as i:
                    self.run(name, e, steps, i)


def general_path(nc, ctx, sem, A, NT, E, PS, IOTA, IDN, PIDX, W, BB, DIS):
    N = NT * TN
    NR = A["sdr"].shape[0]
    CK = 4
    HS = (4, 1)
    sb = lambda name, shape, dt=F32: ctx.enter_context(nc.sbuf_tensor(f"g_{name}", shape, dt))
    dram = lambda name, shape, dt=F32: nc.dram_tensor(f"g_{name}", shape, dt, kind="Internal").ap()
    S = Serial(sem)
    off = lambda ap: bass.IndirectOffsetOnAxis(ap=ap, axis=0)

    DISD = dram("dis_d", (NT, TN, 1))
    HPD = [dram(f"hp{k}_d", (NT, TN, CH)) for k in range(2)]
    ACCD = dram("acc_d", (NT, TN, CH + 4))
    X1 = dram("x1_d", (NT, TN, CH))
    XLD = [dram(f"xl{l}_d", (NT, TN, CH)) for l in range(2)]
    XRD = [dram(f"xr{l}_d", (N + 1, CH)) for l in range(2)]
    LSD = [dram(f"ls{l}_d", (NT, TN, 4)) for l in range(2)]
    LGE = [dram(f"lge{l}_d", (NR, 128, HS[l])) for l in range(2)]
    LGR = [dram(f"lgr{l}_d", (NR, HS[l], 128)) for l in range(2)]
    MXD = [dram(f"mx{l}_d", (N + 1, 4)) for l in range(2)]

    NIO, OHA = sb("nio", [128, N]), sb("oha", [128, N])
    NID = sb("nid", [TN, NT])
    ATG = [sb(f"atg{l}", [128, CH]) for l in range(2)]
    ACC = sb("acc", [TN, NT, CH + 4])
    DGA = [sb(f"dga{k}", [TN, NT]) for k in range(4)]
    SDI, DF, DC, DI, EWC = sb("sdi", [128, 2], I32), sb("df", [128, 1]), sb("dc", [128, 1]), sb("di", [128, 1], I32), sb("ewc", [128, 1])
    GR, GX, GW_ = sb("gr", [128, CH + 4]), sb("gx", [128, CH]), sb("gw", [128, CH])
    LE, LX, MXG, LER = sb("le", [128, 4]), sb("lx", [128, 4]), sb("mxg", [128, 4]), sb("ler", [4, 128])
    DBI, DBF, MK = sb("dbi", [TN, CK * 128], I32), sb("dbf", [TN, CK * 128]), sb("mk", [TN, CK * 128])
    LB, TMP = sb("lb", [TN, CK * 4 * 128]), sb("tmp", [TN, CK * 4 * 128])
    MXA, LSA, MXT = sb("mxa", [TN, NT, 4]), sb("lsa", [TN, NT, 4]), sb("mxt", [TN, 4])
    DIT = sb("dit", [NT, TN])
    W = {"1": sb("w1", [128, 2, CH]), **W}
    ROWP = sb("rowp", [1, CH])
    BIGR = sb("bigr", [1, 4])
    X, Y, Z, AC, T1, T2 = (sb(n, [TN, CH + 4]) for n in ("x", "y", "z", "ac", "t1", "t2"))
    HT = sb("ht", [128, 2, TN])
    DSC, SM, LST = sb("dsc", [TN, 1]), sb("sm", [TN, 8]), sb("lst", [TN, 4])

    dve = lambda *f: ("vector", f)
    act = lambda *f: ("scalar", f)
    pe = lambda *f: ("tensor", f)
    gather = lambda out, table, idx: ("gpsimd", [lambda e, i: e.indirect_dma_start(out=out, out_offset=None, in_=table, in_offset=off(idx))])
    dma = lambda *f: ("sync", [(lambda e, i, x=x: e.dma_start(*x(i))) for x in f])
    at = lambda arr, i: arr[bass.ds(i, 1)].rearrange("a p c -> (a p) c")
    flat = lambda arr: arr.rearrange("t p c -> (t p) c")
    xv = A["x"].rearrange("(t p) c -> t p c", p=TN)
    ov = A["out"].rearrange("(t p) c -> t p c", p=TN)
    x_, y_, z_, t1_, t2_ = (b[:, 0:CH] for b in (X, Y, Z, T1, T2))

    def project(src, Wm):
        return [pe(*[lambda e, i, c=c: e.matmul(PS[0][:, c * TN:(c + 1) * TN], src[:, c * 128:(c + 1) * 128], IDN[0:TN, 0:TN], start=True, stop=True, is_transpose=True) for c in range(2)]),
                act(lambda e, i: e.activation(HT[:], PS[0][:, 0:2 * TN].rearrange("p (k n) -> p k n", k=2), ACT.Copy)),
                pe(*[lambda e, i, c=c: e.matmul(PS[1][0:TN, 0:CH], HT[:, c, :], Wm[:, c, 0:CH], start=(c == 0), stop=(c == 1)) for c in range(2)])]

    targets = [dma(lambda i: (SDI[:], at(A["sdr"], i))),
               dve(lambda e, i: e.tensor_copy(DF[:], SDI[:, 1:2])),
               dve(lambda e, i: e.tensor_scalar(DC[:], DF[:], float(N), None, op0=ALU.min)),
               dve(lambda e, i: e.tensor_copy(DI[:], DC[:]))]
    onehot = dve(lambda e, i: e.tensor_scalar(OHA[:], NIO[:], DF[:, 0:1], None, op0=ALU.is_equal))

    def aggregate(w):
        steps = []
        for t0 in range(0, NT, 8):
            ts = range(t0, min(t0 + 8, NT))
            steps.append(pe(*[lambda e, i, t=t: e.matmul(PS[t % 8][0:TN, 0:w], OHA[:, t * TN:(t + 1) * TN], GR[:, 0:w], start=True, stop=True) for t in ts]))
            steps.append(dve(*[lambda e, i, t=t: e.tensor_tensor(ACC[:, t, 0:w], ACC[:, t, 0:w], PS[t % 8][0:TN, 0:w], op=ALU.add) for t in ts]))
        return steps

    clear = dve(lambda e, i: e.memset(ACC[:], 0.0))
    keep = dma(lambda i: (ACCD.rearrange("t p c -> p t c"), ACC[:]))

    def weighted(table):
        S.once(clear)
        S.loop(NR, *targets, dma(lambda i: (EWC[:], at(A["ewr"], i))), onehot, gather(GR[:, 0:CH], table, SDI[:, 0:1]),
               dve(lambda e, i: e.tensor_scalar(GR[:, 0:CH], GR[:, 0:CH], EWC[:, 0:1], None, op0=ALU.mult)), *aggregate(CH))
        S.once(keep)

    def normed(src, out):
        return [dve(lambda e, i: e.tensor_scalar(SM[:, 1:2], SM[:, 0:1], -1.0 / CH, None, op0=ALU.mult)),
                dve(lambda e, i: e.tensor_scalar(t1_, src, SM[:, 1:2], None, op0=ALU.add)),
                act(lambda e, i: e.activation(t2_, t1_, ACT.Square, accum_out=SM[:, 2:3])),
                dve(lambda e, i: e.tensor_scalar(SM[:, 3:4], SM[:, 2:3], 1.0 / CH, EPS, op0=ALU.mult, op1=ALU.add)),
                act(lambda e, i: e.activation(SM[:, 4:5], SM[:, 3:4], ACT.Sqrt)),
                dve(lambda e, i: e.reciprocal(SM[:, 5:6], SM[:, 4:5])),
                dve(lambda e, i: e.tensor_scalar(out, t1_, SM[:, 5:6], None, op0=ALU.mult))]

    def logits(l, a, b, p, tmp, out):
        H = HS[l]
        return [dve(lambda e, i: e.tensor_tensor(tmp, a, b, op=ALU.add)),
                dve(lambda e, i: e.scalar_tensor_tensor(b, tmp, 0.2, tmp, op0=ALU.mult, op1=ALU.max)),
                dve(lambda e, i: e.tensor_tensor(tmp, b, ATG[l][0:p, :], op=ALU.mult)),
                dve(lambda e, i: e.tensor_reduce(out[:, 0:H], tmp.rearrange("p (h c) -> p h c", h=H), axis=AX.X, op=ALU.add))]

    def sides(l, src):
        return [*project(src, W[f"l{l}"]), act(lambda e, i: e.activation(t1_, PS[1][0:TN, 0:CH], ACT.Copy)),
                *project(src, W[f"r{l}"]), act(lambda e, i: e.activation(t2_, PS[1][0:TN, 0:CH], ACT.Copy)),
                dma(lambda i: (at(XLD[l], i), t1_), lambda i: (at(XRD[l][0:N].rearrange("(t p) c -> t p c", p=TN), i), t2_)),
                *logits(l, t1_, t2_, TN, y_, LST[:]),
                dma(lambda i: (at(LSD[l], i), LST[:]))]

    S.once(dve(*[lambda e, i, t=t: e.tensor_scalar(NIO[:, t * TN:(t + 1) * TN], IOTA[:, 0:TN], float(t * TN), None, op0=ALU.add) for t in range(NT)],
               *[lambda e, i, t=t: e.tensor_scalar(NID[:, t:t + 1], PIDX, float(t * TN), None, op0=ALU.add) for t in range(NT)],
               lambda e, i: e.memset(DGA[0][:], 0.0), lambda e, i: e.memset(LST[:], 0.0), lambda e, i: e.memset(ROWP[:], 0.0), lambda e, i: e.memset(BIGR[:], BIG)),
           dma(lambda i: (W["1"][:], A["W1"].rearrange("(k p) n -> p k n", p=128)), *[lambda i, l=l: (ATG[l][:], A[f"att{l + 1}"].broadcast_to([128, CH])) for l in range(2)],
               *[lambda i, l=l: (XRD[l][N:N + 1], ROWP[:]) for l in range(2)],
               *[lambda i, l=l: (MXD[l][N:N + 1], BIGR[:]) for l in range(2)]))

    S.loop(NR, *targets, dma(lambda i: (EWC[:], at(A["ewr"], i))), onehot,
           pe(*[lambda e, i, t=t: e.matmul(PS[0][0:TN, t:t + 1], OHA[:, t * TN:(t + 1) * TN], EWC[:], start=True, stop=True) for t in range(NT)]),
           dve(lambda e, i: e.tensor_tensor(DGA[0][:], DGA[0][:], PS[0][0:TN, 0:NT], op=ALU.add)))
    a, b, c, d = (x[:] for x in DGA)
    S.once(dve(lambda e, i: e.tensor_scalar(b, a, 1.0, None, op0=ALU.add)),
           dve(lambda e, i: e.tensor_scalar(c, b, 0.0, None, op0=ALU.is_gt)),
           dve(lambda e, i: e.tensor_tensor(d, b, c, op=ALU.mult)),
           dve(lambda e, i: e.scalar_tensor_tensor(b, c, -1.0, d, op0=ALU.mult, op1=ALU.add)),
           dve(lambda e, i: e.tensor_scalar(d, b, 1.0, None, op0=ALU.add)),
           act(lambda e, i: e.activation(b, d, ACT.Sqrt)),
           dve(lambda e, i: e.reciprocal(d, b)),
           dve(lambda e, i: e.tensor_tensor(DIS[:], d, c, op=ALU.mult)),
           pe(lambda e, i: e.matmul(PS[0][0:NT, 0:TN], DIS[:], IDN[0:TN, 0:TN], start=True, stop=True, is_transpose=True)),
           act(lambda e, i: e.activation(DIT[:], PS[0][0:NT, 0:TN], ACT.Copy)),
           dma(lambda i: (DISD.rearrange("t p c -> t (p c)"), DIT[:])))

    S.loop(NT, dma(lambda i: (x_, at(xv, i)), lambda i: (DSC[:], at(DISD, i))), *project(x_, W["1"]),
           act(lambda e, i: e.activation(y_, PS[1][0:TN, 0:CH], ACT.Copy, scale=DSC[:, 0:1])),
           dma(lambda i: (at(HPD[0], i), y_)))
    weighted(flat(HPD[0]))

    def summed(k):
        return [dma(lambda i: (AC[:], at(ACCD, i)), lambda i: (x_, at(HPD[k], i)), lambda i: (DSC[:], at(DISD, i))),
                dve(lambda e, i: e.tensor_tensor(z_, AC[:, 0:CH], x_, op=ALU.add)),
                dve(lambda e, i: e.scalar_tensor_tensor(y_, z_, DSC[:, 0:1], BB[k][:], op0=ALU.mult, op1=ALU.add))]

    S.loop(NT, *summed(0), dve(lambda e, i: e.scalar_tensor_tensor(z_, y_, 0.01, y_, op0=ALU.mult, op1=ALU.max)), *project(z_, W["2"]),
           act(lambda e, i: e.activation(y_, PS[1][0:TN, 0:CH], ACT.Copy, scale=DSC[:, 0:1])),
           dma(lambda i: (at(HPD[1], i), y_)))
    weighted(flat(HPD[1]))
    S.loop(NT, *summed(1), dma(lambda i: (x_, at(xv, i))),
           dve(lambda e, i: e.scalar_tensor_tensor(z_, y_, 1.0, x_, op0=ALU.mult, op1=ALU.add, accum_out=SM[:, 0:1])),
           *normed(z_, x_), dma(lambda i: (at(X1, i), x_)), *sides(0, x_))

    def layer(l):
        H = HS[l]
        C = CH // H
        hv = lambda v: v.rearrange("p (h c) -> p h c", h=H)
        gr, gx, gw = GR[:, 0:CH], GX[:], GW_[:]
        S.loop(NR, *targets, gather(gr, flat(XLD[l]), SDI[:, 0:1]), gather(gx, XRD[l], DI[:, 0:1]), *logits(l, gr, gx, 128, gw, LE[:]),
               pe(lambda e, i: e.matmul(PS[0][0:H, 0:128], LE[:, 0:H], IDN, start=True, stop=True, is_transpose=True)),
               act(lambda e, i: e.activation(LER[0:H, :], PS[0][0:H, 0:128], ACT.Copy)),
               dma(lambda i: (at(LGE[l], i), LE[:, 0:H]), lambda i: (at(LGR[l], i), LER[0:H, :])))
        S.once(dve(lambda e, i: e.memset(MXA[:], -BIG)))
        lb = LB[:, 0:CK * H * 128].rearrange("p (r h e) -> p r h e", r=CK, h=H)
        tmp = TMP[:, 0:CK * H * 128].rearrange("p (r h e) -> p r h e", r=CK, h=H)
        mk = MK[:].rearrange("p (r o e) -> p r o e", r=CK, o=1).broadcast_to([TN, CK, H, 128])
        largest = []
        for t in range(NT):
            largest += [dve(lambda e, i, t=t: e.tensor_scalar(MK[:], DBF[:], NID[:, t:t + 1], -BIG, op0=ALU.not_equal, op1=ALU.mult)),
                        dve(lambda e, i: e.tensor_tensor(tmp, lb, mk, op=ALU.add)),
                        dve(lambda e, i: e.tensor_reduce(MXT[:, 0:H], tmp.rearrange("p r h e -> p h r e"), axis=AX.XY, op=ALU.max)),
                        dve(lambda e, i, t=t: e.tensor_tensor(MXA[:, t, 0:H], MXA[:, t, 0:H], MXT[:, 0:H], op=ALU.max))]
        S.loop(NR // CK,
               dma(lambda i: (DBI[:], A["dr"][bass.ds(i, 1), :].broadcast_to([TN, CK * 128])),
                   lambda i: (LB[:, 0:CK * H * 128], LGR[l].rearrange("(n r) h e -> n (r h e)", r=CK)[bass.ds(i, 1), :].broadcast_to([TN, CK * H * 128]))),
               dve(lambda e, i: e.tensor_copy(DBF[:], DBI[:])), *largest)
        S.once(dma(lambda i: (LSA[:], LSD[l].rearrange("t p h -> p t h"))),
               dve(lambda e, i: e.tensor_tensor(MXA[:], MXA[:], LSA[:], op=ALU.max)),
               dma(lambda i: (MXD[l][0:N].rearrange("(t p) h -> p t h", p=TN), MXA[:])),
               clear)
        S.loop(NR, *targets, onehot, gather(gr, flat(XLD[l]), SDI[:, 0:1]), gather(MXG[:], MXD[l], DI[:, 0:1]), dma(lambda i: (LE[:, 0:H], at(LGE[l], i))),
               dve(lambda e, i: e.tensor_tensor(LX[:, 0:H], LE[:, 0:H], MXG[:, 0:H], op=ALU.subtract)),
               act(lambda e, i: e.activation(GR[:, CH:CH + H], LX[:, 0:H], ACT.Exp)),
               dve(lambda e, i: e.tensor_tensor(hv(gr), hv(gr), GR[:, CH:CH + H].unsqueeze(2).broadcast_to([128, H, C]), op=ALU.mult)),
               *aggregate(CH + H))
        S.once(keep)
        wide = lambda v: v.unsqueeze(2).broadcast_to([TN, H, C])
        out = [dma(lambda i: (AC[:], at(ACCD, i)), lambda i: (x_, at(XLD[l], i)), lambda i: (LST[:], at(LSD[l], i)),
                   lambda i: (MXT[:], at(MXD[l][0:N].rearrange("(t p) h -> t p h", p=TN), i))),
               dve(lambda e, i: e.tensor_tensor(SM[:, 0:H], LST[:, 0:H], MXT[:, 0:H], op=ALU.subtract)),
               act(lambda e, i: e.activation(SM[:, 4:4 + H], SM[:, 0:H], ACT.Exp)),
               dve(lambda e, i: e.tensor_tensor(SM[:, 0:H], SM[:, 4:4 + H], AC[:, CH:CH + H], op=ALU.add)),
               dve(lambda e, i: e.tensor_tensor(hv(y_), hv(x_), wide(SM[:, 4:4 + H]), op=ALU.mult)),
               dve(lambda e, i: e.reciprocal(LST[:, 0:H], SM[:, 0:H])),
               dve(lambda e, i: e.tensor_tensor(z_, y_, AC[:, 0:CH], op=ALU.add)),
               dve(lambda e, i: e.tensor_tensor(hv(y_), hv(z_), wide(LST[:, 0:H]), op=ALU.mult)),
               dve(lambda e, i: e.tensor_tensor(z_, y_, BB[2 + l][:], op=ALU.add))]
        if l == 0:
            out += [dve(lambda e, i: e.tensor_scalar(y_, z_, 0.0, None, op0=ALU.min)),
                    act(lambda e, i: e.activation(t1_, y_, ACT.Exp)),
                    dve(lambda e, i: e.scalar_tensor_tensor(y_, z_, 0.0, t1_, op0=ALU.max, op1=ALU.add)),
                    dve(lambda e, i: e.tensor_scalar(z_, y_, -1.0, None, op0=ALU.add)), *sides(1, z_)]
        else:
            out += [dma(lambda i: (x_, at(X1, i))),
                    dve(lambda e, i: e.scalar_tensor_tensor(y_, z_, 1.0, x_, op0=ALU.mult, op1=ALU.add, accum_out=SM[:, 0:1])),
                    *normed(y_, x_), dma(lambda i: (at(ov, i), x_))]
        S.loop(NT, *out)

    for l in range(2):
        layer(l)
    return S


def layouts(src, dst, ew, NT, E):
    N = NT * TN
    nb = -(-E // BLK)
    nr = nb + KP * ROW // BLK
    length = (nr + ROW // BLK) * BLK
    cw = -(-E // 128)
    length = max(length, 128 * cw + 1)
    length = -(-length // BLK) * BLK

    def padded(a, value):
        out = np.full(length, value, a.dtype)
        out[:E] = a
        return out

    def fill(a, value):
        out = np.full(-(-E // 512) * 512, value, a.dtype)
        out[:E] = a
        return out.reshape(-1, 128)

    s, d, w = padded(src, 0), padded(dst, N + 875), padded(ew, 0)
    rows = lambda a: [a.reshape(-1, BLK)[m:m + nr] for m in range(ROW // BLK)]
    return {
        "sd": np.ascontiguousarray(np.concatenate(rows(s) + rows(d), axis=1)),
        "ew": np.ascontiguousarray(np.concatenate(rows(w), axis=1)),
        "first": np.ascontiguousarray(d.reshape(-1, BLK)[:nb, 0][None]),
        "sdr": np.stack([fill(src, 0), fill(dst, N + 875)], axis=2),
        "ewr": fill(ew, 0)[:, :, None],
        "dr": fill(dst, N + 875).reshape(-1, 4 * 128),
        "dsort": np.ascontiguousarray(np.concatenate([d[:128 * cw].reshape(128, cw), d[cw:128 * cw + 1:cw][:, None]], axis=1)),
    }


def build(nc, A, NT, E, where):
    ctx, Q, FLAG, general = gnn_program(nc, A, NT, E, where)

    def emit(name, e):
        Q.emit(name, e)
        needed = e.value_load(FLAG[0:1, 0:1], min_val=0, max_val=1)
        with e.If(needed == 1):
            general.emit(name, e)

    with ctx:
        with nc.Block() as block:
            block.sync(lambda e: emit("sync", e))
            block.tensor(lambda e: emit("tensor", e))
            block.vector(lambda e: emit("vector", e))
            block.scalar(lambda e: emit("scalar", e))
            block.gpsimd(lambda e: emit("gpsimd", e))


def kernel(**inputs):
    import concourse.bacc as _bacc
    from concourse.bass_utils import run_bass_kernel_spmd as _run

    a = {k: np.asarray(v) for k, v in inputs.items()}
    NT, E = a["x"].shape[0] // TN, a["src"].shape[0]
    arrays = layouts(a["src"], a["dst"], a["edge_weight"], NT, E)
    arrays["x"] = a["x"]
    arrays["W1"], arrays["W2"] = a["L0_gnn_W1"], a["L0_gnn_W2"]
    for l in (1, 2):
        arrays[f"Wl{l}"], arrays[f"Wr{l}"] = a[f"L1_gnn_Wl{l}"], a[f"L1_gnn_Wr{l}"]
        arrays[f"att{l}"] = a[f"L1_gnn_att{l}"].reshape(1, CH)
        arrays[f"att{l}c"] = a[f"L1_gnn_att{l}"].reshape(2, 128).T
    for i, n in enumerate(("L0_gnn_b1", "L0_gnn_b2", "L1_gnn_b1", "L1_gnn_b2")):
        arrays[f"b{i + 1}"] = a[n].reshape(1, CH)
    arrays["const"], where = shape_constants(NT, E)
    arrays = {f"in_{k}": np.ascontiguousarray(v) for k, v in arrays.items()}

    nc = _bacc.Bacc("TRN2", target_bir_lowering=False, num_devices=1)
    A = {k[3:]: nc.dram_tensor(k, v.shape, mybir.dt.from_np(v.dtype), kind="ExternalInput").ap() for k, v in arrays.items()}
    A["out"] = nc.dram_tensor("out", (NT * TN, CH), F32, kind="ExternalOutput").ap()
    build(nc, A, NT, E, where)
    r = _run(nc, [arrays], core_ids=[0])
    return r.results[0]["out"]
```
